# Optimizing a Trainium2 kernel written in Bass

```python
import numpy as np
import jax
import jax.numpy as jnp

def _softmax(x, axis=-1):
    return jax.nn.softmax(x, axis=axis)

def _gelu(x):
    return jax.nn.gelu(x, approximate=True)

def _silu(x):
    return jax.nn.silu(x)

def _sigmoid(x):
    return jax.nn.sigmoid(x)

def _layernorm(x, axis=-1, eps=1e-05):
    m = jnp.mean(x, axis=axis, keepdims=True)
    v = jnp.var(x, axis=axis, keepdims=True)
    return (x - m) / jnp.sqrt(v + eps)

def _scatter_add(tgt, idx, src, axis=0):
    return tgt.at[idx].add(src)

def _segment_sum(src, seg, n):
    return jax.ops.segment_sum(src, seg, n)
kernel_name = 'mk_recurrent_d1_jaxref_r8_b64d6f'

def setup_inputs(seed: int=0):
    np.random.seed(seed)
    _w = jnp.asarray

    def _L0_attn_setup():
        import jax, jax.numpy as jnp
        import numpy as np
        NV, NK, DK, DV, KC = (32, 16, 128, 128, 4)
        EPS = 1e-06

        def _silu(x):
            return x * jax.nn.sigmoid(x)

        def _l2norm(x):
            return x * jax.lax.rsqrt(jnp.sum(x * x, axis=-1, keepdims=True) + EPS)

        def _gated_delta_rule(q, k, v, g, beta):
            tm = lambda x: jnp.moveaxis(x, 1, 0)
            B, T, H = (q.shape[0], q.shape[1], q.shape[2])
            S0 = jnp.zeros((B, H, q.shape[-1], v.shape[-1]), q.dtype)

            def step(S, xs):
                qt, kt, vt, gt, bt = xs
                S = S * jnp.exp(gt)[..., None, None]
                kS = jnp.einsum('bhk,bhkv->bhv', kt, S)
                S = S + bt[..., None, None] * kt[..., :, None] * (vt - kS)[..., None, :]
                o = jnp.einsum('bhk,bhkv->bhv', qt, S)
                return (S, o)
            _, o = jax.lax.scan(step, S0, (tm(q), tm(k), tm(v), tm(g), tm(beta)))
            return jnp.moveaxis(o, 0, 1)
        key = jax.random.key(seed)
        ks = jax.random.split(key, 10)
        B, T, D = (2, 512, 256)
        key_dim, value_dim = (NK * DK, NV * DV)
        conv_dim = 2 * key_dim + value_dim
        s = 0.02
        return {'hidden_states': jax.random.normal(ks[0], (B, T, D), jnp.float32), 'W_qkv': jax.random.normal(ks[1], (D, conv_dim), jnp.float32) * s, 'W_z': jax.random.normal(ks[2], (D, value_dim), jnp.float32) * s, 'W_b': jax.random.normal(ks[3], (D, NV), jnp.float32) * s, 'W_a': jax.random.normal(ks[4], (D, NV), jnp.float32) * s, 'conv_w': jax.random.normal(ks[5], (conv_dim, KC), jnp.float32) * 0.2, 'dt_bias': jnp.ones((NV,), jnp.float32), 'A_log': jnp.log(jax.random.uniform(ks[6], (NV,), jnp.float32, 0.5, 16.0)), 'norm_w': jnp.ones((DV,), jnp.float32), 'W_out': jax.random.normal(ks[7], (value_dim, D), jnp.float32) * s}
    _L0_attn_in = _L0_attn_setup()

    def _L0_ffn_setup():
        import jax, jax.numpy as jnp
        import numpy as np
        H = 256
        I_MOE = 176
        I_SH = 704
        E = 8
        TOP_K = 2
        B, S = (1, 256)

        def _silu_and_mul(gu, inter):
            return jax.nn.silu(gu[..., :inter]) * gu[..., inter:]
        key = jax.random.key(seed)
        ks = jax.random.split(key, 7)
        sc = 0.02
        return {'hidden_states': jax.random.normal(ks[0], (B, S, H), jnp.float32), 'W_router': jax.random.normal(ks[1], (E, H), jnp.float32) * sc, 'W_sgate': jax.random.normal(ks[2], (1, H), jnp.float32) * sc, 'Ws_gate_up': jax.random.normal(ks[3], (H, 2 * I_SH), jnp.float32) * sc, 'Ws_down': jax.random.normal(ks[4], (I_SH, H), jnp.float32) * sc, 'We_gate_up': jax.random.normal(ks[5], (E, H, 2 * I_MOE), jnp.float32) * sc, 'We_down': jax.random.normal(ks[6], (E, I_MOE, H), jnp.float32) * sc}
    _L0_ffn_in = _L0_ffn_setup()
    _d = {'L0_attn_hidden_states': _L0_attn_in['hidden_states'], 'L0_attn_W_qkv': _L0_attn_in['W_qkv'], 'L0_attn_W_z': _L0_attn_in['W_z'], 'L0_attn_W_b': _L0_attn_in['W_b'], 'L0_attn_W_a': _L0_attn_in['W_a'], 'L0_attn_conv_w': _L0_attn_in['conv_w'], 'L0_attn_dt_bias': _L0_attn_in['dt_bias'], 'L0_attn_A_log': _L0_attn_in['A_log'], 'L0_attn_norm_w': _L0_attn_in['norm_w'], 'L0_attn_W_out': _L0_attn_in['W_out'], 'L0_ffn_W_router': _L0_ffn_in['W_router'], 'L0_ffn_W_sgate': _L0_ffn_in['W_sgate'], 'L0_ffn_Ws_gate_up': _L0_ffn_in['Ws_gate_up'], 'L0_ffn_Ws_down': _L0_ffn_in['Ws_down'], 'L0_ffn_We_gate_up': _L0_ffn_in['We_gate_up'], 'L0_ffn_We_down': _L0_ffn_in['We_down']}
    _x0 = _d['L0_attn_hidden_states']
    _d['L0_attn_hidden_states'] = jax.random.normal(jax.random.fold_in(jax.random.key(seed), 1), (4, 512, 256), dtype=_x0.dtype)
    del _x0
    return _d

def reference(L0_attn_hidden_states, L0_attn_W_qkv, L0_attn_W_z, L0_attn_W_b, L0_attn_W_a, L0_attn_conv_w, L0_attn_dt_bias, L0_attn_A_log, L0_attn_norm_w, L0_attn_W_out, L0_ffn_W_router, L0_ffn_W_sgate, L0_ffn_Ws_gate_up, L0_ffn_Ws_down, L0_ffn_We_gate_up, L0_ffn_We_down):

    def _L0_attn_ref(hidden_states, W_qkv, W_z, W_b, W_a, conv_w, dt_bias, A_log, norm_w, W_out):
        import jax, jax.numpy as jnp
        import numpy as np
        NV, NK, DK, DV, KC = (32, 16, 128, 128, 4)
        EPS = 1e-06

        def _silu(x):
            return x * jax.nn.sigmoid(x)

        def _l2norm(x):
            return x * jax.lax.rsqrt(jnp.sum(x * x, axis=-1, keepdims=True) + EPS)

        def _gated_delta_rule(q, k, v, g, beta):
            tm = lambda x: jnp.moveaxis(x, 1, 0)
            B, T, H = (q.shape[0], q.shape[1], q.shape[2])
            S0 = jnp.zeros((B, H, q.shape[-1], v.shape[-1]), q.dtype)

            def step(S, xs):
                qt, kt, vt, gt, bt = xs
                S = S * jnp.exp(gt)[..., None, None]
                kS = jnp.einsum('bhk,bhkv->bhv', kt, S)
                S = S + bt[..., None, None] * kt[..., :, None] * (vt - kS)[..., None, :]
                o = jnp.einsum('bhk,bhkv->bhv', qt, S)
                return (S, o)
            _, o = jax.lax.scan(step, S0, (tm(q), tm(k), tm(v), tm(g), tm(beta)))
            return jnp.moveaxis(o, 0, 1)
        B, T, D = hidden_states.shape
        key_dim, value_dim = (NK * DK, NV * DV)
        mixed = hidden_states @ W_qkv
        z = (hidden_states @ W_z).reshape(B, T, NV, DV)
        beta = jax.nn.sigmoid(hidden_states @ W_b)
        a = hidden_states @ W_a
        g = -jnp.exp(A_log) * jax.nn.softplus(a + dt_bias)
        xp = jnp.pad(mixed, ((0, 0), (KC - 1, 0), (0, 0)))
        conv = sum((xp[:, i:i + T, :] * conv_w[:, i] for i in range(KC)))
        mixed = _silu(conv)
        q, k, v = jnp.split(mixed, [key_dim, 2 * key_dim], axis=-1)
        q = q.reshape(B, T, NK, DK)
        k = k.reshape(B, T, NK, DK)
        v = v.reshape(B, T, NV, DV)
        rep = NV // NK
        q = jnp.repeat(q, rep, axis=2)
        k = jnp.repeat(k, rep, axis=2)
        q = _l2norm(q) * DK ** (-0.5)
        k = _l2norm(k)
        o = _gated_delta_rule(q, k, v, g, beta)
        var = jnp.mean(o * o, axis=-1, keepdims=True)
        o = o * jax.lax.rsqrt(var + 1e-06) * norm_w * _silu(z)
        return o.reshape(B, T, value_dim) @ W_out

    def _L0_ffn_ref(hidden_states, W_router, W_sgate, Ws_gate_up, Ws_down, We_gate_up, We_down):
        import jax, jax.numpy as jnp
        import numpy as np
        H = 256
        I_MOE = 176
        I_SH = 704
        E = 8
        TOP_K = 2
        B, S = (1, 256)

        def _silu_and_mul(gu, inter):
            return jax.nn.silu(gu[..., :inter]) * gu[..., inter:]
        orig_shape = hidden_states.shape
        x = hidden_states.reshape(-1, H)
        T = x.shape[0]
        logits = x @ W_router.T
        probs = jax.nn.softmax(logits.astype(jnp.float32), axis=-1)
        rw, sel = jax.lax.top_k(probs, TOP_K)
        rw = rw.astype(x.dtype)
        combine = jnp.zeros((T, E), x.dtype).at[jnp.arange(T)[:, None], sel].add(rw)
        sh = _silu_and_mul(x @ Ws_gate_up, I_SH) @ Ws_down
        shared_out = sh * jax.nn.sigmoid(x @ W_sgate.T)
        gu = jnp.einsum('th,ehi->eti', x, We_gate_up)
        h = _silu_and_mul(gu, I_MOE)
        eo = jnp.einsum('eti,eih->eth', h, We_down)
        sparse_out = jnp.einsum('eth,te->th', eo, combine)
        return (shared_out + sparse_out).reshape(orig_shape)
    x = L0_attn_hidden_states
    xn = _layernorm(x, axis=-1)
    s = _L0_attn_ref(xn, L0_attn_W_qkv, L0_attn_W_z, L0_attn_W_b, L0_attn_W_a, L0_attn_conv_w, L0_attn_dt_bias, L0_attn_A_log, L0_attn_norm_w, L0_attn_W_out)
    g = _silu(_L0_ffn_ref(xn, L0_ffn_W_router, L0_ffn_W_sgate, L0_ffn_Ws_gate_up, L0_ffn_Ws_down, L0_ffn_We_gate_up, L0_ffn_We_down))
    x = x + s * g
    return x

_drawn_inputs = setup_inputs


def setup_inputs(seed=0):
    import zlib

    import numpy as np

    out = dict(_drawn_inputs(seed))
    spreads = {'L0_attn_dt_bias': (1.0, 0.6), 'L0_attn_norm_w': (1.0, 0.6)}
    factors = {'L0_attn_W_qkv': 8.0,
     'L0_attn_W_z': 8.0,
     'L0_attn_W_b': 8.0,
     'L0_attn_W_a': 8.0,
     'L0_attn_conv_w': 8.0,
     'L0_attn_A_log': 8.0,
     'L0_attn_W_out': 8.0,
     'L0_ffn_W_router': 8.0,
     'L0_ffn_W_sgate': 8.0,
     'L0_ffn_Ws_gate_up': 8.0,
     'L0_ffn_Ws_down': 8.0,
     'L0_ffn_We_gate_up': 8.0,
     'L0_ffn_We_down': 8.0}
    for name, (base, spread) in spreads.items():
        noise = np.random.default_rng([zlib.crc32(name.encode()), seed]).standard_normal(out[name].shape)
        drawn = base * np.exp(spread * noise) if base else spread * noise
        out[name] = jnp.asarray(drawn.astype(out[name].dtype))
    for name, factor in factors.items():
        out[name] = (out[name] * factor).astype(out[name].dtype)
    return out
```

```python
from contextlib import ExitStack

import numpy as np
import concourse.bass as bass
from concourse import mybir

F32 = mybir.dt.float32
BF16 = mybir.dt.bfloat16
ALU = mybir.AluOpType
ACT = mybir.ActivationFunctionType
AX = mybir.AxisListType

P = 128
BASE = 1
BATCH, T, D = 4, 512, 256
KT = D // P
NV, NK, KC = 32, 16, 4
REP = NV // NK
C = 128
NC_ = T // C
TILES = BATCH * NC_
U = REP * NC_
STEPS = NK * BATCH
UNITS = STEPS * U
E, I_MOE, I_SH = 8, 176, 704
F = E * I_MOE + I_SH
FT = -(-F // P)
NSMALL = 2 * NV + E + 1
LN_EPS, L2_EPS, RMS_EPS = 1e-5, 1e-6, 1e-6
LOG_DECAY_MIN = -110.0
ROUND = 1.5 * 2.0 ** 23
MASKED = -30000.0
LEVELS = (2, 4, 8, 16, 32, 64)
NL = len(LEVELS)
BETA, GAM, NGAM, WSUF, GAMC = range(5)
KINDS = 5


def constants():
    r, c = np.arange(P)[:, None], np.arange(P)[None, :]

    def merge(s):
        return ((r // s) % 2 == 0) & (c // s == r // s + 1)

    parts = [r == c, r <= c, r > c, np.ones((P, P), bool), (c < r) * MASKED, merge(1) * -1.0]
    parts += [merge(s) for s in LEVELS]
    parts += [np.broadcast_to(np.arange(E) - E, (P, E))]
    return np.ascontiguousarray(np.concatenate([np.asarray(x, np.float32) for x in parts], 1))


IDENT, UPTO, AFTER, ONES, HIDE, MERGE1, MERGE2 = (P * k for k in range(7))
IOTA = MERGE2 + NL * P
NCONST = IOTA + E


def prepare_block(nc, x, small_w, decay_rows, keep, g_rows, comb_rows):
    cst, xnT, prep = keep["cst"], keep["xnT"], keep["prep"]
    with ExitStack() as ctx:
        def sb(name, shape, dt=F32):
            return ctx.enter_context(nc.sbuf_tensor(name, shape, dt))

        def sem(name):
            return ctx.enter_context(nc.semaphore(name))

        xs = sb("xs", [P, TILES, D])
        ws = sb("ws", [P, KT, NSMALL])
        stats = sb("stats", [P, TILES, 6])
        mean = sb("mean", [P, TILES])
        diff = sb("diff", [P, TILES])
        var = sb("var", [P, TILES])
        rstd = sb("rstd", [P, TILES])
        expo = sb("expo", [P, TILES])
        xn = sb("xn", [P, 2, D])
        xt = sb("xt", [P, 2, D])
        a_b = sb("a_b", [P, UNITS])
        a_a = sb("a_a", [P, UNITS])
        routed = sb("routed", [P, TILES, E + 1])
        dtb = sb("dtb", [P, UNITS])
        a_exp = sb("a_exp", [P, UNITS])
        absu = sb("absu", [P, UNITS])
        em = sb("em", [P, UNITS])
        den = sb("den", [P, UNITS])
        sq = sb("sq", [P, UNITS])
        ser = sb("ser", [P, UNITS])
        g = sb("g", [P, UNITS])
        g_hi = sb("g_hi", [P, UNITS])
        g_lo = sb("g_lo", [P, UNITS])
        sum_hi = sb("sum_hi", [P, UNITS])
        sum_lo = sb("sum_lo", [P, UNITS])
        sum_g = sb("sum_g", [P, UNITS])
        rows = sb("rows", [P, 4, UNITS])
        top = sb("top", [P, TILES])
        pr = sb("pr", [P, TILES, E])
        hit = sb("hit", [P, TILES, E])
        hot1 = sb("hot1", [P, TILES, E])
        hot2 = sb("hot2", [P, TILES, E])
        comb = sb("comb", [P, TILES, E + 1])
        combT = sb("combT", [P, 2, P])
        ps_t = [ctx.enter_context(nc.psum_tensor(f"ps_t{k}", [P, 512], F32)) for k in range(2)]
        ps_s = [ctx.enter_context(nc.psum_tensor(f"ps_s{k}", [P, 512], F32)) for k in range(2)]
        ps_g = [ctx.enter_context(nc.psum_tensor(f"ps_g{k}", [P, 512], F32)) for k in range(4)]

        loaded, w_loaded = sem("x_loaded"), sem("w_loaded")
        vec, act_s, pow_done = sem("vec_chain"), sem("act_chain"), sem("pow_done")
        var_ready, stored = sem("var_ready"), sem("rows_stored")
        xn_ready, xnt_ps, xt_ready, xt_kept = sem("xn_ready"), sem("xnT_ps"), sem("xt_ready"), sem("xnT_kept")
        small_ps, small_out = sem("small_ps"), sem("small_out")
        u_ready, e_ready, g_ready, sums_ps, sums_out = sem("u_ready"), sem("e_ready"), sem("g_ready"), sem("sums_ps"), sem("sums_out")
        sumg_ready, rows_ps, rows_out, gam_ready = sem("sumg_ready"), sem("rows_ps"), sem("rows_out"), sem("gam_ready")
        logit_ready, prob_exp, sg_ready = sem("logit_ready"), sem("prob_exp"), sem("sg_ready")
        comb_ready, comb_ps, comb_out = sem("comb_ready"), sem("comb_ps"), sem("comb_out")
        block = ctx.enter_context(nc.Block())

        @block.sync
        def _(sp):
            for b in range(BATCH):
                sp.dma_start(xs[:, b * NC_:(b + 1) * NC_, :],
                             x[b].rearrange("(c p) d -> p c d", p=P)).then_inc(loaded, 16)
            sp.dma_start(cst[:, :], keep["cst_dram"]).then_inc(w_loaded, 16)
            sp.dma_start(ws[:, :, :], small_w).then_inc(w_loaded, 16)
            sp.dma_start(dtb[:, :], decay_rows[0:1, :].partition_broadcast(P)).then_inc(w_loaded, 16)
            sp.dma_start(a_exp[:, :], decay_rows[1:2, :].partition_broadcast(P)).then_inc(w_loaded, 16)
            sp.wait_ge(comb_out, 2)
            sp.dma_start(comb_rows[0:P, :], combT[:, 0, :]).then_inc(stored, 16)
            sp.dma_start(comb_rows[P:TILES * (E + 1), :], combT[0:TILES * (E + 1) - P, 1, :]).then_inc(stored, 16)
            sp.wait_ge(rows_out, 4)
            for k in range(4):
                sp.dma_start(g_rows[k].rearrange("(q u t) -> u q t", q=4, u=P),
                             rows[:, k, :].rearrange("u (q t) -> u q t", q=4)).then_inc(stored, 16)
            sp.wait_ge(stored, 6 * 16)

        @block.vector
        def _(dve):
            chain = [0]

            def link(ins):
                chain[0] += 1
                ins.then_inc(vec, 1)
                dve.wait_ge(vec, chain[0])

            dve.wait_ge(loaded, BATCH * 16)
            with dve.Fori(0, TILES) as t:
                nc.vector.bn_stats(stats[:, bass.ds(t, 1), :], xs[:, bass.ds(t, 1), :]).then_inc(small_out, 1)
            dve.wait_ge(small_out, TILES)
            link(nc.vector.tensor_tensor(mean[:, :], stats[:, :, 1], stats[:, :, 4], ALU.add))
            link(nc.vector.tensor_tensor(diff[:, :], stats[:, :, 1], stats[:, :, 4], ALU.subtract))
            link(nc.vector.tensor_tensor(var[:, :], stats[:, :, 2], stats[:, :, 5], ALU.add))
            link(nc.vector.tensor_scalar(mean[:, :], mean[:, :], 0.5, None, ALU.mult))
            link(nc.vector.tensor_tensor(diff[:, :], diff[:, :], diff[:, :], ALU.mult))
            link(nc.vector.tensor_scalar(diff[:, :], diff[:, :], 0.25, LN_EPS, ALU.mult, ALU.add))
            link(nc.vector.memset(expo[:, :], -0.5))
            nc.vector.scalar_tensor_tensor(var[:, :], var[:, :], 1.0 / D, diff[:, :],
                                           ALU.mult, ALU.add).then_inc(var_ready, 1)
            dve.wait_ge(pow_done, 1)
            a_bv = a_b[:, :].rearrange("p (h b v c) -> p h b v c", h=NK, b=BATCH, v=REP)
            a_av = a_a[:, :].rearrange("p (h b v c) -> p h b v c", h=NK, b=BATCH, v=REP)
            with dve.Fori(0, BATCH) as b:
                for c in range(NC_):
                    k = c % 2
                    dve.wait_ge(xnt_ps, b * NC_ + max(c - 1, 0) + BASE)
                    nc.vector.tensor_scalar(xn[:, k, :], xs[:, bass.ds(b * NC_ + c, 1), :],
                                            mean[:, bass.ds(b * NC_ + c, 1)], rstd[:, bass.ds(b * NC_ + c, 1)],
                                            ALU.subtract, ALU.mult).then_inc(xn_ready, 1)
                    dve.wait_ge(small_ps, b * NC_ + c + 1 + BASE)
                    nc.vector.tensor_copy(a_bv[:, :, bass.ds(b, 1), :, c],
                                          ps_s[k][:, 0:NV].rearrange("p (h o v) -> p h o v", v=REP, o=1)).then_inc(small_out, 1)
                    nc.vector.tensor_copy(a_av[:, :, bass.ds(b, 1), :, c],
                                          ps_s[k][:, NV:2 * NV].rearrange("p (h o v) -> p h o v", v=REP, o=1)).then_inc(small_out, 1)
                    nc.vector.tensor_copy(routed[:, bass.ds(b * NC_ + c, 1), :],
                                          ps_s[k][:, 2 * NV:NSMALL]).then_inc(small_out, 1)
            dve.wait_ge(small_out, 4 * TILES)
            dve.wait_ge(w_loaded, 64)
            nc.vector.tensor_tensor(a_a[:, :], a_a[:, :], dtb[:, :], ALU.add).then_inc(u_ready, 1)
            link(nc.vector.tensor_reduce(top[:, :], routed[:, :, 0:E], AX.X, ALU.max))
            nc.vector.tensor_tensor(pr[:, :, :], routed[:, :, 0:E],
                                    top[:, :].unsqueeze(2).to_broadcast([P, TILES, E]), ALU.subtract).then_inc(logit_ready, 1)
            dve.wait_ge(e_ready, 1)
            link(nc.vector.tensor_scalar(den[:, :], em[:, :], 2.0, None, ALU.add))
            link(nc.vector.reciprocal(den[:, :], den[:, :]))
            link(nc.vector.tensor_tensor(em[:, :], em[:, :], den[:, :], ALU.mult))
            link(nc.vector.tensor_tensor(sq[:, :], em[:, :], em[:, :], ALU.mult))
            link(nc.vector.tensor_scalar(ser[:, :], sq[:, :], 1.0 / 17, None, ALU.mult))
            for odd in (15, 13, 11, 9, 7, 5, 3):
                link(nc.vector.scalar_tensor_tensor(ser[:, :], ser[:, :], 1.0 / odd, sq[:, :], ALU.add, ALU.mult))
            link(nc.vector.scalar_tensor_tensor(ser[:, :], ser[:, :], 1.0, em[:, :], ALU.add, ALU.mult))
            link(nc.vector.tensor_scalar(ser[:, :], ser[:, :], 2.0, None, ALU.mult))
            link(nc.vector.scalar_tensor_tensor(ser[:, :], a_a[:, :], 0.0, ser[:, :], ALU.max, ALU.add))
            dve.wait_ge(e_ready, 2)
            link(nc.vector.scalar_tensor_tensor(g[:, :], ser[:, :], -1.0, a_exp[:, :], ALU.mult, ALU.mult))
            link(nc.vector.tensor_scalar(g[:, :], g[:, :], LOG_DECAY_MIN, None, ALU.max))
            link(nc.vector.tensor_scalar(g_hi[:, :], g[:, :], ROUND, -ROUND, ALU.add, ALU.add))
            nc.vector.tensor_tensor(g_lo[:, :], g[:, :], g_hi[:, :], ALU.subtract).then_inc(g_ready, 1)
            dve.wait_ge(prob_exp, 1)
            link(nc.vector.tensor_reduce(top[:, :], pr[:, :, :], AX.X, ALU.add))
            link(nc.vector.reciprocal(top[:, :], top[:, :]))
            link(nc.vector.tensor_tensor(pr[:, :, :], pr[:, :, :], top[:, :].unsqueeze(2).to_broadcast([P, TILES, E]), ALU.mult))
            iota = cst[:, IOTA:IOTA + E].unsqueeze(1).to_broadcast([P, TILES, E])

            def pick(hot, src):
                link(nc.vector.tensor_reduce(top[:, :], src[:, :, :], AX.X, ALU.max))
                topb = top[:, :].unsqueeze(2).to_broadcast([P, TILES, E])
                link(nc.vector.tensor_tensor(hit[:, :, :], src[:, :, :], topb, ALU.is_equal))
                link(nc.vector.tensor_tensor(hit[:, :, :], hit[:, :, :], iota, ALU.mult))
                link(nc.vector.tensor_reduce(top[:, :], hit[:, :, :], AX.X, ALU.min))
                link(nc.vector.tensor_tensor(hot[:, :, :], iota, topb, ALU.is_equal))

            pick(hot1, pr)
            link(nc.vector.scalar_tensor_tensor(hot2[:, :, :], hot1[:, :, :], -2.0, pr[:, :, :], ALU.mult, ALU.add))
            link(nc.vector.tensor_copy(comb[:, :, 0:E], hot2[:, :, :]))
            pick(hot2, comb[:, :, 0:E])
            link(nc.vector.tensor_tensor(hot1[:, :, :], hot1[:, :, :], hot2[:, :, :], ALU.add))
            nc.vector.tensor_tensor(comb[:, :, 0:E], hot1[:, :, :], pr[:, :, :], ALU.mult).then_inc(comb_ready, 1)
            dve.wait_ge(sums_out, 2)
            nc.vector.tensor_tensor(sum_g[:, :], sum_hi[:, :], sum_lo[:, :], ALU.add).then_inc(sumg_ready, 1)
            dve.wait_ge(gam_ready, 1)
            link(nc.vector.tensor_scalar(prep[:, :, NGAM * U:(NGAM + 1) * U], prep[:, :, GAM * U:(GAM + 1) * U],
                                         -1.0, None, ALU.mult))

        @block.gpsimd
        def _(pool):
            pool.wait_ge(var_ready, 1)
            nc.gpsimd.tensor_tensor(rstd[:, :], var[:, :], expo[:, :], ALU.pow).then_inc(pow_done, 1)

        @block.scalar
        def _(act):
            act.sem_inc(xt_kept, BASE)
            with act.Fori(0, BATCH) as b:
                for c in range(NC_):
                    k = c % 2
                    act.wait_ge(xnt_ps, b * NC_ + c + 1 + BASE)
                    act.wait_ge(small_ps, b * NC_ + max(c - 1, 0) + BASE)
                    nc.scalar.activation(xt[:, k, :], ps_t[k][:, 0:D], ACT.Copy).then_inc(xt_ready, 1)
                    nc.scalar.activation(xnT[:, :, bass.ds((b * NC_ + c) * P, P)],
                                         ps_t[k][:, 0:D].rearrange("p (k t) -> p k t", k=KT), ACT.Copy).then_inc(xt_kept, 1)
            act.wait_ge(small_out, 4 * TILES)
            act.wait_ge(w_loaded, 64)

            def units(ap):
                return ap.rearrange("p (s u) -> p s u", u=U)

            nc.scalar.activation(prep[:, :, BETA * U:(BETA + 1) * U], units(a_b[:, :]), ACT.Sigmoid).then_inc(act_s, 1)
            nc.scalar.activation(comb[:, :, E:E + 1], routed[:, :, E:E + 1], ACT.Sigmoid).then_inc(sg_ready, 1)
            act.wait_ge(u_ready, 1)
            nc.scalar.activation(absu[:, :], a_a[:, :], ACT.Abs).then_inc(act_s, 1)
            act.wait_ge(act_s, 2)
            nc.scalar.activation(em[:, :], absu[:, :], ACT.Exp, scale=-1.0).then_inc(e_ready, 1)
            nc.scalar.activation(a_exp[:, :], a_exp[:, :], ACT.Exp).then_inc(e_ready, 1)
            act.wait_ge(logit_ready, 1)
            nc.scalar.activation(pr[:, :, :], pr[:, :, :], ACT.Exp).then_inc(prob_exp, 1)
            act.wait_ge(sums_ps, 4)
            nc.scalar.activation(sum_hi[:, :], ps_g[0][:, :], ACT.Copy).then_inc(sums_out, 1)
            nc.scalar.activation(sum_lo[:, :], ps_g[1][:, :], ACT.Copy).then_inc(sums_out, 1)
            nc.scalar.activation(prep[:, :, WSUF * U:(WSUF + 1) * U], units(ps_g[2][:, :]), ACT.Exp).then_inc(act_s, 1)
            nc.scalar.activation(prep[:, :, GAMC * U:(GAMC + 1) * U], units(ps_g[3][:, :]), ACT.Exp).then_inc(act_s, 1)
            act.wait_ge(sumg_ready, 1)
            nc.scalar.activation(prep[:, :, GAM * U:(GAM + 1) * U], units(sum_g[:, :]), ACT.Exp).then_inc(gam_ready, 1)
            act.wait_ge(rows_ps, 2)
            for k in range(4):
                nc.scalar.activation(rows[:, k, :], ps_t[k % 2][:, :], ACT.Copy,
                                     scale=1.0 if k < 2 else -1.0).then_inc(rows_out, 1)
            act.wait_ge(comb_ps, 1)
            nc.scalar.activation(combT[:, 0, :], ps_s[0][:, 0:P], ACT.Copy).then_inc(comb_out, 1)
            rest = TILES * (E + 1) - P
            nc.scalar.activation(combT[0:rest, 1, :], ps_s[1][0:rest, 0:P], ACT.Copy).then_inc(comb_out, 1)

        @block.tensor
        def _(pe):
            ident = cst[:, IDENT:IDENT + P]
            pe.sem_inc(xnt_ps, BASE)
            pe.sem_inc(small_ps, BASE)
            pe.wait_ge(w_loaded, 64)
            with pe.Fori(0, BATCH) as b:
                for c in range(NC_):
                    k = c % 2
                    pe.wait_ge(xn_ready, b * NC_ + c + 1)
                    pe.wait_ge(xt_kept, b * NC_ + max(c - 1, 0) + BASE)
                    for m in range(KT):
                        last = nc.tensor.transpose(ps_t[k][:, m * P:(m + 1) * P], xn[:, k, m * P:(m + 1) * P], ident)
                    last.then_inc(xnt_ps, 1)
                    pe.wait_ge(xt_ready, b * NC_ + c + 1)
                    pe.wait_ge(small_out, TILES + 3 * (b * NC_ + max(c - 1, 0)))
                    for m in range(KT):
                        last = nc.tensor.matmul(ps_s[k][:, 0:NSMALL], xt[:, k, m * P:(m + 1) * P], ws[:, m, :],
                                                start=(m == 0), stop=(m == KT - 1))
                    last.then_inc(small_ps, 1)
            pe.wait_ge(g_ready, 1)
            for k, (at, src) in enumerate(((UPTO, g_hi), (UPTO, g_lo), (AFTER, g), (ONES, g))):
                nc.tensor.matmul(ps_g[k][:, :], cst[:, at:at + P], src[:, :], start=True, stop=True).then_inc(sums_ps, 1)
            pe.wait_ge(sums_out, 2)
            for k, src in enumerate((sum_hi, sum_lo)):
                for q in range(UNITS // P):
                    last = nc.tensor.transpose(ps_t[k][:, q * P:(q + 1) * P], src[:, q * P:(q + 1) * P], ident)
                last.then_inc(rows_ps, 1)
            pe.wait_ge(comb_ready, 1)
            pe.wait_ge(sg_ready, 1)
            flat = comb[:, :, :].rearrange("p t e -> p (t e)")
            rest = TILES * (E + 1) - P
            nc.tensor.transpose(ps_s[0][:, 0:P], flat[:, 0:P], ident)
            nc.tensor.transpose(ps_s[1][0:rest, 0:P], flat[:, P:P + rest], ident).then_inc(comb_ps, 1)


def ffn_block(nc, wg_dram, wu_dram, wd_dram, keep, comb_rows):
    xnT, gate = keep["xnT"], keep["gate"]
    spans = []
    for j in range(FT):
        at = j * P
        while at < (j + 1) * P:
            e = min(at // I_MOE, E)
            end = (j + 1) * P if e == E else min((e + 1) * I_MOE, (j + 1) * P)
            spans.append((j, at - j * P, end - j * P, e))
            at = end
    GROUPS = ((0, 1), (1, 4), (4, 9), (9, FT))
    comb_v = comb_rows.rearrange("(t e) c -> t e c", e=E + 1)
    with ExitStack() as ctx:
        def sb(name, shape, dt=F32):
            return ctx.enter_context(nc.sbuf_tensor(name, shape, dt))

        def sem(name):
            return ctx.enter_context(nc.semaphore(name))

        wg = sb("wg", [P, KT, FT * P])
        wu = sb("wu", [P, KT, FT * P])
        wd = sb("wd", [P, FT, D])
        hid = sb("hid", [P, FT, T])
        scale = sb("scale", [P, FT, T])
        silu_g = sb("silu_g", [P, 2, T])
        ps_g = [ctx.enter_context(nc.psum_tensor(f"fps_g{k}", [P, 512], F32)) for k in range(2)]
        ps_u = [ctx.enter_context(nc.psum_tensor(f"fps_u{k}", [P, 512], F32)) for k in range(2)]
        ps_o = [ctx.enter_context(nc.psum_tensor(f"fps_o{k}", [P, 512], F32)) for k in range(2)]
        w_in, wd_in, scale_in = [sem(f"ffn_w_in{k}") for k in range(len(GROUPS))], sem("wd_in"), sem("scale_in")
        g_ps, u_ps, silu_done, prod_done, hid_done = sem("g_ps"), sem("u_ps"), sem("silu_done"), sem("prod_done"), sem("hid_done")
        o_ps, gate_done = sem("o_ps"), sem("gate_done")
        block = ctx.enter_context(nc.Block())

        @block.sync
        def _(sp):
            for k, (j0, j1) in enumerate(GROUPS):
                cols = slice(j0 * P, j1 * P)
                sp.dma_start(wg[:, :, cols], wg_dram[:, :, cols]).then_inc(w_in[k], 16)
                sp.dma_start(wu[:, :, cols], wu_dram[:, :, cols]).then_inc(w_in[k], 16)
            sp.dma_start(wd[:, :, :], wd_dram).then_inc(wd_in, 16)

        @block.gpsimd
        def _(pool):
            with pool.Fori(0, BATCH) as b:
                pool.wait_ge(hid_done, b * FT + BASE)
                for j, p0, p1, e in spans:
                    src = comb_v[bass.ds(b * NC_, NC_), e, :].unsqueeze(0).to_broadcast([p1 - p0, NC_, P])
                    nc.gpsimd.dma_start(scale[p0:p1, j, :].rearrange("p (c t) -> p c t", c=NC_), src).then_inc(scale_in, 16)

        @block.scalar
        def _(act):
            act.sem_inc(silu_done, BASE)
            act.sem_inc(gate_done, BASE)
            with act.Fori(0, BATCH) as b:
                for j in range(FT):
                    act.wait_ge(g_ps, b * FT + j + 1)
                    act.wait_ge(hid_done, b * FT + max(j - 1, 0) + BASE)
                    nc.scalar.activation(silu_g[:, j % 2, :], ps_g[j % 2][:, :], ACT.Silu).then_inc(silu_done, 1)
                for c in range(NC_):
                    act.wait_ge(o_ps, b * NC_ + c + 1 + BASE)
                    nc.scalar.activation(gate[:, bass.ds(b * NC_ + c, 1), :], ps_o[c % 2][:, 0:D],
                                         ACT.Silu).then_inc(gate_done, 1)

        @block.vector
        def _(dve):
            dve.sem_inc(prod_done, BASE)
            dve.sem_inc(hid_done, BASE)
            with dve.Fori(0, BATCH) as b:
                dve.wait_ge(scale_in, b * (16 * len(spans)) + 16 * len(spans))
                for j in range(FT):
                    dve.wait_ge(silu_done, b * FT + j + 1 + BASE)
                    dve.wait_ge(u_ps, b * FT + j + 1)
                    if j == 0:
                        dve.wait_ge(o_ps, b * NC_ + BASE)
                    nc.vector.tensor_tensor(silu_g[:, j % 2, :], ps_u[j % 2][:, :], silu_g[:, j % 2, :],
                                            ALU.mult).then_inc(prod_done, 1)
                    dve.wait_ge(prod_done, b * FT + j + 1 + BASE)
                    nc.vector.tensor_tensor(hid[:, j, :], silu_g[:, j % 2, :], scale[:, j, :],
                                            ALU.mult).then_inc(hid_done, 1)

        @block.tensor
        def _(pe):
            pe.sem_inc(o_ps, BASE)
            with pe.Fori(0, BATCH) as b:
                for j in range(FT):
                    for k, (j0, _) in enumerate(GROUPS):
                        if j == j0:
                            pe.wait_ge(w_in[k], 32)
                    pe.wait_ge(silu_done, b * FT + max(j - 1, 0) + BASE)
                    pe.wait_ge(prod_done, b * FT + max(j - 1, 0) + BASE)
                    for w, ps, done in ((wg, ps_g, g_ps), (wu, ps_u, u_ps)):
                        for m in range(KT):
                            last = nc.tensor.matmul(ps[j % 2][:, :], w[:, m, j * P:(j + 1) * P],
                                                    xnT[:, m, bass.ds(b * T, T)], start=(m == 0), stop=(m == KT - 1))
                        last.then_inc(done, 1)
                pe.wait_ge(wd_in, 16)
                for c in range(NC_):
                    pe.wait_ge(gate_done, b * NC_ + max(c - 1, 0) + BASE)
                    if c == 0:
                        pe.wait_ge(hid_done, b * FT + FT + BASE)
                    for j in range(FT):
                        last = nc.tensor.matmul(ps_o[c % 2][:, 0:D], hid[:, j, c * P:(c + 1) * P], wd[:, j, :],
                                                start=(j == 0), stop=(j == FT - 1))
                    last.then_inc(o_ps, 1)


def recurrent_block(nc, x, w_in_dram, w_z_dram, w_out_dram, norm_dram, keep, g_rows, out):
    cst, xnT, prep, gate = keep["cst"], keep["xnT"], keep["prep"], keep["gate"]
    with ExitStack() as ctx:
        def sb(name, shape, dt=F32):
            return ctx.enter_context(nc.sbuf_tensor(name, shape, dt))

        def sem(name):
            return ctx.enter_context(nc.semaphore(name))

        acc = sb("acc", [P, TILES, D])
        w_in = sb("w_in", [P, KT * 4 * P + 4 * KC])
        w_z = sb("w_z", [P, KT, REP * P])
        w_out = sb("w_out", [P, REP, D])
        w_outn = sb("w_outn", [P, REP, D])
        norm_w = sb("norm_w", [P, 1])
        hide = sb("hide", [P, NC_, C], BF16)
        identb = sb("identb", [P, P], BF16)
        lrow = sb("lrow", [4, U * C])
        rrow = sb("rrow", [4, U * C])
        cols = [sb(f"cols{k}", [P, KINDS * U]) for k in range(2)]
        eps8 = sb("eps8", [P, U])
        half8 = sb("half8", [P, U])
        qk_scale8 = sb("qk_scale8", [P, U])
        decay = sb("decay", [P, U, C])
        conv = sb("conv", [P, 4, T])
        mixed = sb("mixed", [P, 4, T])
        qk_sq = sb("qk_sq", [P, U])
        qk_t = sb("qk_t", [P, U])
        qk_p = sb("qk_p", [P, U])
        qk_r = sb("qk_r", [P, U])
        qk = sb("qk", [P, U, P])
        qkT = [sb(f"qkT{k}", [P, 2, T]) for k in range(2)]
        v = [sb(f"v{k}", [P, U, P]) for k in range(2)]
        kw = [sb(f"kw{k}", [P, U, P]) for k in range(2)]
        scores = [sb(f"scores{k}", [P, U, C]) for k in range(2)]
        bmat = sb("bmat", [P, U, C])
        bm1 = sb("bm1", [P, U, C])
        bs = [[sb(f"bs{g}{k}", [P, NC_, C]) for k in range(2)] for g in range(REP)]
        inv = [sb(f"inv{k}", [P, U, C]) for k in range(2)]
        invT = sb("invT", [P, U, C])
        wneg = sb("wneg", [P, U, C])
        state = sb("state", [P, REP * P])
        resid = sb("resid", [P, REP * P])
        from_state = sb("from_state", [P, REP * P])
        upd = sb("upd", [P, REP * P])
        o = sb("o", [P, NC_, REP * P])
        o_sq = sb("o_sq", [P, U])
        o_t = sb("o_t", [P, U])
        o_r = sb("o_r", [P, U])
        inv128 = sb("inv128", [P, U])
        z = sb("z", [P, NC_, REP * P])
        gated = sb("gated", [P, NC_, REP * P])
        gatedT = sb("gatedT", [P, REP, T])
        ps = [ctx.enter_context(nc.psum_tensor(f"rps{k}", [P, 512], F32)) for k in range(8)]

        rows_in, cols_in, win_in, wz_in, wout_in, norm_in = (sem(s) for s in ("rows_in", "cols_in", "win_in", "wz_in", "wout_in", "norm_in"))
        init = sem("init")
        passed = sem("passed")
        dt_ps, proj_ps, qk_ps, v_ps, qkT_ps, kk_ps, b1_ps, w_ps, xy_ps = (
            sem(s) for s in ("dt_ps", "proj_ps", "qk_ps", "v_ps", "qkT_ps", "kk_ps", "b1_ps", "w_ps", "xy_ps"))
        z_ps, ks_ps, qs_ps, u_ps, o_ps, gT_ps, out_ps = (
            sem(s) for s in ("z_ps", "ks_ps", "qs_ps", "u_ps", "o_ps", "gT_ps", "out_ps"))
        decay_done, conv0_done, mixed_done, sq_done, qk_done, v_done, qkT_done, w_done = (
            sem(s) for s in ("decay_done", "conv0_done", "mixed_done", "sq_done", "qk_done", "v_done", "qkT_done", "w_done"))
        z_done, fs_done, upd_done, osq_done, gT_done, wout_done = (
            sem(s) for s in ("z_done", "fs_done", "upd_done", "osq_done", "gT_done", "wout_done"))
        tap_done, conv_done, b_done, m_done, kw_done, inv1_done, inv_done = (
            sem(s) for s in ("tap_done", "conv_done", "b_done", "m_done", "kw_done", "inv1_done", "inv_done"))
        r_done, st_done, o_done, gated_done, acc_done = (sem(s) for s in ("r_done", "st_done", "o_done", "gated_done", "acc_done"))
        qk_pow, b1_done, x1_done, bs_done, o_pow = (sem(s) for s in ("qk_pow", "b1_done", "x1_done", "bs_done", "o_pow"))
        x_in, stored, final = sem("x_in"), sem("stored"), sem("final")
        x_back = [t[:, :, :].rearrange("p a n -> p (a n)")[:, 0:NC_ * D] for t in (decay, bmat, conv, mixed)]
        block = ctx.enter_context(nc.Block())

        DEC = 2 * NL
        INV = 4 * NL - 2

        @block.sync
        def _(sp):
            sp.dma_start(norm_w[:, :], norm_dram).then_inc(norm_in, 16)
            sp.dma_start(w_z[:, :, :], w_z_dram[0]).then_inc(wz_in, 16)
            sp.dma_start(w_out[:, :, :], w_out_dram[0]).then_inc(wout_in, 16)
            sp.wait_ge(init, 1)
            with sp.Fori(0, NK) as i:
                proj_used, taps_used = sp.snap(i * (4 * BATCH) + BASE), sp.snap(i * (12 * BATCH) + BASE)
                sp.wait_ge(proj_ps, proj_used)
                sp.sem_inc(passed, 1)
                sp.wait_ge(tap_done, taps_used)
                sp.sem_inc(passed, 1)
                sp.dma_start(w_in[:, :], w_in_dram[bass.ds(i, 1)].rearrange("o p n -> (o p) n")).then_inc(win_in, 16)
                for b in range(BATCH):
                    step = sp.snap(i * BATCH + b)
                    at = sp.snap(step * (U * C))
                    rows_used = sp.snap(step * 2 + BASE)
                    sp.wait_ge(dt_ps, rows_used)
                    sp.sem_inc(passed, 1)
                    sp.dma_start(lrow[1:4:2, :], g_rows[2:4, bass.ds(at, U * C)]).then_inc(rows_in, 16)
                    sp.dma_start(rrow[0:3:2, :], g_rows[0:2, bass.ds(at, U * C)]).then_inc(rows_in, 16)
                    upd_used, st_used, fs_used = sp.snap(step * 4 + BASE), sp.snap(step * 5 + BASE), sp.snap(step * 6 + BASE)
                    sp.wait_ge(upd_done, upd_used)
                    sp.sem_inc(passed, 1)
                    sp.wait_ge(st_done, st_used)
                    sp.sem_inc(passed, 1)
                    sp.wait_ge(fs_done, fs_used)
                    sp.sem_inc(passed, 1)
                    sp.dma_start(cols[b % 2][:, :], prep[:, bass.ds(step, 1), :]).then_inc(cols_in, 16)
                    if b == 0:
                        z_used, out_used = sp.snap(i * (2 * BATCH) + 2 + BASE), sp.snap(i + 1)
                        sp.wait_ge(z_ps, z_used)
                        sp.sem_inc(passed, 1)
                        sp.dma_start(w_z[:, :, :], w_z_dram[bass.ds(i, 1)].rearrange("o p k n -> (o p) k n")).then_inc(wz_in, 16)
                        sp.wait_ge(wout_done, out_used)
                        sp.sem_inc(passed, 1)
                        sp.dma_start(w_out[:, :, :], w_out_dram[bass.ds(i, 1)].rearrange("o p v n -> (o p) v n")).then_inc(wout_in, 16)
            for k, (used, count) in enumerate(((m_done, 2), (bs_done, DEC), (mixed_done, 4), (v_ps, 2))):
                sp.wait_ge(used, STEPS * count + BASE)
                sp.dma_start(x_back[k].rearrange("p (c d) -> p c d", c=NC_),
                             x[k].rearrange("(c p) d -> p c d", p=P)).then_inc(x_in, 16)
            sp.wait_ge(final, BATCH)
            for b in range(BATCH):
                sp.dma_start(out[b].rearrange("(c p) d -> p c d", p=P), acc[:, b * NC_:(b + 1) * NC_, :]).then_inc(stored, 16)
            sp.wait_ge(stored, 16 * BATCH)

        @block.tensor
        def _(pe):
            ident = cst[:, IDENT:IDENT + P]

            def stage_two(r, tb, n, wloads):
                def read_state(c):
                    pe.wait_ge(st_done, n(5) + (2 * c - 1))
                    pe.wait_ge(upd_done, n(4) + c)
                    pe.wait_ge(o_done, n(4) + c)
                    cs = slice(c * C, (c + 1) * C)
                    nc.tensor.matmul(ps[6][:, 0:REP * P], qkT[r][:, 1, cs], state[:, :], start=True, stop=True).then_inc(ks_ps, 1)
                    nc.tensor.matmul(ps[7][:, 0:REP * P], qkT[r][:, 0, cs], state[:, :], start=True, stop=True).then_inc(qs_ps, 1)

                def solve(c):
                    if c:
                        pe.wait_ge(r_done, n(6) + 2 * c)
                    else:
                        pe.wait_ge(acc_done, n(2))
                    for g in range(REP):
                        rhs = resid[:, g * P:(g + 1) * P] if c else v[r][:, g * NC_, :]
                        last = nc.tensor.matmul(ps[6][:, g * P:(g + 1) * P], inv[r][:, g * NC_ + c, :], rhs,
                                                start=True, stop=True)
                    last.then_inc(u_ps, 1)

                def attend(c):
                    pe.wait_ge(upd_done, n(4) + c + 1)
                    if c:
                        pe.wait_ge(fs_done, n(6) + 2 * c)
                    for g in range(REP):
                        last = nc.tensor.matmul(ps[7][:, g * P:(g + 1) * P], scores[r][:, g * NC_ + c, :],
                                                upd[:, g * P:(g + 1) * P], start=True, stop=True)
                    if c < NC_ - 1:
                        for g in range(REP):
                            last = nc.tensor.matmul(ps[7][:, (REP + g) * P:(REP + g + 1) * P], kw[r][:, g * NC_ + c, :],
                                                    upd[:, g * P:(g + 1) * P], start=True, stop=True)
                    last.then_inc(o_ps, 1)

                def gated_transpose():
                    pe.wait_ge(gated_done, n(8) + 8)
                    for g in range(REP):
                        for c in range(NC_):
                            last = nc.tensor.transpose(ps[6 + g][:, c * C:(c + 1) * C], gated[:, c, g * P:(g + 1) * P], ident)
                        last.then_inc(gT_ps, 1)

                def project_out():
                    pe.wait_ge(gT_done, n(2) + 2)
                    pe.wait_ge(wout_done, wloads)
                    for h in range(2):
                        for c in (2 * h, 2 * h + 1):
                            for g in range(REP):
                                last = nc.tensor.matmul(ps[6 + h][:, (c % 2) * D:(c % 2 + 1) * D],
                                                        gatedT[:, g, c * C:(c + 1) * C], w_outn[:, g, :],
                                                        start=(g == 0), stop=(g == REP - 1))
                        last.then_inc(out_ps, 1)

                def project_z():
                    pe.wait_ge(wz_in, wloads * 16)
                    for h in range(2):
                        for c in (2 * h, 2 * h + 1):
                            for m in range(KT):
                                last = nc.tensor.matmul(ps[h][:, (c % 2) * D:(c % 2 + 1) * D],
                                                        xnT[:, m, tb * T + c * C:tb * T + (c + 1) * C], w_z[:, m, :],
                                                        start=(m == 0), stop=(m == KT - 1))
                        last.then_inc(z_ps, 1)

                return read_state, solve, attend, gated_transpose, project_out, project_z

            for s in (dt_ps, proj_ps, qk_ps, v_ps, qkT_ps, kk_ps, b1_ps, w_ps, xy_ps,
                      z_ps, ks_ps, qs_ps, u_ps, o_ps, gT_ps, out_ps):
                pe.sem_inc(s, BASE)
            pe.wait_ge(init, 5)
            with pe.Fori(0, NK) as i:
                for b in range(BATCH):
                    p = b % 2

                    def n(k, i=i, b=b):
                        return i * (k * BATCH) + k * b + BASE

                    read_state, solve, attend, gated_transpose, project_out, project_z = stage_two(
                        1 - p, (b - 1) % BATCH, n, i + (1 if b == 0 else 2))
                    pe.wait_ge(inv_done, n(INV))
                    pe.wait_ge(rows_in, n(32) - BASE + 32)
                    for g in range(REP):
                        nc.tensor.matmul(ps[4 + g][:, :], identb[:, :], hide[:, :, :].rearrange("p c t -> p (c t)"),
                                         start=True, stop=False)
                        for c in range(NC_):
                            at = slice((g * NC_ + c) * C, (g * NC_ + c + 1) * C)
                            last = nc.tensor.matmul(ps[4 + g][:, c * C:(c + 1) * C], lrow[:, at], rrow[:, at],
                                                    start=False, stop=(c == NC_ - 1))
                        last.then_inc(dt_ps, 1)
                    project_z()
                    solve(0)
                    pe.wait_ge(win_in, i * 16 + 16)
                    for j in range(4):
                        if j == 2:
                            attend(0)
                            pe.wait_ge(z_done, n(2) + 2)
                        for m in range(KT):
                            last = nc.tensor.matmul(ps[(2, 3, 0, 1)[j]][:, :], w_in[:, m * 4 * P + j * P:m * 4 * P + (j + 1) * P],
                                                    xnT[:, m, b * T:(b + 1) * T], start=(m == 0), stop=(m == KT - 1))
                        last.then_inc(proj_ps, 1)
                    read_state(1)
                    pe.wait_ge(decay_done, n(2) + 2)
                    for j in range(2):
                        pe.wait_ge(mixed_done, n(4) + j + 1)
                        for c in range(NC_):
                            last = nc.tensor.transpose(ps[4 + j][:, c * C:(c + 1) * C], mixed[:, j, c * C:(c + 1) * C], ident)
                        last.then_inc(qk_ps, 1)
                    solve(1)
                    for j in range(2):
                        pe.wait_ge(mixed_done, n(4) + j + 3)
                        for c in range(NC_):
                            last = nc.tensor.transpose(ps[j][:, c * C:(c + 1) * C], mixed[:, 2 + j, c * C:(c + 1) * C], ident)
                        last.then_inc(v_ps, 1)
                    attend(1)
                    for j in range(2):
                        pe.wait_ge(qk_done, n(8) + 4 * j + 4)
                        for c in range(NC_):
                            last = nc.tensor.transpose(ps[2 + j][:, c * C:(c + 1) * C], qk[:, j * NC_ + c, :], ident)
                        last.then_inc(qkT_ps, 1)
                    read_state(2)
                    pe.wait_ge(qkT_done, n(2) + 2)
                    for j, other in enumerate((1, 0)):
                        for c in range(NC_):
                            cs = slice(c * C, (c + 1) * C)
                            last = nc.tensor.matmul(ps[4 + j][:, cs], qkT[p][:, 1, cs], qkT[p][:, other, cs], start=True, stop=True)
                        last.then_inc(kk_ps, 1)
                    solve(2)
                    attend(2)
                    for g in range(REP):
                        pe.wait_ge(b1_done, n(2) + g + 1)
                        for c in range(NC_):
                            last = nc.tensor.transpose(ps[2 + g][:, c * C:(c + 1) * C], bm1[:, g * NC_ + c, :], ident)
                        last.then_inc(b1_ps, 1)
                    for lv in range(NL):
                        for g in range(REP):
                            pe.wait_ge(bs_done, n(DEC) + 2 * lv + g + 1)
                            if lv == 0:
                                pe.wait_ge(inv1_done, n(2) + g + 1)
                                pe.wait_ge(v_done, n(2) + 2)
                            else:
                                pe.wait_ge(inv_done, n(INV) + 4 * (lv - 1) + 2 * g + 2)
                            for c in range(NC_):
                                last = nc.tensor.matmul(ps[g][:, c * C:(c + 1) * C], bs[g][lv % 2][:, c, :],
                                                        invT[:, g * NC_ + c, :], start=True, stop=True)
                            last.then_inc(w_ps, 1)
                        if lv == 0:
                            read_state(3)
                        if lv == 1:
                            attend(3)
                        for g in range(REP):
                            pe.wait_ge(w_done, n(DEC) + 2 * lv + g + 1)
                            if lv == 0:
                                pe.wait_ge(x1_done, n(2) + g + 1)
                                pe.wait_ge(b_done, n(8) + 8)
                                pe.wait_ge(m_done, n(2) + 2)
                                pe.wait_ge(inv1_done, n(2) + 2)
                            for c in range(NC_):
                                u = g * NC_ + c
                                last = nc.tensor.matmul(ps[2 + 2 * g][:, c * C:(c + 1) * C], wneg[:, u, :], inv[p][:, u, :],
                                                        start=True, stop=True)
                            if lv < NL - 1:
                                for c in range(NC_):
                                    u = g * NC_ + c
                                    last = nc.tensor.matmul(ps[3 + 2 * g][:, c * C:(c + 1) * C], inv[p][:, u, :], wneg[:, u, :],
                                                            start=True, stop=True)
                            last.then_inc(xy_ps, 1)
                        if lv == 0:
                            solve(3)
                        if lv == NL - 2:
                            gated_transpose()
                    project_out()
            def n_end(k):
                return STEPS * k + BASE

            read_state, solve, attend, gated_transpose, project_out, project_z = stage_two(1, BATCH - 1, n_end, NK + 1)
            pe.wait_ge(inv_done, n_end(INV))
            project_z()
            for c in range(NC_):
                if c:
                    read_state(c)
                solve(c)
                attend(c)
            gated_transpose()
            project_out()

        @block.scalar
        def _(act):
            def col(r, kind, u):
                return cols[r][:, kind * U + u:kind * U + u + 1]

            def stage_two(r, n):
                def take_updates(c):
                    act.wait_ge(u_ps, n(4) + c + 1)
                    act.wait_ge(o_ps, n(4) + c)
                    for g in range(REP):
                        last = nc.scalar.activation(upd[:, g * P:(g + 1) * P], ps[6][:, g * P:(g + 1) * P], ACT.Copy,
                                                    scale=col(r, BETA, g * NC_ + c))
                    last.then_inc(upd_done, 1)

                def take_state_part(c):
                    act.wait_ge(qs_ps, n(3) + c)
                    act.wait_ge(o_done, n(4) + c)
                    for g in range(REP):
                        nc.scalar.activation(from_state[:, g * P:(g + 1) * P], ps[7][:, g * P:(g + 1) * P], ACT.Copy,
                                             scale=col(r, GAM, g * NC_ + c)).then_inc(fs_done, 1)

                def squares(c):
                    act.wait_ge(o_done, n(4) + c + 1)
                    if c == 0:
                        act.wait_ge(o_pow, n(3))
                        act.wait_ge(gT_ps, n(2))
                    for g in range(REP):
                        u = g * NC_ + c
                        last = nc.scalar.activation(gated[:, c, g * P:(g + 1) * P], o[:, c, g * P:(g + 1) * P], ACT.Square, accum_out=o_sq[:, u:u + 1])
                    last.then_inc(osq_done, 1)

                def take_transposes():
                    act.wait_ge(out_ps, n(2))
                    for g in range(REP):
                        act.wait_ge(gT_ps, n(2) + g + 1)
                        nc.scalar.activation(gatedT[:, g, :], ps[6 + g][:, :], ACT.Copy).then_inc(gT_done, 1)

                def gate_z():
                    act.wait_ge(gated_done, n(8))
                    for h in range(2):
                        act.wait_ge(z_ps, n(2) + h + 1)
                        nc.scalar.activation(z[:, 2 * h:2 * h + 2, :], ps[h][:, :].rearrange("p (c d) -> p c d", c=2),
                                             ACT.Silu).then_inc(z_done, 1)

                return take_updates, take_state_part, squares, take_transposes, gate_z

            def scale_out_weights(loads):
                act.wait_ge(wout_in, loads * 16)
                nc.scalar.activation(w_outn[:, :, :], w_out[:, :, :], ACT.Copy, scale=norm_w[:, 0:1]).then_inc(wout_done, 1)

            for s in (decay_done, conv0_done, mixed_done, sq_done, qk_done, v_done, qkT_done, w_done,
                      z_done, fs_done, upd_done, osq_done, gT_done):
                act.sem_inc(s, BASE)
            act.wait_ge(norm_in, 16)
            act.wait_ge(init, 5)
            scale_out_weights(1)
            with act.Fori(0, NK) as i:
                for b in range(BATCH):
                    p = b % 2

                    def n(k, i=i, b=b):
                        return i * (k * BATCH) + k * b + BASE

                    take_updates, take_state_part, squares, take_transposes, gate_z = stage_two(1 - p, n)
                    act.wait_ge(b_done, n(8))
                    act.wait_ge(m_done, n(2))
                    for g in range(REP):
                        act.wait_ge(dt_ps, n(2) + g + 1)
                        nc.scalar.activation(decay[:, g * NC_:(g + 1) * NC_, :],
                                             ps[4 + g][:, :].rearrange("p (c t) -> p c t", c=NC_), ACT.Exp).then_inc(decay_done, 1)
                    gate_z()
                    if b == 1:
                        act.wait_ge(out_ps, n(2))
                        scale_out_weights(i + 2)
                    take_updates(0)
                    for j in range(4):
                        if j == 2:
                            squares(0)
                        act.wait_ge(proj_ps, n(4) + j + 1)
                        if j == 0:
                            act.wait_ge(mixed_done, n(4))
                        nc.scalar.activation(conv[:, j, :], ps[(2, 3, 0, 1)[j]][:, :], ACT.Copy,
                                             scale=w_in[:, KT * 4 * P + j * KC + KC - 1:KT * 4 * P + (j + 1) * KC]).then_inc(conv0_done, 1)
                    take_state_part(1)
                    act.wait_ge(qk_ps, n(2))
                    for j in range(2):
                        act.wait_ge(conv_done, n(4) + j + 1)
                        nc.scalar.activation(mixed[:, j, :], conv[:, j, :], ACT.Silu).then_inc(mixed_done, 1)
                    take_updates(1)
                    act.wait_ge(v_ps, n(2))
                    act.wait_ge(qk_pow, n(3))
                    for j in range(2):
                        act.wait_ge(qk_ps, n(2) + j + 1)
                        for c in range(NC_):
                            u = j * NC_ + c
                            nc.scalar.activation(kw[p][:, u, :], ps[4 + j][:, c * C:(c + 1) * C], ACT.Square,
                                                 accum_out=qk_sq[:, u:u + 1]).then_inc(sq_done, 1)
                        act.wait_ge(conv_done, n(4) + j + 3)
                        nc.scalar.activation(mixed[:, 2 + j, :], conv[:, 2 + j, :], ACT.Silu).then_inc(mixed_done, 1)
                    squares(1)
                    act.wait_ge(qk_pow, n(3) + 3)
                    act.wait_ge(qkT_ps, n(2))
                    act.wait_ge(kw_done, n(8))
                    for j in range(2):
                        for c in range(NC_):
                            u = j * NC_ + c
                            nc.scalar.activation(qk[:, u, :], ps[4 + j][:, c * C:(c + 1) * C], ACT.Copy,
                                                 scale=qk_r[:, u:u + 1]).then_inc(qk_done, 1)
                    for j in range(2):
                        act.wait_ge(v_ps, n(2) + j + 1)
                        nc.scalar.activation(v[p][:, j * NC_:(j + 1) * NC_, :], ps[j][:, :].rearrange("p (c t) -> p c t", c=NC_),
                                             ACT.Copy).then_inc(v_done, 1)
                    take_state_part(2)
                    for j in range(2):
                        act.wait_ge(qkT_ps, n(2) + j + 1)
                        nc.scalar.activation(qkT[p][:, j, :], ps[2 + j][:, :], ACT.Copy).then_inc(qkT_done, 1)
                    take_updates(2)
                    squares(2)
                    for lv in range(NL):
                        for g in range(REP):
                            act.wait_ge(w_ps, n(DEC) + 2 * lv + g + 1)
                            act.wait_ge(xy_ps, n(DEC) + max(2 * lv + g - 1, 0))
                            nc.scalar.activation(wneg[:, g * NC_:(g + 1) * NC_, :],
                                                 ps[g][:, :].rearrange("p (c t) -> p c t", c=NC_), ACT.Copy,
                                                 scale=-1.0).then_inc(w_done, 1)
                        if lv == 0:
                            take_state_part(3)
                            take_updates(3)
                        if lv == 1:
                            squares(3)
                        if lv == NL - 2:
                            take_transposes()

            def n_end(k):
                return STEPS * k + BASE

            take_updates, take_state_part, squares, take_transposes, gate_z = stage_two(1, n_end)
            gate_z()
            for c in range(NC_):
                if c:
                    take_state_part(c)
                take_updates(c)
                squares(c)
            take_transposes()

        @block.vector
        def _(dve):
            def col(r, kind, u):
                return cols[r][:, kind * U + u:kind * U + u + 1]

            def stage_two(r, tb, n):
                def residual(c):
                    dve.wait_ge(ks_ps, n(3) + c)
                    dve.wait_ge(u_ps, n(4) + c)
                    for g in range(REP):
                        u = g * NC_ + c
                        nc.vector.scalar_tensor_tensor(resid[:, g * P:(g + 1) * P], ps[6][:, g * P:(g + 1) * P],
                                                       col(r, NGAM, u), v[r][:, u, :], ALU.mult, ALU.add).then_inc(r_done, 1)

                def output(c):
                    dve.wait_ge(o_ps, n(4) + c + 1)
                    if c == 0:
                        dve.wait_ge(osq_done, n(4))
                    else:
                        dve.wait_ge(fs_done, n(6) + 2 * c)
                    if c < NC_ - 1:
                        dve.wait_ge(st_done, n(5) + max(2 * c - 1, 0))
                        for g in range(REP):
                            u = g * NC_ + c
                            part = slice(g * P, (g + 1) * P)
                            kv = ps[7][:, (REP + g) * P:(REP + g + 1) * P]
                            if c:
                                nc.vector.scalar_tensor_tensor(state[:, part], state[:, part], col(r, GAMC, u), kv,
                                                               ALU.mult, ALU.add).then_inc(st_done, 1)
                        if c == 0:
                            nc.vector.tensor_copy(state[:, :], ps[7][:, REP * P:2 * REP * P]).then_inc(st_done, 1)
                    if c:
                        nc.vector.tensor_tensor(o[:, c, :], ps[7][:, 0:REP * P], from_state[:, :], ALU.add).then_inc(o_done, 1)
                    else:
                        nc.vector.tensor_copy(o[:, c, :], ps[7][:, 0:REP * P]).then_inc(o_done, 1)

                def gating():
                    dve.wait_ge(o_pow, n(3) + 3)
                    dve.wait_ge(o_done, n(4) + 4)
                    dve.wait_ge(z_done, n(2) + 2)
                    dve.wait_ge(gT_ps, n(2))
                    for g in range(REP):
                        for c in range(NC_):
                            u = g * NC_ + c
                            part = slice(g * P, (g + 1) * P)
                            nc.vector.scalar_tensor_tensor(gated[:, c, part], o[:, c, part], o_r[:, u:u + 1], z[:, c, part],
                                                           ALU.mult, ALU.mult).then_inc(gated_done, 1)

                def add_out():
                    for h in range(2):
                        dve.wait_ge(out_ps, n(2) + h + 1)
                        at = slice(tb * NC_ + 2 * h, tb * NC_ + 2 * h + 2)
                        nc.vector.tensor_tensor(acc[:, at, :], ps[6 + h][:, :].rearrange("p (c d) -> p c d", c=2),
                                                acc[:, at, :], ALU.add).then_inc(acc_done, 1)

                return residual, output, gating, add_out

            for s in (tap_done, conv_done, b_done, m_done, kw_done, inv1_done, inv_done,
                      r_done, st_done, o_done, gated_done, acc_done):
                dve.sem_inc(s, BASE)
            nc.vector.memset(lrow[:, :], 1.0)
            nc.vector.memset(rrow[:, :], 1.0).then_inc(init, 1)
            nc.vector.memset(acc[:, :, :], 0.0)
            for t in (qkT[1], v[1], kw[1], scores[1], inv[1]):
                nc.vector.memset(t[:, :, :], 0.0)
            nc.vector.memset(eps8[:, :], L2_EPS)
            nc.vector.memset(half8[:, :], -0.5)
            nc.vector.memset(inv128[:, :], 1.0 / P)
            nc.vector.memset(qk_scale8[:, 0:NC_], float(P) ** -0.5)
            nc.vector.memset(qk_scale8[:, NC_:U], 1.0).then_inc(init, 1)
            nc.vector.memset(cols[1][:, :], 0.0).then_inc(init, 1)
            nc.vector.tensor_copy(identb[:, :], cst[:, IDENT:IDENT + P]).then_inc(init, 1)
            nc.vector.tensor_copy(hide[:, :, :], cst[:, HIDE:HIDE + P].unsqueeze(1).to_broadcast([P, NC_, C])).then_inc(init, 1)
            dve.wait_ge(init, 5)

            with dve.Fori(0, NK) as i:
                for b in range(BATCH):
                    p = b % 2

                    def n(k, i=i, b=b):
                        return i * (k * BATCH) + k * b + BASE

                    residual, output, gating, add_out = stage_two(1 - p, (b - 1) % BATCH, n)

                    def taps(pair):
                        for t in range(KC - 1):
                            shift = KC - 1 - t
                            for j in pair:
                                k = 4 * KT * P + j * KC + t
                                if t == 0:
                                    dve.wait_ge(conv0_done, n(4) + j + 1)
                                else:
                                    dve.wait_ge(tap_done, n(12) + 3 * pair[0] + 2 * (t - 1) + (j - pair[0]) + 1)
                                last = nc.vector.scalar_tensor_tensor(
                                    conv[:, j, shift:T], ps[(2, 3, 0, 1)[j]][:, 0:T - shift], w_in[:, k:k + 1],
                                    conv[:, j, shift:T], ALU.mult, ALU.add).then_inc(tap_done, 1)
                        for j in pair:
                            dve.wait_ge(tap_done, n(12) + 3 * pair[0] + 5 + (j - pair[0]))
                            nc.vector.nop().then_inc(conv_done, 1)

                    output(0)
                    taps((0, 1))
                    residual(1)
                    taps((2, 3))
                    output(1)
                    residual(2)
                    dve.wait_ge(qk_done, n(8) + 8)
                    dve.wait_ge(cols_in, n(16) - BASE + 16)
                    dve.wait_ge(o_ps, n(4) + 2)
                    for u in range(U):
                        nc.vector.tensor_scalar(kw[p][:, u, :], qk[:, NC_ + u % NC_, :], col(p, WSUF, u), None,
                                                ALU.mult).then_inc(kw_done, 1)
                    dve.wait_ge(kk_ps, n(2) + 1)
                    dve.wait_ge(decay_done, n(2) + 2)
                    dve.wait_ge(bs_done, n(DEC))
                    for u in range(U):
                        c = u % NC_
                        nc.vector.scalar_tensor_tensor(bmat[:, u, :], ps[4][:, c * C:(c + 1) * C], col(p, BETA, u),
                                                       decay[:, u, :], ALU.mult, ALU.mult).then_inc(b_done, 1)
                    dve.wait_ge(kk_ps, n(2) + 2)
                    for g in range(REP):
                        us = slice(g * NC_, (g + 1) * NC_)
                        nc.vector.tensor_tensor(scores[p][:, us, :], ps[5][:, :].rearrange("p (c t) -> p c t", c=NC_),
                                                decay[:, us, :], ALU.mult).then_inc(m_done, 1)
                    output(2)
                    ident4 = cst[:, IDENT:IDENT + P].unsqueeze(1).to_broadcast([P, NC_, P])
                    dve.wait_ge(w_ps, n(DEC))
                    dve.wait_ge(xy_ps, n(DEC))
                    for g in range(REP):
                        dve.wait_ge(b1_ps, n(2) + g + 1)
                        us = slice(g * NC_, (g + 1) * NC_)
                        nc.vector.tensor_tensor(invT[:, us, :], ps[2 + g][:, :].rearrange("p (c t) -> p c t", c=NC_),
                                                ident4, ALU.add).then_inc(inv1_done, 1)
                    for lv in range(NL):
                        if lv == 0:
                            residual(3)
                        if lv == 1:
                            output(3)
                        for g in range(REP):
                            us = slice(g * NC_, (g + 1) * NC_)
                            dve.wait_ge(xy_ps, n(DEC) + 2 * lv + g + 1)
                            if lv == 0:
                                dve.wait_ge(x1_done, n(2) + g + 1)
                            else:
                                dve.wait_ge(inv_done, n(INV) + 4 * (lv - 1) + 2 * g + 2)
                            nc.vector.tensor_tensor(inv[p][:, us, :], ps[2 + 2 * g][:, :].rearrange("p (c t) -> p c t", c=NC_),
                                                    inv[p][:, us, :], ALU.add).then_inc(inv_done, 1)
                            if lv < NL - 1:
                                nc.vector.tensor_tensor(invT[:, us, :], ps[3 + 2 * g][:, :].rearrange("p (c t) -> p c t", c=NC_),
                                                        invT[:, us, :], ALU.add).then_inc(inv_done, 1)
                        if lv == NL - 3:
                            gating()
                    add_out()

            def n_end(k):
                return STEPS * k + BASE

            residual, output, gating, add_out = stage_two(1, BATCH - 1, n_end)
            for c in range(NC_):
                if c:
                    residual(c)
                output(c)
            gating()
            add_out()
            for b in range(BATCH):
                at = slice(b * NC_, (b + 1) * NC_)
                if b == 0:
                    dve.wait_ge(acc_done, n_end(2) + 2)
                nc.vector.tensor_tensor(acc[:, at, :], acc[:, at, :], gate[:, at, :], ALU.mult).then_inc(acc_done, 1)
                dve.wait_ge(acc_done, n_end(2) + 3 + b)
                if b == 0:
                    dve.wait_ge(x_in, 16 * BATCH)
                nc.vector.tensor_tensor(acc[:, at, :].rearrange("p c d -> p (c d)"), acc[:, at, :].rearrange("p c d -> p (c d)"),
                                        x_back[b], ALU.add).then_inc(final, 1)

        @block.gpsimd
        def _(pool):
            def output_norms(n):
                pool.wait_ge(osq_done, n(4) + 4)
                pool.wait_ge(gated_done, n(8))
                nc.gpsimd.tensor_tensor(o_t[:, :], o_sq[:, :], inv128[:, :], ALU.mult).then_inc(o_pow, 1)
                pool.wait_ge(o_pow, n(3) + 1)
                nc.gpsimd.tensor_tensor(o_t[:, :], o_t[:, :], eps8[:, :], ALU.add).then_inc(o_pow, 1)
                pool.wait_ge(o_pow, n(3) + 2)
                nc.gpsimd.tensor_tensor(o_r[:, :], o_t[:, :], half8[:, :], ALU.pow).then_inc(o_pow, 1)

            for s in (qk_pow, b1_done, x1_done, bs_done, o_pow):
                pool.sem_inc(s, BASE)
            pool.wait_ge(init, 5)
            with pool.Fori(0, NK) as i:
                for b in range(BATCH):
                    p = b % 2

                    def n(k, i=i, b=b):
                        return i * (k * BATCH) + k * b + BASE

                    pool.wait_ge(sq_done, n(8) + 8)
                    pool.wait_ge(qk_done, n(8))
                    nc.gpsimd.tensor_tensor(qk_t[:, :], qk_sq[:, :], eps8[:, :], ALU.add).then_inc(qk_pow, 1)
                    pool.wait_ge(qk_pow, n(3) + 1)
                    nc.gpsimd.tensor_tensor(qk_p[:, :], qk_t[:, :], half8[:, :], ALU.pow).then_inc(qk_pow, 1)
                    pool.wait_ge(qk_pow, n(3) + 2)
                    nc.gpsimd.tensor_tensor(qk_r[:, :], qk_p[:, :], qk_scale8[:, :], ALU.mult).then_inc(qk_pow, 1)

                    def masked(dst, g, at):
                        mask = cst[:, at:at + P].unsqueeze(1).to_broadcast([P, NC_, P])
                        return nc.gpsimd.tensor_tensor(dst, bmat[:, g * NC_:(g + 1) * NC_, :], mask, ALU.mult)

                    pool.wait_ge(b1_ps, n(2))
                    for g in range(REP):
                        us = slice(g * NC_, (g + 1) * NC_)
                        pool.wait_ge(b_done, n(8) + NC_ * (g + 1))
                        masked(bm1[:, us, :], g, MERGE1).then_inc(b1_done, 1)
                    ident4 = cst[:, IDENT:IDENT + P].unsqueeze(1).to_broadcast([P, NC_, P])
                    pool.wait_ge(u_ps, n(4))
                    for lv in range(NL):
                        for g in range(REP):
                            us = slice(g * NC_, (g + 1) * NC_)
                            pool.wait_ge(w_ps, n(DEC) + max(2 * (lv - 2) + g + 1, 0))
                            masked(bs[g][lv % 2][:, :, :], g, MERGE2 + lv * P).then_inc(bs_done, 1)
                            if lv == 0:
                                pool.wait_ge(b1_done, n(2) + g + 1)
                                nc.gpsimd.tensor_tensor(inv[p][:, us, :], bm1[:, us, :], ident4, ALU.add).then_inc(x1_done, 1)
                        if lv == 2:
                            output_norms(n)

            def n_end(k):
                return STEPS * k + BASE

            output_norms(n_end)


_INS = ["x", "small_w", "decay_rows", "consts", "ffn_gate", "ffn_up", "ffn_down", "w_in", "w_z", "w_out", "norm_w"]


def program(nc, a, out):
    with ExitStack() as ctx:
        def sb(name, shape):
            return ctx.enter_context(nc.sbuf_tensor(name, shape, F32))

        keep = {
            "cst": sb("cst", [P, NCONST]),
            "xnT": sb("xnT", [P, KT, BATCH * T]),
            "gate": sb("gate", [P, TILES, D]),
            "prep": sb("prep", [P, STEPS, KINDS * U]),
            "cst_dram": a["consts"],
        }
        g_rows = nc.dram_tensor("g_rows", [4, UNITS * C], F32).ap()
        comb_rows = nc.dram_tensor("comb_rows", [TILES * (E + 1), P], F32).ap()
        prepare_block(nc, a["x"], a["small_w"], a["decay_rows"], keep, g_rows, comb_rows)
        ffn_block(nc, a["ffn_gate"], a["ffn_up"], a["ffn_down"], keep, comb_rows)
        recurrent_block(nc, a["x"], a["w_in"], a["w_z"], a["w_out"], a["norm_w"], keep, g_rows, out)


def kernel(**inputs):
    import concourse.bacc as bacc
    from concourse.bass_utils import run_bass_kernel_spmd

    x = {k: np.asarray(v_) for k, v_ in inputs.items()}

    def rows(w):
        return w.reshape(KT, P, -1).transpose(1, 0, 2)

    def padded(w):
        return np.concatenate([w, np.zeros((FT * P - F,) + w.shape[1:], w.dtype)])

    def by_unit(row):
        return np.broadcast_to(row.reshape(NK, 1, REP, 1), (NK, BATCH, REP, NC_)).reshape(UNITS)

    keys = NK * P
    wqkv, conv_w = x["L0_attn_W_qkv"], x["L0_attn_conv_w"]
    heads = [wqkv[:, :keys].reshape(D, NK, 1, P), wqkv[:, keys:2 * keys].reshape(D, NK, 1, P),
             wqkv[:, 2 * keys:].reshape(D, NK, REP, P)]
    w_in = np.concatenate(heads, 2).reshape(KT, P, NK, 4 * P).transpose(2, 1, 0, 3).reshape(NK, P, KT * 4 * P)
    taps = np.concatenate([conv_w[:keys].reshape(NK, 1, P, KC), conv_w[keys:2 * keys].reshape(NK, 1, P, KC),
                           conv_w[2 * keys:].reshape(NK, REP, P, KC)], 1).transpose(0, 2, 1, 3).reshape(NK, P, 4 * KC)
    gu_e, gu_s = x["L0_ffn_We_gate_up"], x["L0_ffn_Ws_gate_up"]

    def up_or_gate(k):
        return padded(np.concatenate([gu_e[:, :, k * I_MOE:(k + 1) * I_MOE].transpose(0, 2, 1).reshape(E * I_MOE, D),
                                      gu_s[:, k * I_SH:(k + 1) * I_SH].T])).T

    down = padded(np.concatenate([x["L0_ffn_We_down"].reshape(E * I_MOE, D), x["L0_ffn_Ws_down"]]))
    data = {
        "x": x["L0_attn_hidden_states"],
        "small_w": rows(np.concatenate([x["L0_attn_W_b"], x["L0_attn_W_a"], x["L0_ffn_W_router"].T, x["L0_ffn_W_sgate"].T], 1)),
        "decay_rows": np.stack([by_unit(x["L0_attn_dt_bias"]), by_unit(x["L0_attn_A_log"])]),
        "consts": constants(),
        "ffn_gate": rows(up_or_gate(0)),
        "ffn_up": rows(up_or_gate(1)),
        "ffn_down": down.reshape(FT, P, D).transpose(1, 0, 2),
        "w_in": np.concatenate([w_in, taps], 2),
        "w_z": x["L0_attn_W_z"].reshape(KT, P, NK, REP * P).transpose(2, 1, 0, 3),
        "w_out": x["L0_attn_W_out"].reshape(NK, REP, P, D).transpose(0, 2, 1, 3),
        "norm_w": x["L0_attn_norm_w"].reshape(P, 1),
    }
    nc = bacc.Bacc("TRN2", target_bir_lowering=False, num_devices=1)
    arrays, aps = {}, {}
    for name in _INS:
        arr = np.ascontiguousarray(data[name])
        arrays[f"in_{name}"] = arr
        aps[name] = nc.dram_tensor(f"in_{name}", arr.shape, mybir.dt.from_np(arr.dtype), kind="ExternalInput").ap()
    out = nc.dram_tensor("out", [BATCH, T, D], F32, kind="ExternalOutput").ap()
    program(nc, aps, out)
    r = run_bass_kernel_spmd(nc, [arrays], core_ids=[0])
    return r.results[0]["out"]
```

```python
from contextlib import ExitStack

import numpy as np
import concourse.bass as bass
from concourse import mybir

F32 = mybir.dt.float32
BF16 = mybir.dt.bfloat16
ALU = mybir.AluOpType
ACT = mybir.ActivationFunctionType
AX = mybir.AxisListType

P = 128
BASE = 1
BATCH, T, D = 4, 512, 256
KT = D // P
NV, NK, KC = 32, 16, 4
REP = NV // NK
C = 128
NC_ = T // C
TILES = BATCH * NC_
U = REP * NC_
STEPS = NK * BATCH
UNITS = STEPS * U
E, I_MOE, I_SH = 8, 176, 704
F = E * I_MOE + I_SH
FT = -(-F // P)
NSMALL = 2 * NV + E + 1
LN_EPS, L2_EPS, RMS_EPS = 1e-5, 1e-6, 1e-6
LOG_DECAY_MIN = -110.0
ROUND = 1.5 * 2.0 ** 23
MASKED = -30000.0
LEVELS = (2, 4, 8, 16, 32, 64)
NL = len(LEVELS)
BETA, GAM, NGAM, WSUF, GAMC = range(5)
KINDS = 5


def constants():
    r, c = np.arange(P)[:, None], np.arange(P)[None, :]

    def merge(s):
        return ((r // s) % 2 == 0) & (c // s == r // s + 1)

    parts = [r == c, r <= c, r > c, np.ones((P, P), bool), (c < r) * MASKED, merge(1) * -1.0]
    parts += [merge(s) for s in LEVELS]
    parts += [np.broadcast_to(np.arange(E) - E, (P, E))]
    return np.ascontiguousarray(np.concatenate([np.asarray(x, np.float32) for x in parts], 1))


IDENT, UPTO, AFTER, ONES, HIDE, MERGE1, MERGE2 = (P * k for k in range(7))
IOTA = MERGE2 + NL * P
NCONST = IOTA + E


def prepare_block(nc, x, small_w, decay_rows, keep, g_rows, comb_rows):
    cst, xnT, prep = keep["cst"], keep["xnT"], keep["prep"]
    with ExitStack() as ctx:
        def sb(name, shape, dt=F32):
            return ctx.enter_context(nc.sbuf_tensor(name, shape, dt))

        def sem(name):
            return ctx.enter_context(nc.semaphore(name))

        xs = sb("xs", [P, TILES, D])
        ws = sb("ws", [P, KT, NSMALL])
        stats = sb("stats", [P, TILES, 6])
        mean = sb("mean", [P, TILES])
        diff = sb("diff", [P, TILES])
        var = sb("var", [P, TILES])
        rstd = sb("rstd", [P, TILES])
        expo = sb("expo", [P, TILES])
        xn = sb("xn", [P, 2, D])
        xt = sb("xt", [P, 2, D])
        a_b = sb("a_b", [P, UNITS])
        a_a = sb("a_a", [P, UNITS])
        routed = sb("routed", [P, TILES, E + 1])
        dtb = sb("dtb", [P, UNITS])
        a_exp = sb("a_exp", [P, UNITS])
        absu = sb("absu", [P, UNITS])
        em = sb("em", [P, UNITS])
        den = sb("den", [P, UNITS])
        sq = sb("sq", [P, UNITS])
        ser = sb("ser", [P, UNITS])
        g = sb("g", [P, UNITS])
        g_hi = sb("g_hi", [P, UNITS])
        g_lo = sb("g_lo", [P, UNITS])
        sum_hi = sb("sum_hi", [P, UNITS])
        sum_lo = sb("sum_lo", [P, UNITS])
        sum_g = sb("sum_g", [P, UNITS])
        rows = sb("rows", [P, 4, UNITS])
        top = sb("top", [P, TILES])
        pr = sb("pr", [P, TILES, E])
        hit = sb("hit", [P, TILES, E])
        hot1 = sb("hot1", [P, TILES, E])
        hot2 = sb("hot2", [P, TILES, E])
        comb = sb("comb", [P, TILES, E + 1])
        combT = sb("combT", [P, 2, P])
        ps_t = [ctx.enter_context(nc.psum_tensor(f"ps_t{k}", [P, 512], F32)) for k in range(2)]
        ps_s = [ctx.enter_context(nc.psum_tensor(f"ps_s{k}", [P, 512], F32)) for k in range(2)]
        ps_g = [ctx.enter_context(nc.psum_tensor(f"ps_g{k}", [P, 512], F32)) for k in range(4)]

        loaded, w_loaded = sem("x_loaded"), sem("w_loaded")
        vec, act_s, pow_done = sem("vec_chain"), sem("act_chain"), sem("pow_done")
        var_ready, stored = sem("var_ready"), sem("rows_stored")
        xn_ready, xnt_ps, xt_ready, xt_kept = sem("xn_ready"), sem("xnT_ps"), sem("xt_ready"), sem("xnT_kept")
        small_ps, small_out = sem("small_ps"), sem("small_out")
        u_ready, e_ready, g_ready, sums_ps, sums_out = sem("u_ready"), sem("e_ready"), sem("g_ready"), sem("sums_ps"), sem("sums_out")
        sumg_ready, rows_ps, rows_out, gam_ready = sem("sumg_ready"), sem("rows_ps"), sem("rows_out"), sem("gam_ready")
        logit_ready, prob_exp, sg_ready = sem("logit_ready"), sem("prob_exp"), sem("sg_ready")
        comb_ready, comb_ps, comb_out = sem("comb_ready"), sem("comb_ps"), sem("comb_out")
        block = ctx.enter_context(nc.Block())

        @block.sync
        def _(sp):
            for b in range(BATCH):
                sp.dma_start(xs[:, b * NC_:(b + 1) * NC_, :],
                             x[b].rearrange("(c p) d -> p c d", p=P)).then_inc(loaded, 16)
            sp.dma_start(cst[:, :], keep["cst_dram"]).then_inc(w_loaded, 16)
            sp.dma_start(ws[:, :, :], small_w).then_inc(w_loaded, 16)
            sp.dma_start(dtb[:, :], decay_rows[0:1, :].partition_broadcast(P)).then_inc(w_loaded, 16)
            sp.dma_start(a_exp[:, :], decay_rows[1:2, :].partition_broadcast(P)).then_inc(w_loaded, 16)
            sp.wait_ge(comb_out, 2)
            sp.dma_start(comb_rows[0:P, :], combT[:, 0, :]).then_inc(stored, 16)
            sp.dma_start(comb_rows[P:TILES * (E + 1), :], combT[0:TILES * (E + 1) - P, 1, :]).then_inc(stored, 16)
            sp.wait_ge(rows_out, 4)
            for k in range(4):
                sp.dma_start(g_rows[k].rearrange("(q u t) -> u q t", q=4, u=P),
                             rows[:, k, :].rearrange("u (q t) -> u q t", q=4)).then_inc(stored, 16)
            sp.wait_ge(stored, 6 * 16)

        @block.vector
        def _(dve):
            chain = [0]

            def link(ins):
                chain[0] += 1
                ins.then_inc(vec, 1)
                dve.wait_ge(vec, chain[0])

            dve.wait_ge(loaded, BATCH * 16)
            with dve.Fori(0, TILES) as t:
                nc.vector.bn_stats(stats[:, bass.ds(t, 1), :], xs[:, bass.ds(t, 1), :]).then_inc(small_out, 1)
            dve.wait_ge(small_out, TILES)
            link(nc.vector.tensor_tensor(mean[:, :], stats[:, :, 1], stats[:, :, 4], ALU.add))
            link(nc.vector.tensor_tensor(diff[:, :], stats[:, :, 1], stats[:, :, 4], ALU.subtract))
            link(nc.vector.tensor_tensor(var[:, :], stats[:, :, 2], stats[:, :, 5], ALU.add))
            link(nc.vector.tensor_scalar(mean[:, :], mean[:, :], 0.5, None, ALU.mult))
            link(nc.vector.tensor_tensor(diff[:, :], diff[:, :], diff[:, :], ALU.mult))
            link(nc.vector.tensor_scalar(diff[:, :], diff[:, :], 0.25, LN_EPS, ALU.mult, ALU.add))
            link(nc.vector.memset(expo[:, :], -0.5))
            nc.vector.scalar_tensor_tensor(var[:, :], var[:, :], 1.0 / D, diff[:, :],
                                           ALU.mult, ALU.add).then_inc(var_ready, 1)
            dve.wait_ge(pow_done, 1)
            a_bv = a_b[:, :].rearrange("p (h b v c) -> p h b v c", h=NK, b=BATCH, v=REP)
            a_av = a_a[:, :].rearrange("p (h b v c) -> p h b v c", h=NK, b=BATCH, v=REP)
            with dve.Fori(0, BATCH) as b:
                for c in range(NC_):
                    k = c % 2
                    dve.wait_ge(xnt_ps, b * NC_ + max(c - 1, 0) + BASE)
                    nc.vector.tensor_scalar(xn[:, k, :], xs[:, bass.ds(b * NC_ + c, 1), :],
                                            mean[:, bass.ds(b * NC_ + c, 1)], rstd[:, bass.ds(b * NC_ + c, 1)],
                                            ALU.subtract, ALU.mult).then_inc(xn_ready, 1)
                    dve.wait_ge(small_ps, b * NC_ + c + 1 + BASE)
                    nc.vector.tensor_copy(a_bv[:, :, bass.ds(b, 1), :, c],
                                          ps_s[k][:, 0:NV].rearrange("p (h o v) -> p h o v", v=REP, o=1)).then_inc(small_out, 1)
                    nc.vector.tensor_copy(a_av[:, :, bass.ds(b, 1), :, c],
                                          ps_s[k][:, NV:2 * NV].rearrange("p (h o v) -> p h o v", v=REP, o=1)).then_inc(small_out, 1)
                    nc.vector.tensor_copy(routed[:, bass.ds(b * NC_ + c, 1), :],
                                          ps_s[k][:, 2 * NV:NSMALL]).then_inc(small_out, 1)
            dve.wait_ge(small_out, 4 * TILES)
            dve.wait_ge(w_loaded, 64)
            nc.vector.tensor_tensor(a_a[:, :], a_a[:, :], dtb[:, :], ALU.add).then_inc(u_ready, 1)
            link(nc.vector.tensor_reduce(top[:, :], routed[:, :, 0:E], AX.X, ALU.max))
            nc.vector.tensor_tensor(pr[:, :, :], routed[:, :, 0:E],
                                    top[:, :].unsqueeze(2).to_broadcast([P, TILES, E]), ALU.subtract).then_inc(logit_ready, 1)
            dve.wait_ge(e_ready, 1)
            link(nc.vector.tensor_scalar(den[:, :], em[:, :], 2.0, None, ALU.add))
            link(nc.vector.reciprocal(den[:, :], den[:, :]))
            link(nc.vector.tensor_tensor(em[:, :], em[:, :], den[:, :], ALU.mult))
            link(nc.vector.tensor_tensor(sq[:, :], em[:, :], em[:, :], ALU.mult))
            link(nc.vector.tensor_scalar(ser[:, :], sq[:, :], 1.0 / 17, None, ALU.mult))
            for odd in (15, 13, 11, 9, 7, 5, 3):
                link(nc.vector.scalar_tensor_tensor(ser[:, :], ser[:, :], 1.0 / odd, sq[:, :], ALU.add, ALU.mult))
            link(nc.vector.scalar_tensor_tensor(ser[:, :], ser[:, :], 1.0, em[:, :], ALU.add, ALU.mult))
            link(nc.vector.tensor_scalar(ser[:, :], ser[:, :], 2.0, None, ALU.mult))
            link(nc.vector.scalar_tensor_tensor(ser[:, :], a_a[:, :], 0.0, ser[:, :], ALU.max, ALU.add))
            dve.wait_ge(e_ready, 2)
            link(nc.vector.scalar_tensor_tensor(g[:, :], ser[:, :], -1.0, a_exp[:, :], ALU.mult, ALU.mult))
            link(nc.vector.tensor_scalar(g[:, :], g[:, :], LOG_DECAY_MIN, None, ALU.max))
            link(nc.vector.tensor_scalar(g_hi[:, :], g[:, :], ROUND, -ROUND, ALU.add, ALU.add))
            nc.vector.tensor_tensor(g_lo[:, :], g[:, :], g_hi[:, :], ALU.subtract).then_inc(g_ready, 1)
            dve.wait_ge(prob_exp, 1)
            link(nc.vector.tensor_reduce(top[:, :], pr[:, :, :], AX.X, ALU.add))
            link(nc.vector.reciprocal(top[:, :], top[:, :]))
            link(nc.vector.tensor_tensor(pr[:, :, :], pr[:, :, :], top[:, :].unsqueeze(2).to_broadcast([P, TILES, E]), ALU.mult))
            iota = cst[:, IOTA:IOTA + E].unsqueeze(1).to_broadcast([P, TILES, E])

            def pick(hot, src):
                link(nc.vector.tensor_reduce(top[:, :], src[:, :, :], AX.X, ALU.max))
                topb = top[:, :].unsqueeze(2).to_broadcast([P, TILES, E])
                link(nc.vector.tensor_tensor(hit[:, :, :], src[:, :, :], topb, ALU.is_equal))
                link(nc.vector.tensor_tensor(hit[:, :, :], hit[:, :, :], iota, ALU.mult))
                link(nc.vector.tensor_reduce(top[:, :], hit[:, :, :], AX.X, ALU.min))
                link(nc.vector.tensor_tensor(hot[:, :, :], iota, topb, ALU.is_equal))

            pick(hot1, pr)
            link(nc.vector.scalar_tensor_tensor(hot2[:, :, :], hot1[:, :, :], -2.0, pr[:, :, :], ALU.mult, ALU.add))
            link(nc.vector.tensor_copy(comb[:, :, 0:E], hot2[:, :, :]))
            pick(hot2, comb[:, :, 0:E])
            link(nc.vector.tensor_tensor(hot1[:, :, :], hot1[:, :, :], hot2[:, :, :], ALU.add))
            nc.vector.tensor_tensor(comb[:, :, 0:E], hot1[:, :, :], pr[:, :, :], ALU.mult).then_inc(comb_ready, 1)
            dve.wait_ge(sums_out, 2)
            nc.vector.tensor_tensor(sum_g[:, :], sum_hi[:, :], sum_lo[:, :], ALU.add).then_inc(sumg_ready, 1)
            dve.wait_ge(gam_ready, 1)
            link(nc.vector.tensor_scalar(prep[:, :, NGAM * U:(NGAM + 1) * U], prep[:, :, GAM * U:(GAM + 1) * U],
                                         -1.0, None, ALU.mult))

        @block.gpsimd
        def _(pool):
            pool.wait_ge(var_ready, 1)
            nc.gpsimd.tensor_tensor(rstd[:, :], var[:, :], expo[:, :], ALU.pow).then_inc(pow_done, 1)

        @block.scalar
        def _(act):
            act.sem_inc(xt_kept, BASE)
            with act.Fori(0, BATCH) as b:
                for c in range(NC_):
                    k = c % 2
                    act.wait_ge(xnt_ps, b * NC_ + c + 1 + BASE)
                    act.wait_ge(small_ps, b * NC_ + max(c - 1, 0) + BASE)
                    nc.scalar.activation(xt[:, k, :], ps_t[k][:, 0:D], ACT.Copy).then_inc(xt_ready, 1)
                    nc.scalar.activation(xnT[:, :, bass.ds((b * NC_ + c) * P, P)],
                                         ps_t[k][:, 0:D].rearrange("p (k t) -> p k t", k=KT), ACT.Copy).then_inc(xt_kept, 1)
            act.wait_ge(small_out, 4 * TILES)
            act.wait_ge(w_loaded, 64)

            def units(ap):
                return ap.rearrange("p (s u) -> p s u", u=U)

            nc.scalar.activation(prep[:, :, BETA * U:(BETA + 1) * U], units(a_b[:, :]), ACT.Sigmoid).then_inc(act_s, 1)
            nc.scalar.activation(comb[:, :, E:E + 1], routed[:, :, E:E + 1], ACT.Sigmoid).then_inc(sg_ready, 1)
            act.wait_ge(u_ready, 1)
            nc.scalar.activation(absu[:, :], a_a[:, :], ACT.Abs).then_inc(act_s, 1)
            act.wait_ge(act_s, 2)
            nc.scalar.activation(em[:, :], absu[:, :], ACT.Exp, scale=-1.0).then_inc(e_ready, 1)
            nc.scalar.activation(a_exp[:, :], a_exp[:, :], ACT.Exp).then_inc(e_ready, 1)
            act.wait_ge(logit_ready, 1)
            nc.scalar.activation(pr[:, :, :], pr[:, :, :], ACT.Exp).then_inc(prob_exp, 1)
            act.wait_ge(sums_ps, 4)
            nc.scalar.activation(sum_hi[:, :], ps_g[0][:, :], ACT.Copy).then_inc(sums_out, 1)
            nc.scalar.activation(sum_lo[:, :], ps_g[1][:, :], ACT.Copy).then_inc(sums_out, 1)
            nc.scalar.activation(prep[:, :, WSUF * U:(WSUF + 1) * U], units(ps_g[2][:, :]), ACT.Exp).then_inc(act_s, 1)
            nc.scalar.activation(prep[:, :, GAMC * U:(GAMC + 1) * U], units(ps_g[3][:, :]), ACT.Exp).then_inc(act_s, 1)
            act.wait_ge(sumg_ready, 1)
            nc.scalar.activation(prep[:, :, GAM * U:(GAM + 1) * U], units(sum_g[:, :]), ACT.Exp).then_inc(gam_ready, 1)
            act.wait_ge(rows_ps, 2)
            for k in range(4):
                nc.scalar.activation(rows[:, k, :], ps_t[k % 2][:, :], ACT.Copy,
                                     scale=1.0 if k < 2 else -1.0).then_inc(rows_out, 1)
            act.wait_ge(comb_ps, 1)
            nc.scalar.activation(combT[:, 0, :], ps_s[0][:, 0:P], ACT.Copy).then_inc(comb_out, 1)
            rest = TILES * (E + 1) - P
            nc.scalar.activation(combT[0:rest, 1, :], ps_s[1][0:rest, 0:P], ACT.Copy).then_inc(comb_out, 1)

        @block.tensor
        def _(pe):
            ident = cst[:, IDENT:IDENT + P]
            pe.sem_inc(xnt_ps, BASE)
            pe.sem_inc(small_ps, BASE)
            pe.wait_ge(w_loaded, 64)
            with pe.Fori(0, BATCH) as b:
                for c in range(NC_):
                    k = c % 2
                    pe.wait_ge(xn_ready, b * NC_ + c + 1)
                    pe.wait_ge(xt_kept, b * NC_ + max(c - 1, 0) + BASE)
                    for m in range(KT):
                        last = nc.tensor.transpose(ps_t[k][:, m * P:(m + 1) * P], xn[:, k, m * P:(m + 1) * P], ident)
                    last.then_inc(xnt_ps, 1)
                    pe.wait_ge(xt_ready, b * NC_ + c + 1)
                    pe.wait_ge(small_out, TILES + 3 * (b * NC_ + max(c - 1, 0)))
                    for m in range(KT):
                        last = nc.tensor.matmul(ps_s[k][:, 0:NSMALL], xt[:, k, m * P:(m + 1) * P], ws[:, m, :],
                                                start=(m == 0), stop=(m == KT - 1))
                    last.then_inc(small_ps, 1)
            pe.wait_ge(g_ready, 1)
            for k, (at, src) in enumerate(((UPTO, g_hi), (UPTO, g_lo), (AFTER, g), (ONES, g))):
                nc.tensor.matmul(ps_g[k][:, :], cst[:, at:at + P], src[:, :], start=True, stop=True).then_inc(sums_ps, 1)
            pe.wait_ge(sums_out, 2)
            for k, src in enumerate((sum_hi, sum_lo)):
                for q in range(UNITS // P):
                    last = nc.tensor.transpose(ps_t[k][:, q * P:(q + 1) * P], src[:, q * P:(q + 1) * P], ident)
                last.then_inc(rows_ps, 1)
            pe.wait_ge(comb_ready, 1)
            pe.wait_ge(sg_ready, 1)
            flat = comb[:, :, :].rearrange("p t e -> p (t e)")
            rest = TILES * (E + 1) - P
            nc.tensor.transpose(ps_s[0][:, 0:P], flat[:, 0:P], ident)
            nc.tensor.transpose(ps_s[1][0:rest, 0:P], flat[:, P:P + rest], ident).then_inc(comb_ps, 1)


def ffn_block(nc, wg_dram, wu_dram, wd_dram, keep, comb_rows):
    xnT, gate = keep["xnT"], keep["gate"]
    spans = []
    for j in range(FT):
        at = j * P
        while at < (j + 1) * P:
            e = min(at // I_MOE, E)
            end = (j + 1) * P if e == E else min((e + 1) * I_MOE, (j + 1) * P)
            spans.append((j, at - j * P, end - j * P, e))
            at = end
    GROUPS = ((0, 1), (1, 4), (4, 9), (9, FT))
    comb_v = comb_rows.rearrange("(t e) c -> t e c", e=E + 1)
    with ExitStack() as ctx:
        def sb(name, shape, dt=F32):
            return ctx.enter_context(nc.sbuf_tensor(name, shape, dt))

        def sem(name):
            return ctx.enter_context(nc.semaphore(name))

        wg = sb("wg", [P, KT, FT * P])
        wu = sb("wu", [P, KT, FT * P])
        wd = sb("wd", [P, FT, D])
        hid = sb("hid", [P, FT, T])
        scale = sb("scale", [P, FT, T])
        silu_g = sb("silu_g", [P, 2, T])
        ps_g = [ctx.enter_context(nc.psum_tensor(f"fps_g{k}", [P, 512], F32)) for k in range(2)]
        ps_u = [ctx.enter_context(nc.psum_tensor(f"fps_u{k}", [P, 512], F32)) for k in range(2)]
        ps_o = [ctx.enter_context(nc.psum_tensor(f"fps_o{k}", [P, 512], F32)) for k in range(2)]
        w_in, wd_in, scale_in = [sem(f"ffn_w_in{k}") for k in range(len(GROUPS))], sem("wd_in"), sem("scale_in")
        g_ps, u_ps, silu_done, prod_done, hid_done = sem("g_ps"), sem("u_ps"), sem("silu_done"), sem("prod_done"), sem("hid_done")
        o_ps, gate_done = sem("o_ps"), sem("gate_done")
        block = ctx.enter_context(nc.Block())

        @block.sync
        def _(sp):
            for k, (j0, j1) in enumerate(GROUPS):
                cols = slice(j0 * P, j1 * P)
                sp.dma_start(wg[:, :, cols], wg_dram[:, :, cols]).then_inc(w_in[k], 16)
                sp.dma_start(wu[:, :, cols], wu_dram[:, :, cols]).then_inc(w_in[k], 16)
            sp.dma_start(wd[:, :, :], wd_dram).then_inc(wd_in, 16)

        @block.gpsimd
        def _(pool):
            with pool.Fori(0, BATCH) as b:
                pool.wait_ge(hid_done, b * FT + BASE)
                for j, p0, p1, e in spans:
                    src = comb_v[bass.ds(b * NC_, NC_), e, :].unsqueeze(0).to_broadcast([p1 - p0, NC_, P])
                    nc.gpsimd.dma_start(scale[p0:p1, j, :].rearrange("p (c t) -> p c t", c=NC_), src).then_inc(scale_in, 16)

        @block.scalar
        def _(act):
            act.sem_inc(silu_done, BASE)
            act.sem_inc(gate_done, BASE)
            with act.Fori(0, BATCH) as b:
                for j in range(FT):
                    act.wait_ge(g_ps, b * FT + j + 1)
                    act.wait_ge(hid_done, b * FT + max(j - 1, 0) + BASE)
                    nc.scalar.activation(silu_g[:, j % 2, :], ps_g[j % 2][:, :], ACT.Silu).then_inc(silu_done, 1)
                for c in range(NC_):
                    act.wait_ge(o_ps, b * NC_ + c + 1 + BASE)
                    nc.scalar.activation(gate[:, bass.ds(b * NC_ + c, 1), :], ps_o[c % 2][:, 0:D],
                                         ACT.Silu).then_inc(gate_done, 1)

        @block.vector
        def _(dve):
            dve.sem_inc(prod_done, BASE)
            dve.sem_inc(hid_done, BASE)
            with dve.Fori(0, BATCH) as b:
                dve.wait_ge(scale_in, b * (16 * len(spans)) + 16 * len(spans))
                for j in range(FT):
                    dve.wait_ge(silu_done, b * FT + j + 1 + BASE)
                    dve.wait_ge(u_ps, b * FT + j + 1)
                    if j == 0:
                        dve.wait_ge(o_ps, b * NC_ + BASE)
                    nc.vector.tensor_tensor(silu_g[:, j % 2, :], ps_u[j % 2][:, :], silu_g[:, j % 2, :],
                                            ALU.mult).then_inc(prod_done, 1)
                    dve.wait_ge(prod_done, b * FT + j + 1 + BASE)
                    nc.vector.tensor_tensor(hid[:, j, :], silu_g[:, j % 2, :], scale[:, j, :],
                                            ALU.mult).then_inc(hid_done, 1)

        @block.tensor
        def _(pe):
            pe.sem_inc(o_ps, BASE)
            with pe.Fori(0, BATCH) as b:
                for j in range(FT):
                    for k, (j0, _) in enumerate(GROUPS):
                        if j == j0:
                            pe.wait_ge(w_in[k], 32)
                    pe.wait_ge(silu_done, b * FT + max(j - 1, 0) + BASE)
                    pe.wait_ge(prod_done, b * FT + max(j - 1, 0) + BASE)
                    for w, ps, done in ((wg, ps_g, g_ps), (wu, ps_u, u_ps)):
                        for m in range(KT):
                            last = nc.tensor.matmul(ps[j % 2][:, :], w[:, m, j * P:(j + 1) * P],
                                                    xnT[:, m, bass.ds(b * T, T)], start=(m == 0), stop=(m == KT - 1))
                        last.then_inc(done, 1)
                pe.wait_ge(wd_in, 16)
                for c in range(NC_):
                    pe.wait_ge(gate_done, b * NC_ + max(c - 1, 0) + BASE)
                    if c == 0:
                        pe.wait_ge(hid_done, b * FT + FT + BASE)
                    for j in range(FT):
                        last = nc.tensor.matmul(ps_o[c % 2][:, 0:D], hid[:, j, c * P:(c + 1) * P], wd[:, j, :],
                                                start=(j == 0), stop=(j == FT - 1))
                    last.then_inc(o_ps, 1)


def recurrent_block(nc, x, w_in_dram, w_z_dram, w_out_dram, norm_dram, keep, g_rows, out):
    cst, xnT, prep, gate = keep["cst"], keep["xnT"], keep["prep"], keep["gate"]
    with ExitStack() as ctx:
        def sb(name, shape, dt=F32):
            return ctx.enter_context(nc.sbuf_tensor(name, shape, dt))

        def sem(name):
            return ctx.enter_context(nc.semaphore(name))

        acc = sb("acc", [P, TILES, D])
        w_in = sb("w_in", [P, KT * 4 * P + 4 * KC])
        w_z = sb("w_z", [P, KT, REP * P])
        w_out = sb("w_out", [P, REP, D])
        w_outn = sb("w_outn", [P, REP, D])
        norm_w = sb("norm_w", [P, 1])
        hide = sb("hide", [P, NC_, C], BF16)
        identb = sb("identb", [P, P], BF16)
        lrow = sb("lrow", [4, U * C])
        rrow = sb("rrow", [4, U * C])
        cols = [sb(f"cols{k}", [P, KINDS * U]) for k in range(2)]
        eps8 = sb("eps8", [P, U])
        half8 = sb("half8", [P, U])
        qk_scale8 = sb("qk_scale8", [P, U])
        inv128 = sb("inv128", [P, U])
        decay = sb("decay", [P, U, C])
        decay1 = sb("decay1", [P, U, C])
        conv = sb("conv", [P, 4, T])
        mixed = sb("mixed", [P, 4, T])
        qk_sq = sb("qk_sq", [P, U])
        qk_t = sb("qk_t", [P, U])
        qk_p = sb("qk_p", [P, U])
        qk_r = sb("qk_r", [P, U])
        qk = sb("qk", [P, U, P])
        qkT = [sb(f"qkT{k}", [P, 2, T]) for k in range(2)]
        v = [sb(f"v{k}", [P, U, P]) for k in range(2)]
        kw = [sb(f"kw{k}", [P, U, P]) for k in range(2)]
        scores = [sb(f"scores{k}", [P, U, C]) for k in range(2)]
        bmat = sb("bmat", [P, U, C])
        bm1 = sb("bm1", [P, U, C])
        bs = [[sb(f"bs{g}{k}", [P, NC_, C]) for k in range(2)] for g in range(REP)]
        inv = [sb(f"inv{k}", [P, U, C]) for k in range(2)]
        invT = sb("invT", [P, U, C])
        wneg = sb("wneg", [P, U, C])
        state = sb("state", [P, REP * P])
        resid = sb("resid", [P, REP * P])
        from_state = sb("from_state", [P, REP * P])
        upd = sb("upd", [P, REP * P])
        o = sb("o", [P, NC_, REP * P])
        o_sq = sb("o_sq", [P, U])
        o_t = sb("o_t", [P, U])
        o_r = sb("o_r", [P, U])
        z = sb("z", [P, NC_, REP * P])
        gated = sb("gated", [P, NC_, REP * P])
        gatedT = sb("gatedT", [P, REP, T])
        ps = [ctx.enter_context(nc.psum_tensor(f"rps{k}", [P, 512], F32)) for k in range(8)]
        PROJ_BANK = (4, 5, 6, 7)

        rows_in, cols_in, win_in, wz_in, wout_in, norm_in = (sem(s) for s in ("rows_in", "cols_in", "win_in", "wz_in", "wout_in", "norm_in"))
        init, passed = sem("init"), sem("passed")
        dt_ps, proj_ps, qk_ps, v_ps, qkT_ps, kk_ps, b1_ps, w_ps, x_ps = (
            sem(s) for s in ("dt_ps", "proj_ps", "qk_ps", "v_ps", "qkT_ps", "kk_ps", "b1_ps", "w_ps", "x_ps"))
        z_ps, ks_ps, qs_ps, u_ps, o_ps, gT_ps, out_ps = (
            sem(s) for s in ("z_ps", "ks_ps", "qs_ps", "u_ps", "o_ps", "gT_ps", "out_ps"))
        decay_done, conv0_done, mixed_done, sq_done, qk_done, v_done, qkT_done, w_done = (
            sem(s) for s in ("decay_done", "conv0_done", "mixed_done", "sq_done", "qk_done", "v_done", "qkT_done", "w_done"))
        z_done, fs_done, upd_done, osq_done, gT_done, wout_done = (
            sem(s) for s in ("z_done", "fs_done", "upd_done", "osq_done", "gT_done", "wout_done"))
        tap_done, bm1_done, b_done, m_done, kw_done, inv1_done, inv_done = (
            sem(s) for s in ("tap_done", "bm1_done", "b_done", "m_done", "kw_done", "inv1_done", "inv_done"))
        r_done, st_done, o_done, gated_done, acc_done = (sem(s) for s in ("r_done", "st_done", "o_done", "gated_done", "acc_done"))
        qk_pow, d1_done, x1_done, bs01_done, bs_done, o_pow = (
            sem(s) for s in ("qk_pow", "d1_done", "x1_done", "bs01_done", "bs_done", "o_pow"))
        x_in, stored, final = sem("x_in"), sem("stored"), sem("final")
        WX = 2 * NL
        INV = 4 * NL - 2
        x_back = [t[:, :, :].rearrange("p a n -> p (a n)")[:, 0:NC_ * D] for t in (decay, bm1, conv, mixed)]
        block = ctx.enter_context(nc.Block())

        def counts(i, b):
            return lambda k: i * (k * BATCH) + k * b + BASE

        @block.sync
        def _(sp):
            sp.dma_start(norm_w[:, :], norm_dram).then_inc(norm_in, 16)
            sp.dma_start(w_z[:, :, :], w_z_dram[0]).then_inc(wz_in, 16)
            sp.dma_start(w_out[:, :, :], w_out_dram[0]).then_inc(wout_in, 16)
            sp.wait_ge(init, 1)
            with sp.Fori(0, NK) as i:
                proj_used, taps_used = sp.snap(i * (4 * BATCH) + BASE), sp.snap(i * (12 * BATCH) + BASE)
                sp.wait_ge(proj_ps, proj_used)
                sp.sem_inc(passed, 1)
                sp.wait_ge(tap_done, taps_used)
                sp.sem_inc(passed, 1)
                sp.dma_start(w_in[:, :], w_in_dram[bass.ds(i, 1)].rearrange("o p n -> (o p) n")).then_inc(win_in, 16)
                for b in range(BATCH):
                    step = sp.snap(i * BATCH + b)
                    at = sp.snap(step * (U * C))
                    rows_used = sp.snap(step * 2 + BASE)
                    sp.wait_ge(dt_ps, rows_used)
                    sp.sem_inc(passed, 1)
                    sp.dma_start(lrow[1:4:2, :], g_rows[2:4, bass.ds(at, U * C)]).then_inc(rows_in, 16)
                    sp.dma_start(rrow[0:3:2, :], g_rows[0:2, bass.ds(at, U * C)]).then_inc(rows_in, 16)
                    upd_used, st_used, fs_used = sp.snap(step * 4 + BASE), sp.snap(step * 5 + BASE), sp.snap(step * 6 + BASE)
                    sp.wait_ge(upd_done, upd_used)
                    sp.sem_inc(passed, 1)
                    sp.wait_ge(st_done, st_used)
                    sp.sem_inc(passed, 1)
                    sp.wait_ge(fs_done, fs_used)
                    sp.sem_inc(passed, 1)
                    sp.dma_start(cols[b % 2][:, :], prep[:, bass.ds(step, 1), :]).then_inc(cols_in, 16)
                    if b == 0:
                        z_used, out_used = sp.snap(i * (2 * BATCH) + 2 + BASE), sp.snap(i + 1)
                        sp.wait_ge(z_ps, z_used)
                        sp.sem_inc(passed, 1)
                        sp.dma_start(w_z[:, :, :], w_z_dram[bass.ds(i, 1)].rearrange("o p k n -> (o p) k n")).then_inc(wz_in, 16)
                        sp.wait_ge(wout_done, out_used)
                        sp.sem_inc(passed, 1)
                        sp.dma_start(w_out[:, :, :], w_out_dram[bass.ds(i, 1)].rearrange("o p v n -> (o p) v n")).then_inc(wout_in, 16)
            for k, (used, count) in enumerate(((m_done, 2), (x1_done, 2), (mixed_done, 4), (v_ps, 2))):
                sp.wait_ge(used, STEPS * count + BASE)
                if k == 1:
                    sp.wait_ge(b1_ps, STEPS * 2 + BASE)
                sp.dma_start(x_back[k].rearrange("p (c d) -> p c d", c=NC_),
                             x[k].rearrange("(c p) d -> p c d", p=P)).then_inc(x_in, 16)
            sp.wait_ge(final, BATCH)
            for b in range(BATCH):
                sp.dma_start(out[b].rearrange("(c p) d -> p c d", p=P), acc[:, b * NC_:(b + 1) * NC_, :]).then_inc(stored, 16)
            sp.wait_ge(stored, 16 * BATCH)

        @block.tensor
        def _(pe):
            ident = cst[:, IDENT:IDENT + P]

            def scan_parts(r, n):
                def read_state(c):
                    pe.wait_ge(st_done, n(5) + (2 * c - 1))
                    pe.wait_ge(upd_done, n(4) + c)
                    pe.wait_ge(o_done, n(4) + c)
                    cs = slice(c * C, (c + 1) * C)
                    nc.tensor.matmul(ps[6][:, 0:REP * P], qkT[r][:, 1, cs], state[:, :], start=True, stop=True).then_inc(ks_ps, 1)
                    nc.tensor.matmul(ps[7][:, 0:REP * P], qkT[r][:, 0, cs], state[:, :], start=True, stop=True).then_inc(qs_ps, 1)

                def solve(c):
                    if c:
                        pe.wait_ge(r_done, n(6) + 2 * c)
                    for g in range(REP):
                        rhs = resid[:, g * P:(g + 1) * P] if c else v[r][:, g * NC_, :]
                        last = nc.tensor.matmul(ps[6][:, g * P:(g + 1) * P], inv[r][:, g * NC_ + c, :], rhs,
                                                start=True, stop=True)
                    last.then_inc(u_ps, 1)

                def attend(c):
                    pe.wait_ge(upd_done, n(4) + c + 1)
                    if c:
                        pe.wait_ge(fs_done, n(6) + 2 * c)
                    for g in range(REP):
                        last = nc.tensor.matmul(ps[7][:, g * P:(g + 1) * P], scores[r][:, g * NC_ + c, :],
                                                upd[:, g * P:(g + 1) * P], start=True, stop=True)
                    if c < NC_ - 1:
                        for g in range(REP):
                            last = nc.tensor.matmul(ps[7][:, (REP + g) * P:(REP + g + 1) * P], kw[r][:, g * NC_ + c, :],
                                                    upd[:, g * P:(g + 1) * P], start=True, stop=True)
                    last.then_inc(o_ps, 1)

                return read_state, solve, attend

            def gated_transpose(n):
                pe.wait_ge(gated_done, n(8) + 8)
                pe.wait_ge(upd_done, n(4))
                pe.wait_ge(o_done, n(4))
                for g in range(REP):
                    for c in range(NC_):
                        last = nc.tensor.transpose(ps[6 + g][:, c * C:(c + 1) * C], gated[:, c, g * P:(g + 1) * P], ident)
                    last.then_inc(gT_ps, 1)

            def project_out(n, loads):
                pe.wait_ge(gT_done, n(2) + 2)
                pe.wait_ge(wout_done, loads)
                for h in range(2):
                    for c in (2 * h, 2 * h + 1):
                        for g in range(REP):
                            last = nc.tensor.matmul(ps[6 + h][:, (c % 2) * D:(c % 2 + 1) * D],
                                                    gatedT[:, g, c * C:(c + 1) * C], w_outn[:, g, :],
                                                    start=(g == 0), stop=(g == REP - 1))
                    last.then_inc(out_ps, 1)

            def project_z(n, tb, h):
                for c in (2 * h, 2 * h + 1):
                    for m in range(KT):
                        last = nc.tensor.matmul(ps[4 + h][:, (c % 2) * D:(c % 2 + 1) * D],
                                                xnT[:, m, tb * T + c * C:tb * T + (c + 1) * C], w_z[:, m, :],
                                                start=(m == 0), stop=(m == KT - 1))
                last.then_inc(z_ps, 1)

            def merge_w(n, lv, g):
                if lv < 2:
                    pe.wait_ge(bs01_done, n(4))
                else:
                    pe.wait_ge(bs_done, n(WX - 4) + 2 * (lv - 2) + g + 1)
                if lv == 0:
                    pe.wait_ge(inv1_done, n(2))
                    pe.wait_ge(m_done, n(2))
                else:
                    pe.wait_ge(inv_done, n(INV) + 4 * (lv - 1) + 2 * g + 2)
                for c in range(NC_):
                    last = nc.tensor.matmul(ps[g][:, c * C:(c + 1) * C], bs[g][lv % 2][:, c, :],
                                            invT[:, g * NC_ + c, :], start=True, stop=True)
                last.then_inc(w_ps, 1)

            def merge_x(n, lv, g, r):
                pe.wait_ge(w_done, n(WX) + 2 * lv + g + 1)
                if lv == 0:
                    pe.wait_ge(x1_done, n(2))
                for c in range(NC_):
                    u = g * NC_ + c
                    last = nc.tensor.matmul(ps[2 + g][:, c * C:(c + 1) * C], wneg[:, u, :], inv[r][:, u, :], start=True, stop=True)
                if lv == NL - 2:
                    for c in range(NC_):
                        u = g * NC_ + c
                        last = nc.tensor.matmul(ps[g][:, c * C:(c + 1) * C], inv[r][:, u, :], wneg[:, u, :], start=True, stop=True)
                last.then_inc(x_ps, 1)

            for s in (dt_ps, proj_ps, qk_ps, v_ps, qkT_ps, kk_ps, b1_ps, w_ps, x_ps,
                      z_ps, ks_ps, qs_ps, u_ps, o_ps, gT_ps, out_ps):
                pe.sem_inc(s, BASE)
            pe.wait_ge(init, 5)
            with pe.Fori(0, NK) as i:
                for b in range(BATCH):
                    p, r = b % 2, 1 - b % 2
                    n = counts(i, b)
                    read_state, solve, attend = scan_parts(r, n)

                    def differences():
                        pe.wait_ge(rows_in, n(32) - BASE + 32)
                        pe.wait_ge(z_done, n(2))
                        for g in range(REP):
                            nc.tensor.matmul(ps[4 + g][:, :], identb[:, :], hide[:, :, :].rearrange("p c t -> p (c t)"),
                                             start=True, stop=False)
                            for c in range(NC_):
                                at = slice((g * NC_ + c) * C, (g * NC_ + c + 1) * C)
                                last = nc.tensor.matmul(ps[4 + g][:, c * C:(c + 1) * C], lrow[:, at], rrow[:, at],
                                                        start=False, stop=(c == NC_ - 1))
                            last.then_inc(dt_ps, 1)

                    def project(j):
                        if j < 2:
                            pe.wait_ge(decay_done, n(2) + j + 1)
                        else:
                            pe.wait_ge(acc_done, n(2) + j - 1)
                        if j == 0:
                            pe.wait_ge(win_in, i * 16 + 16)
                        for m in range(KT):
                            last = nc.tensor.matmul(ps[PROJ_BANK[j]][:, :], w_in[:, m * 4 * P + j * P:m * 4 * P + (j + 1) * P],
                                                    xnT[:, m, b * T:(b + 1) * T], start=(m == 0), stop=(m == KT - 1))
                        last.then_inc(proj_ps, 1)

                    def by_token(j):
                        pe.wait_ge(mixed_done, n(4) + j + 1)
                        for c in range(NC_):
                            last = nc.tensor.transpose(ps[PROJ_BANK[j]][:, c * C:(c + 1) * C], mixed[:, j, c * C:(c + 1) * C], ident)
                        last.then_inc(qk_ps if j < 2 else v_ps, 1)

                    differences()
                    for lv in range(NL):
                        merge_w(n, lv, 0)
                        merge_w(n, lv, 1)
                        if lv == 0:
                            gated_transpose(n)
                        if lv == 1:
                            project_out(n, i + (1 if b < 2 else 2))
                        if lv == 2:
                            project(2)
                        if lv == 3:
                            by_token(1)
                        merge_x(n, lv, 0, r)
                        merge_x(n, lv, 1, r)
                        if lv == 0:
                            project(0)
                        if lv == 1:
                            project(1)
                        if lv == 2:
                            project(3)
                            by_token(0)
                        if lv == 4:
                            by_token(2)
                        if lv == 5:
                            by_token(3)
                    pe.wait_ge(inv_done, n(INV) + INV)
                    pe.wait_ge(v_done, n(2) + 2)
                    solve(0)
                    for j in range(2):
                        pe.wait_ge(qk_done, n(8) + 4 * j + 4)
                        for c in range(NC_):
                            last = nc.tensor.transpose(ps[2 + j][:, c * C:(c + 1) * C], qk[:, j * NC_ + c, :], ident)
                        last.then_inc(qkT_ps, 1)
                    attend(0)
                    pe.wait_ge(qkT_done, n(2) + 2)
                    for j, other in enumerate((1, 0)):
                        for c in range(NC_):
                            cs = slice(c * C, (c + 1) * C)
                            last = nc.tensor.matmul(ps[j][:, cs], qkT[p][:, 1, cs], qkT[p][:, other, cs], start=True, stop=True)
                        last.then_inc(kk_ps, 1)
                    read_state(1)
                    pe.wait_ge(wz_in, (i + (1 if b == 0 else 2)) * 16)
                    project_z(n, (b - 1) % BATCH, 0)
                    solve(1)
                    project_z(n, (b - 1) % BATCH, 1)
                    attend(1)
                    read_state(2)
                    for g in range(REP):
                        pe.wait_ge(bm1_done, n(8) + NC_ * (g + 1))
                        for c in range(NC_):
                            last = nc.tensor.transpose(ps[2 + g][:, c * C:(c + 1) * C], bm1[:, g * NC_ + c, :], ident)
                        last.then_inc(b1_ps, 1)
                    solve(2)
                    attend(2)
                    read_state(3)
                    solve(3)
                    attend(3)
            n = counts(NK, 0)
            read_state, solve, attend = scan_parts(1, n)
            for lv in range(NL):
                merge_w(n, lv, 0)
                merge_w(n, lv, 1)
                if lv == 0:
                    gated_transpose(n)
                if lv == 1:
                    project_out(n, NK + 1)
                merge_x(n, lv, 0, 1)
                merge_x(n, lv, 1, 1)
            pe.wait_ge(inv_done, n(INV) + INV)
            pe.wait_ge(acc_done, n(2) + 2)
            project_z(n, BATCH - 1, 0)
            project_z(n, BATCH - 1, 1)
            for c in range(NC_):
                if c:
                    read_state(c)
                solve(c)
                attend(c)
            n = counts(NK, 1)
            gated_transpose(n)
            project_out(n, NK + 1)

        @block.scalar
        def _(act):
            def col(r, kind, u):
                return cols[r][:, kind * U + u:kind * U + u + 1]

            def chunks(ap):
                return ap.rearrange("p (c t) -> p c t", c=NC_)

            def scan_parts(r, n):
                def take_updates(c):
                    act.wait_ge(u_ps, n(4) + c + 1)
                    act.wait_ge(o_ps, n(4) + c)
                    for g in range(REP):
                        last = nc.scalar.activation(upd[:, g * P:(g + 1) * P], ps[6][:, g * P:(g + 1) * P], ACT.Copy,
                                                    scale=col(r, BETA, g * NC_ + c))
                    last.then_inc(upd_done, 1)

                def take_state_part(c):
                    act.wait_ge(qs_ps, n(3) + c)
                    act.wait_ge(o_done, n(4) + c)
                    for g in range(REP):
                        nc.scalar.activation(from_state[:, g * P:(g + 1) * P], ps[7][:, g * P:(g + 1) * P], ACT.Copy,
                                             scale=col(r, GAM, g * NC_ + c)).then_inc(fs_done, 1)

                def squares(c):
                    act.wait_ge(o_done, n(4) + c + 1)
                    if c == 0:
                        act.wait_ge(o_pow, n(3))
                        act.wait_ge(gT_ps, n(2) + 2)
                    for g in range(REP):
                        u = g * NC_ + c
                        last = nc.scalar.activation(gated[:, c, g * P:(g + 1) * P], o[:, c, g * P:(g + 1) * P], ACT.Square,
                                                    accum_out=o_sq[:, u:u + 1])
                    last.then_inc(osq_done, 1)

                return take_updates, take_state_part, squares

            def take_transposes(n):
                act.wait_ge(out_ps, n(2))
                for g in range(REP):
                    act.wait_ge(gT_ps, n(2) + g + 1)
                    nc.scalar.activation(gatedT[:, g, :], ps[6 + g][:, :], ACT.Copy).then_inc(gT_done, 1)

            def gate_z(n, h):
                act.wait_ge(gated_done, n(8) + 8)
                act.wait_ge(z_ps, n(2) + h + 1)
                nc.scalar.activation(z[:, 2 * h:2 * h + 2, :], ps[4 + h][:, :].rearrange("p (c d) -> p c d", c=2),
                                     ACT.Silu).then_inc(z_done, 1)

            def take_w(n, lv, g):
                act.wait_ge(w_ps, n(WX) + 2 * lv + g + 1)
                act.wait_ge(x_ps, n(WX) + max(2 * lv + g - 1, 0))
                nc.scalar.activation(wneg[:, g * NC_:(g + 1) * NC_, :], chunks(ps[g][:, :]), ACT.Copy, scale=-1.0).then_inc(w_done, 1)

            def scale_out_weights(loads):
                act.wait_ge(wout_in, loads * 16)
                nc.scalar.activation(w_outn[:, :, :], w_out[:, :, :], ACT.Copy, scale=norm_w[:, 0:1]).then_inc(wout_done, 1)

            for s in (decay_done, conv0_done, mixed_done, sq_done, qk_done, v_done, qkT_done, w_done,
                      z_done, fs_done, upd_done, osq_done, gT_done):
                act.sem_inc(s, BASE)
            act.wait_ge(norm_in, 16)
            act.wait_ge(init, 5)
            scale_out_weights(1)
            with act.Fori(0, NK) as i:
                for b in range(BATCH):
                    p, r = b % 2, 1 - b % 2
                    n = counts(i, b)
                    take_updates, take_state_part, squares = scan_parts(r, n)

                    def first_tap(j):
                        act.wait_ge(proj_ps, n(4) + j + 1)
                        act.wait_ge(mixed_done, n(4))
                        nc.scalar.activation(conv[:, j, :], ps[PROJ_BANK[j]][:, :], ACT.Copy,
                                             scale=w_in[:, KT * 4 * P + j * KC + KC - 1:KT * 4 * P + (j + 1) * KC]).then_inc(conv0_done, 1)

                    def silu(j):
                        act.wait_ge(tap_done, n(12) + 3 * j + 3)
                        act.wait_ge(qk_ps if j < 2 else v_ps, n(2))
                        nc.scalar.activation(mixed[:, j, :], conv[:, j, :], ACT.Silu).then_inc(mixed_done, 1)

                    def qk_squares(j):
                        act.wait_ge(qk_ps, n(2) + j + 1)
                        act.wait_ge(qk_pow, n(3))
                        act.wait_ge(o_ps, n(4))
                        for c in range(NC_):
                            u = j * NC_ + c
                            nc.scalar.activation(kw[p][:, u, :], ps[4 + j][:, c * C:(c + 1) * C], ACT.Square,
                                                 accum_out=qk_sq[:, u:u + 1]).then_inc(sq_done, 1)

                    def normalise(j):
                        act.wait_ge(qk_pow, n(3) + 3)
                        act.wait_ge(qkT_ps, n(2))
                        act.wait_ge(kw_done, n(8))
                        for c in range(NC_):
                            u = j * NC_ + c
                            nc.scalar.activation(qk[:, u, :], ps[4 + j][:, c * C:(c + 1) * C], ACT.Copy,
                                                 scale=qk_r[:, u:u + 1]).then_inc(qk_done, 1)

                    def take_v(j):
                        act.wait_ge(v_ps, n(2) + j + 1)
                        nc.scalar.activation(v[p][:, j * NC_:(j + 1) * NC_, :], chunks(ps[6 + j][:, :]), ACT.Copy).then_inc(v_done, 1)

                    act.wait_ge(b_done, n(8))
                    act.wait_ge(m_done, n(2))
                    act.wait_ge(d1_done, n(2))
                    for g in range(REP):
                        act.wait_ge(dt_ps, n(2) + g + 1)
                        nc.scalar.activation(decay[:, g * NC_:(g + 1) * NC_, :], chunks(ps[4 + g][:, :]), ACT.Exp).then_inc(decay_done, 1)
                    if b == 2:
                        act.wait_ge(out_ps, n(2))
                        scale_out_weights(i + 2)
                    for lv in range(NL):
                        take_w(n, lv, 0)
                        take_w(n, lv, 1)
                        if lv == 0:
                            take_transposes(n)
                            first_tap(0)
                        if lv == 1:
                            first_tap(1)
                            silu(0)
                        if lv == 2:
                            first_tap(2)
                            silu(1)
                            first_tap(3)
                            qk_squares(0)
                        if lv == 3:
                            qk_squares(1)
                            silu(2)
                        if lv == 4:
                            silu(3)
                            normalise(0)
                    normalise(1)
                    for j in range(2):
                        take_v(j)
                    take_updates(0)
                    for j in range(2):
                        act.wait_ge(qkT_ps, n(2) + j + 1)
                        nc.scalar.activation(qkT[p][:, j, :], ps[2 + j][:, :], ACT.Copy).then_inc(qkT_done, 1)
                    squares(0)
                    take_state_part(1)
                    gate_z(n, 0)
                    take_updates(1)
                    gate_z(n, 1)
                    squares(1)
                    take_state_part(2)
                    take_updates(2)
                    squares(2)
                    take_state_part(3)
                    take_updates(3)
                    squares(3)
            n = counts(NK, 0)
            take_updates, take_state_part, squares = scan_parts(1, n)
            for lv in range(NL):
                take_w(n, lv, 0)
                take_w(n, lv, 1)
                if lv == 0:
                    take_transposes(n)
            gate_z(n, 0)
            gate_z(n, 1)
            for c in range(NC_):
                if c:
                    take_state_part(c)
                take_updates(c)
                squares(c)
            take_transposes(counts(NK, 1))

        @block.vector
        def _(dve):
            def col(r, kind, u):
                return cols[r][:, kind * U + u:kind * U + u + 1]

            def chunks(ap):
                return ap.rearrange("p (c t) -> p c t", c=NC_)

            def scan_parts(r, n):
                def residual(c):
                    dve.wait_ge(ks_ps, n(3) + c)
                    dve.wait_ge(u_ps, n(4) + c)
                    for g in range(REP):
                        u = g * NC_ + c
                        nc.vector.scalar_tensor_tensor(resid[:, g * P:(g + 1) * P], ps[6][:, g * P:(g + 1) * P],
                                                       col(r, NGAM, u), v[r][:, u, :], ALU.mult, ALU.add).then_inc(r_done, 1)

                def output(c):
                    dve.wait_ge(o_ps, n(4) + c + 1)
                    if c < NC_ - 1:
                        dve.wait_ge(st_done, n(5) + max(2 * c - 1, 0))
                        if c:
                            for g in range(REP):
                                part = slice(g * P, (g + 1) * P)
                                nc.vector.scalar_tensor_tensor(state[:, part], state[:, part], col(r, GAMC, g * NC_ + c),
                                                               ps[7][:, (REP + g) * P:(REP + g + 1) * P],
                                                               ALU.mult, ALU.add).then_inc(st_done, 1)
                        else:
                            nc.vector.tensor_copy(state[:, :], ps[7][:, REP * P:2 * REP * P]).then_inc(st_done, 1)
                    if c:
                        dve.wait_ge(fs_done, n(6) + 2 * c)
                        nc.vector.tensor_tensor(o[:, c, :], ps[7][:, 0:REP * P], from_state[:, :], ALU.add).then_inc(o_done, 1)
                    else:
                        dve.wait_ge(osq_done, n(4))
                        nc.vector.tensor_copy(o[:, c, :], ps[7][:, 0:REP * P]).then_inc(o_done, 1)

                return residual, output

            def gating(n):
                dve.wait_ge(o_pow, n(3))
                dve.wait_ge(o_done, n(4))
                dve.wait_ge(z_done, n(2))
                dve.wait_ge(gT_ps, n(2))
                for g in range(REP):
                    for c in range(NC_):
                        u = g * NC_ + c
                        part = slice(g * P, (g + 1) * P)
                        nc.vector.scalar_tensor_tensor(gated[:, c, part], o[:, c, part], o_r[:, u:u + 1], z[:, c, part],
                                                       ALU.mult, ALU.mult).then_inc(gated_done, 1)

            def add_out(n, tb):
                for h in range(2):
                    dve.wait_ge(out_ps, n(2) + h + 1)
                    at = slice(tb * NC_ + 2 * h, tb * NC_ + 2 * h + 2)
                    nc.vector.tensor_tensor(acc[:, at, :], ps[6 + h][:, :].rearrange("p (c d) -> p c d", c=2),
                                            acc[:, at, :], ALU.add).then_inc(acc_done, 1)

            def update_inverse(n, lv, g, r):
                us = slice(g * NC_, (g + 1) * NC_)
                dve.wait_ge(x_ps, n(WX) + 2 * lv + g + 1)
                if lv:
                    dve.wait_ge(inv_done, n(INV) + 4 * (lv - 1) + 2 * g + 2)
                nc.vector.tensor_tensor(inv[r][:, us, :], chunks(ps[2 + g][:, :]), inv[r][:, us, :], ALU.add).then_inc(inv_done, 1)
                if lv < NL - 2:
                    dve.wait_ge(inv_done, n(INV) + 4 * lv + 2 * g + 1)
                    nc.vector.transpose(invT[:, us, :], inv[r][:, us, :]).then_inc(inv_done, 1)
                elif lv == NL - 2:
                    nc.vector.tensor_tensor(invT[:, us, :], chunks(ps[g][:, :]), invT[:, us, :], ALU.add).then_inc(inv_done, 1)

            for s in (tap_done, bm1_done, b_done, m_done, kw_done, inv1_done, inv_done,
                      r_done, st_done, o_done, gated_done, acc_done):
                dve.sem_inc(s, BASE)
            nc.vector.memset(lrow[:, :], 1.0)
            nc.vector.memset(rrow[:, :], 1.0).then_inc(init, 1)
            for t in (acc, qkT[1], v[1], kw[1], scores[1], inv[1], invT, bmat, o, z, bs[0][0], bs[0][1], bs[1][0], bs[1][1]):
                nc.vector.memset(t[:, :, :], 0.0)
            nc.vector.memset(o_r[:, :], 0.0)
            nc.vector.memset(eps8[:, :], L2_EPS)
            nc.vector.memset(half8[:, :], -0.5)
            nc.vector.memset(inv128[:, :], 1.0 / P)
            nc.vector.memset(qk_scale8[:, 0:NC_], float(P) ** -0.5)
            nc.vector.memset(qk_scale8[:, NC_:U], 1.0).then_inc(init, 1)
            nc.vector.memset(cols[1][:, :], 0.0).then_inc(init, 1)
            nc.vector.tensor_copy(identb[:, :], cst[:, IDENT:IDENT + P]).then_inc(init, 1)
            nc.vector.tensor_copy(hide[:, :, :], cst[:, HIDE:HIDE + P].unsqueeze(1).to_broadcast([P, NC_, C])).then_inc(init, 1)
            dve.wait_ge(init, 5)

            with dve.Fori(0, NK) as i:
                for b in range(BATCH):
                    p, r = b % 2, 1 - b % 2
                    n = counts(i, b)
                    residual, output = scan_parts(r, n)

                    def taps(j):
                        for t in range(KC - 1):
                            shift = KC - 1 - t
                            k = 4 * KT * P + j * KC + t
                            if t == 0:
                                dve.wait_ge(conv0_done, n(4) + j + 1)
                            else:
                                dve.wait_ge(tap_done, n(12) + 3 * j + t)
                            nc.vector.scalar_tensor_tensor(conv[:, j, shift:T], ps[PROJ_BANK[j]][:, 0:T - shift], w_in[:, k:k + 1],
                                                           conv[:, j, shift:T], ALU.mult, ALU.add).then_inc(tap_done, 1)

                    def b_of_head(g):
                        for dst, scale, done in ((bm1, decay1, bm1_done), (bmat, decay, b_done)):
                            for c in range(NC_):
                                u = g * NC_ + c
                                nc.vector.scalar_tensor_tensor(dst[:, u, :], ps[0][:, c * C:(c + 1) * C], col(p, BETA, u),
                                                               scale[:, u, :], ALU.mult, ALU.mult).then_inc(done, 1)

                    def decayed_k(g):
                        for c in range(NC_):
                            u = g * NC_ + c
                            nc.vector.tensor_scalar(kw[p][:, u, :], qk[:, NC_ + c, :], col(p, WSUF, u), None,
                                                    ALU.mult).then_inc(kw_done, 1)

                    def first_transpose(g):
                        us = slice(g * NC_, (g + 1) * NC_)
                        dve.wait_ge(b1_ps, n(2) + g + 1)
                        nc.vector.tensor_tensor(invT[:, us, :], chunks(ps[2 + g][:, :]),
                                                cst[:, IDENT:IDENT + P].unsqueeze(1).to_broadcast([P, NC_, P]),
                                                ALU.add).then_inc(inv1_done, 1)

                    gating(n)
                    for lv in range(NL):
                        update_inverse(n, lv, 0, r)
                        update_inverse(n, lv, 1, r)
                        if lv == 0:
                            taps(0)
                        if lv == 1:
                            add_out(n, (b - 2) % BATCH)
                            taps(1)
                        if lv == 2:
                            taps(2)
                        if lv == 3:
                            taps(3)
                    output(0)
                    dve.wait_ge(kk_ps, n(2) + 1)
                    dve.wait_ge(cols_in, n(16) - BASE + 16)
                    dve.wait_ge(decay_done, n(2) + 2)
                    dve.wait_ge(d1_done, n(2) + 2)
                    dve.wait_ge(bs_done, n(WX - 4) + WX - 4)
                    dve.wait_ge(bs01_done, n(4))
                    dve.wait_ge(x1_done, n(2))
                    dve.wait_ge(b1_ps, n(2))
                    b_of_head(0)
                    residual(1)
                    b_of_head(1)
                    output(1)
                    dve.wait_ge(kk_ps, n(2) + 2)
                    for g in range(REP):
                        us = slice(g * NC_, (g + 1) * NC_)
                        nc.vector.tensor_tensor(scores[p][:, us, :], chunks(ps[1][:, :]), decay[:, us, :], ALU.mult).then_inc(m_done, 1)
                    residual(2)
                    dve.wait_ge(qk_done, n(8) + 8)
                    decayed_k(0)
                    output(2)
                    dve.wait_ge(w_ps, n(WX) + WX)
                    first_transpose(0)
                    residual(3)
                    first_transpose(1)
                    output(3)
                    decayed_k(1)

            n = counts(NK, 0)
            residual, output = scan_parts(1, n)
            gating(n)
            for lv in range(NL):
                update_inverse(n, lv, 0, 1)
                update_inverse(n, lv, 1, 1)
                if lv == 1:
                    add_out(n, BATCH - 2)
            for c in range(NC_):
                if c:
                    residual(c)
                output(c)
            n = counts(NK, 1)
            gating(n)
            add_out(n, BATCH - 1)
            dve.wait_ge(acc_done, n(2) + 2)
            for b in range(BATCH):
                at = slice(b * NC_, (b + 1) * NC_)
                nc.vector.tensor_tensor(acc[:, at, :], acc[:, at, :], gate[:, at, :], ALU.mult).then_inc(acc_done, 1)
            dve.wait_ge(x_in, 16 * BATCH)
            dve.wait_ge(acc_done, n(2) + 2 + BATCH)
            for b in range(BATCH):
                row = acc[:, b * NC_:(b + 1) * NC_, :].rearrange("p c d -> p (c d)")
                nc.vector.tensor_tensor(row, row, x_back[b], ALU.add).then_inc(final, 1)

        @block.gpsimd
        def _(pool):
            def output_norms(n):
                pool.wait_ge(osq_done, n(4) + 4)
                pool.wait_ge(gated_done, n(8) + 8)
                nc.gpsimd.tensor_tensor(o_t[:, :], o_sq[:, :], inv128[:, :], ALU.mult).then_inc(o_pow, 1)
                pool.wait_ge(o_pow, n(3) + 1)
                nc.gpsimd.tensor_tensor(o_t[:, :], o_t[:, :], eps8[:, :], ALU.add).then_inc(o_pow, 1)
                pool.wait_ge(o_pow, n(3) + 2)
                nc.gpsimd.tensor_tensor(o_r[:, :], o_t[:, :], half8[:, :], ALU.pow).then_inc(o_pow, 1)

            def masked(dst, src, g, at):
                mask = cst[:, at:at + P].unsqueeze(1).to_broadcast([P, NC_, P])
                return nc.gpsimd.tensor_tensor(dst, src[:, g * NC_:(g + 1) * NC_, :], mask, ALU.mult)

            def mask_level(n, lv, g):
                pool.wait_ge(w_ps, n(WX) + 2 * (lv - 2) + g + 1)
                masked(bs[g][lv % 2][:, :, :], bmat, g, MERGE2 + lv * P).then_inc(bs_done, 1)

            for s in (qk_pow, d1_done, x1_done, bs01_done, bs_done, o_pow):
                pool.sem_inc(s, BASE)
            pool.wait_ge(init, 5)
            with pool.Fori(0, NK) as i:
                for b in range(BATCH):
                    p = b % 2
                    n = counts(i, b)
                    for lv in range(2, NL):
                        for g in range(REP):
                            mask_level(n, lv, g)
                        if lv == 2:
                            pool.wait_ge(bm1_done, n(8))
                            for g in range(REP):
                                pool.wait_ge(decay_done, n(2) + g + 1)
                                masked(decay1[:, g * NC_:(g + 1) * NC_, :], decay, g, MERGE1).then_inc(d1_done, 1)
                    pool.wait_ge(sq_done, n(8) + 8)
                    pool.wait_ge(qk_done, n(8))
                    nc.gpsimd.tensor_tensor(qk_t[:, :], qk_sq[:, :], eps8[:, :], ALU.add).then_inc(qk_pow, 1)
                    pool.wait_ge(qk_pow, n(3) + 1)
                    nc.gpsimd.tensor_tensor(qk_p[:, :], qk_t[:, :], half8[:, :], ALU.pow).then_inc(qk_pow, 1)
                    pool.wait_ge(qk_pow, n(3) + 2)
                    nc.gpsimd.tensor_tensor(qk_r[:, :], qk_p[:, :], qk_scale8[:, :], ALU.mult).then_inc(qk_pow, 1)
                    for g in range(REP):
                        pool.wait_ge(b_done, n(8) + NC_ * (g + 1))
                        pool.wait_ge(w_ps, n(WX) + WX)
                        masked(bs[g][0][:, :, :], bmat, g, MERGE2).then_inc(bs01_done, 1)
                    for g in range(REP):
                        us = slice(g * NC_, (g + 1) * NC_)
                        pool.wait_ge(u_ps, n(4))
                        nc.gpsimd.tensor_tensor(inv[p][:, us, :], bm1[:, us, :],
                                                cst[:, IDENT:IDENT + P].unsqueeze(1).to_broadcast([P, NC_, P]),
                                                ALU.add).then_inc(x1_done, 1)
                    for g in range(REP):
                        pool.wait_ge(b_done, n(8) + NC_ * (g + 1))
                        masked(bs[g][1][:, :, :], bmat, g, MERGE2 + P).then_inc(bs01_done, 1)
                    output_norms(n)
            n = counts(NK, 0)
            for lv in range(2, NL):
                for g in range(REP):
                    mask_level(n, lv, g)
            output_norms(n)


_INS = ["x", "small_w", "decay_rows", "consts", "ffn_gate", "ffn_up", "ffn_down", "w_in", "w_z", "w_out", "norm_w"]


def program(nc, a, out):
    with ExitStack() as ctx:
        def sb(name, shape):
            return ctx.enter_context(nc.sbuf_tensor(name, shape, F32))

        keep = {
            "cst": sb("cst", [P, NCONST]),
            "xnT": sb("xnT", [P, KT, BATCH * T]),
            "gate": sb("gate", [P, TILES, D]),
            "prep": sb("prep", [P, STEPS, KINDS * U]),
            "cst_dram": a["consts"],
        }
        g_rows = nc.dram_tensor("g_rows", [4, UNITS * C], F32).ap()
        comb_rows = nc.dram_tensor("comb_rows", [TILES * (E + 1), P], F32).ap()
        prepare_block(nc, a["x"], a["small_w"], a["decay_rows"], keep, g_rows, comb_rows)
        ffn_block(nc, a["ffn_gate"], a["ffn_up"], a["ffn_down"], keep, comb_rows)
        recurrent_block(nc, a["x"], a["w_in"], a["w_z"], a["w_out"], a["norm_w"], keep, g_rows, out)


def kernel(**inputs):
    import concourse.bacc as bacc
    from concourse.bass_utils import run_bass_kernel_spmd

    x = {k: np.asarray(v_) for k, v_ in inputs.items()}

    def rows(w):
        return w.reshape(KT, P, -1).transpose(1, 0, 2)

    def padded(w):
        return np.concatenate([w, np.zeros((FT * P - F,) + w.shape[1:], w.dtype)])

    def by_unit(row):
        return np.broadcast_to(row.reshape(NK, 1, REP, 1), (NK, BATCH, REP, NC_)).reshape(UNITS)

    keys = NK * P
    wqkv, conv_w = x["L0_attn_W_qkv"], x["L0_attn_conv_w"]
    heads = [wqkv[:, :keys].reshape(D, NK, 1, P), wqkv[:, keys:2 * keys].reshape(D, NK, 1, P),
             wqkv[:, 2 * keys:].reshape(D, NK, REP, P)]
    w_in = np.concatenate(heads, 2).reshape(KT, P, NK, 4 * P).transpose(2, 1, 0, 3).reshape(NK, P, KT * 4 * P)
    taps = np.concatenate([conv_w[:keys].reshape(NK, 1, P, KC), conv_w[keys:2 * keys].reshape(NK, 1, P, KC),
                           conv_w[2 * keys:].reshape(NK, REP, P, KC)], 1).transpose(0, 2, 1, 3).reshape(NK, P, 4 * KC)
    gu_e, gu_s = x["L0_ffn_We_gate_up"], x["L0_ffn_Ws_gate_up"]

    def up_or_gate(k):
        return padded(np.concatenate([gu_e[:, :, k * I_MOE:(k + 1) * I_MOE].transpose(0, 2, 1).reshape(E * I_MOE, D),
                                      gu_s[:, k * I_SH:(k + 1) * I_SH].T])).T

    down = padded(np.concatenate([x["L0_ffn_We_down"].reshape(E * I_MOE, D), x["L0_ffn_Ws_down"]]))
    data = {
        "x": x["L0_attn_hidden_states"],
        "small_w": rows(np.concatenate([x["L0_attn_W_b"], x["L0_attn_W_a"], x["L0_ffn_W_router"].T, x["L0_ffn_W_sgate"].T], 1)),
        "decay_rows": np.stack([by_unit(x["L0_attn_dt_bias"]), by_unit(x["L0_attn_A_log"])]),
        "consts": constants(),
        "ffn_gate": rows(up_or_gate(0)),
        "ffn_up": rows(up_or_gate(1)),
        "ffn_down": down.reshape(FT, P, D).transpose(1, 0, 2),
        "w_in": np.concatenate([w_in, taps], 2),
        "w_z": x["L0_attn_W_z"].reshape(KT, P, NK, REP * P).transpose(2, 1, 0, 3),
        "w_out": x["L0_attn_W_out"].reshape(NK, REP, P, D).transpose(0, 2, 1, 3),
        "norm_w": x["L0_attn_norm_w"].reshape(P, 1),
    }
    nc = bacc.Bacc("TRN2", target_bir_lowering=False, num_devices=1)
    arrays, aps = {}, {}
    for name in _INS:
        arr = np.ascontiguousarray(data[name])
        arrays[f"in_{name}"] = arr
        aps[name] = nc.dram_tensor(f"in_{name}", arr.shape, mybir.dt.from_np(arr.dtype), kind="ExternalInput").ap()
    out = nc.dram_tensor("out", [BATCH, T, D], F32, kind="ExternalOutput").ap()
    program(nc, aps, out)
    r = run_bass_kernel_spmd(nc, [arrays], core_ids=[0])
    return r.results[0]["out"]
```

```python
from contextlib import ExitStack

import numpy as np
import concourse.bass as bass
from concourse import mybir

F32 = mybir.dt.float32
ALU = mybir.AluOpType
ACT = mybir.ActivationFunctionType
AX = mybir.AxisListType

P = 128
BASE = 1
BATCH, T, D = 4, 512, 256
KT = D // P
NV, NK, KC = 32, 16, 4
REP = NV // NK
C = 128
NC_ = T // C
TILES = BATCH * NC_
U = REP * NC_
STEPS = NK * BATCH
UNITS = STEPS * U
E, I_MOE, I_SH = 8, 176, 704
F = E * I_MOE + I_SH
FT = -(-F // P)
NSMALL = 2 * NV + E + 1
LN_EPS, L2_EPS, RMS_EPS = 1e-5, 1e-6, 1e-6
LOG_DECAY_MIN = -110.0
ROUND = 1.5 * 2.0 ** 23
MASKED = -30000.0
LEVELS = (2, 4, 8, 16, 32, 64)
NL = len(LEVELS)
BETA, GAM, NGAM, WSUF, GAMC, NHI, NLO = range(7)
KINDS = 7


def constants():
    r, c = np.arange(P)[:, None], np.arange(P)[None, :]

    def merge(s):
        return ((r // s) % 2 == 0) & (c // s == r // s + 1)

    parts = [r == c, r <= c, r > c, np.ones((P, P), bool), (c < r) * MASKED, merge(1) * -1.0]
    parts += [merge(s) for s in LEVELS]
    parts += [np.broadcast_to(np.arange(E) - E, (P, E))]
    return np.ascontiguousarray(np.concatenate([np.asarray(x, np.float32) for x in parts], 1))


IDENT, UPTO, AFTER, ONES, HIDE, MERGE1, MERGE2 = (P * k for k in range(7))
IOTA = MERGE2 + NL * P
NCONST = IOTA + E


def prepare_block(nc, x, small_w, decay_rows, keep, g_rows, comb_rows):
    cst, xnT, prep = keep["cst"], keep["xnT"], keep["prep"]
    with ExitStack() as ctx:
        def sb(name, shape, dt=F32):
            return ctx.enter_context(nc.sbuf_tensor(name, shape, dt))

        def sem(name):
            return ctx.enter_context(nc.semaphore(name))

        xs = sb("xs", [P, TILES, D])
        ws = sb("ws", [P, KT, NSMALL])
        stats = sb("stats", [P, TILES, 6])
        mean = sb("mean", [P, TILES])
        diff = sb("diff", [P, TILES])
        var = sb("var", [P, TILES])
        rstd = sb("rstd", [P, TILES])
        expo = sb("expo", [P, TILES])
        xn = sb("xn", [P, 2, D])
        xt = sb("xt", [P, 2, D])
        a_b = sb("a_b", [P, UNITS])
        a_a = sb("a_a", [P, UNITS])
        routed = sb("routed", [P, TILES, E + 1])
        dtb = sb("dtb", [P, UNITS])
        a_exp = sb("a_exp", [P, UNITS])
        absu = sb("absu", [P, UNITS])
        em = sb("em", [P, UNITS])
        den = sb("den", [P, UNITS])
        sq = sb("sq", [P, UNITS])
        ser = sb("ser", [P, UNITS])
        g = sb("g", [P, UNITS])
        g_hi = sb("g_hi", [P, UNITS])
        g_lo = sb("g_lo", [P, UNITS])
        sum_hi = sb("sum_hi", [P, UNITS])
        sum_lo = sb("sum_lo", [P, UNITS])
        sum_g = sb("sum_g", [P, UNITS])
        rows = sb("rows", [P, 2, UNITS])
        top = sb("top", [P, TILES])
        pr = sb("pr", [P, TILES, E])
        hit = sb("hit", [P, TILES, E])
        hot1 = sb("hot1", [P, TILES, E])
        hot2 = sb("hot2", [P, TILES, E])
        comb = sb("comb", [P, TILES, E + 1])
        combT = sb("combT", [P, 2, P])
        ps_t = [ctx.enter_context(nc.psum_tensor(f"ps_t{k}", [P, 512], F32)) for k in range(2)]
        ps_s = [ctx.enter_context(nc.psum_tensor(f"ps_s{k}", [P, 512], F32)) for k in range(2)]
        ps_g = [ctx.enter_context(nc.psum_tensor(f"ps_g{k}", [P, 512], F32)) for k in range(4)]

        loaded, w_loaded = sem("x_loaded"), sem("w_loaded")
        vec, act_s, pow_done = sem("vec_chain"), sem("act_chain"), sem("pow_done")
        var_ready, stored = sem("var_ready"), sem("rows_stored")
        xn_ready, xnt_ps, xt_ready, xt_kept = sem("xn_ready"), sem("xnT_ps"), sem("xt_ready"), sem("xnT_kept")
        small_ps, small_out = sem("small_ps"), sem("small_out")
        u_ready, e_ready, g_ready, sums_ps, sums_out = sem("u_ready"), sem("e_ready"), sem("g_ready"), sem("sums_ps"), sem("sums_out")
        sumg_ready, rows_ps, rows_out, gam_ready = sem("sumg_ready"), sem("rows_ps"), sem("rows_out"), sem("gam_ready")
        logit_ready, prob_exp, sg_ready = sem("logit_ready"), sem("prob_exp"), sem("sg_ready")
        comb_ready, comb_ps, comb_out = sem("comb_ready"), sem("comb_ps"), sem("comb_out")
        block = ctx.enter_context(nc.Block())

        @block.sync
        def _(sp):
            for b in range(BATCH):
                sp.dma_start(xs[:, b * NC_:(b + 1) * NC_, :],
                             x[b].rearrange("(c p) d -> p c d", p=P)).then_inc(loaded, 16)
            sp.dma_start(cst[:, :], keep["cst_dram"]).then_inc(w_loaded, 16)
            sp.dma_start(ws[:, :, :], small_w).then_inc(w_loaded, 16)
            sp.dma_start(dtb[:, :], decay_rows[0:1, :].partition_broadcast(P)).then_inc(w_loaded, 16)
            sp.dma_start(a_exp[:, :], decay_rows[1:2, :].partition_broadcast(P)).then_inc(w_loaded, 16)
            sp.wait_ge(comb_out, 2)
            sp.dma_start(comb_rows[0:P, :], combT[:, 0, :]).then_inc(stored, 16)
            sp.dma_start(comb_rows[P:TILES * (E + 1), :], combT[0:TILES * (E + 1) - P, 1, :]).then_inc(stored, 16)
            sp.wait_ge(rows_out, 2)
            for k in range(2):
                sp.dma_start(g_rows[k].rearrange("(q u t) -> u q t", q=4, u=P),
                             rows[:, k, :].rearrange("u (q t) -> u q t", q=4)).then_inc(stored, 16)
            sp.wait_ge(stored, 4 * 16)

        @block.vector
        def _(dve):
            chain = [0]

            def link(ins):
                chain[0] += 1
                ins.then_inc(vec, 1)
                dve.wait_ge(vec, chain[0])

            dve.wait_ge(loaded, BATCH * 16)
            with dve.Fori(0, TILES) as t:
                nc.vector.bn_stats(stats[:, bass.ds(t, 1), :], xs[:, bass.ds(t, 1), :]).then_inc(small_out, 1)
            dve.wait_ge(small_out, TILES)
            link(nc.vector.tensor_tensor(mean[:, :], stats[:, :, 1], stats[:, :, 4], ALU.add))
            link(nc.vector.tensor_tensor(diff[:, :], stats[:, :, 1], stats[:, :, 4], ALU.subtract))
            link(nc.vector.tensor_tensor(var[:, :], stats[:, :, 2], stats[:, :, 5], ALU.add))
            link(nc.vector.tensor_scalar(mean[:, :], mean[:, :], 0.5, None, ALU.mult))
            link(nc.vector.tensor_tensor(diff[:, :], diff[:, :], diff[:, :], ALU.mult))
            link(nc.vector.tensor_scalar(diff[:, :], diff[:, :], 0.25, LN_EPS, ALU.mult, ALU.add))
            link(nc.vector.memset(expo[:, :], -0.5))
            nc.vector.scalar_tensor_tensor(var[:, :], var[:, :], 1.0 / D, diff[:, :],
                                           ALU.mult, ALU.add).then_inc(var_ready, 1)
            dve.wait_ge(pow_done, 1)
            a_bv = a_b[:, :].rearrange("p (h b v c) -> p h b v c", h=NK, b=BATCH, v=REP)
            a_av = a_a[:, :].rearrange("p (h b v c) -> p h b v c", h=NK, b=BATCH, v=REP)
            with dve.Fori(0, BATCH) as b:
                def normalise(c):
                    k = c % 2
                    dve.wait_ge(xnt_ps, b * NC_ + max(c - 1, 0) + BASE)
                    nc.vector.tensor_scalar(xn[:, k, :], xs[:, bass.ds(b * NC_ + c, 1), :],
                                            mean[:, bass.ds(b * NC_ + c, 1)], rstd[:, bass.ds(b * NC_ + c, 1)],
                                            ALU.subtract, ALU.mult).then_inc(xn_ready, 1)

                def take_small(c):
                    k = c % 2
                    dve.wait_ge(small_ps, b * NC_ + c + 1 + BASE)
                    nc.vector.tensor_copy(a_bv[:, :, bass.ds(b, 1), :, c],
                                          ps_s[k][:, 0:NV].rearrange("p (h o v) -> p h o v", v=REP, o=1)).then_inc(small_out, 1)
                    nc.vector.tensor_copy(a_av[:, :, bass.ds(b, 1), :, c],
                                          ps_s[k][:, NV:2 * NV].rearrange("p (h o v) -> p h o v", v=REP, o=1)).then_inc(small_out, 1)
                    nc.vector.tensor_copy(routed[:, bass.ds(b * NC_ + c, 1), :],
                                          ps_s[k][:, 2 * NV:NSMALL]).then_inc(small_out, 1)

                normalise(0)
                for c in range(NC_):
                    if c < NC_ - 1:
                        normalise(c + 1)
                    take_small(c)
            dve.wait_ge(small_out, 4 * TILES)
            dve.wait_ge(w_loaded, 64)
            nc.vector.tensor_tensor(a_a[:, :], a_a[:, :], dtb[:, :], ALU.add).then_inc(u_ready, 1)
            link(nc.vector.tensor_reduce(top[:, :], routed[:, :, 0:E], AX.X, ALU.max))
            nc.vector.tensor_tensor(pr[:, :, :], routed[:, :, 0:E],
                                    top[:, :].unsqueeze(2).to_broadcast([P, TILES, E]), ALU.subtract).then_inc(logit_ready, 1)
            dve.wait_ge(e_ready, 1)
            link(nc.vector.tensor_scalar(den[:, :], em[:, :], 2.0, None, ALU.add))
            link(nc.vector.reciprocal(den[:, :], den[:, :]))
            link(nc.vector.tensor_tensor(em[:, :], em[:, :], den[:, :], ALU.mult))
            link(nc.vector.tensor_tensor(sq[:, :], em[:, :], em[:, :], ALU.mult))
            link(nc.vector.tensor_scalar(ser[:, :], sq[:, :], 1.0 / 17, None, ALU.mult))
            for odd in (15, 13, 11, 9, 7, 5, 3):
                link(nc.vector.scalar_tensor_tensor(ser[:, :], ser[:, :], 1.0 / odd, sq[:, :], ALU.add, ALU.mult))
            link(nc.vector.scalar_tensor_tensor(ser[:, :], ser[:, :], 1.0, em[:, :], ALU.add, ALU.mult))
            link(nc.vector.tensor_scalar(ser[:, :], ser[:, :], 2.0, None, ALU.mult))
            link(nc.vector.scalar_tensor_tensor(ser[:, :], a_a[:, :], 0.0, ser[:, :], ALU.max, ALU.add))
            dve.wait_ge(e_ready, 2)
            link(nc.vector.scalar_tensor_tensor(g[:, :], ser[:, :], -1.0, a_exp[:, :], ALU.mult, ALU.mult))
            link(nc.vector.tensor_scalar(g[:, :], g[:, :], LOG_DECAY_MIN, None, ALU.max))
            link(nc.vector.tensor_scalar(g_hi[:, :], g[:, :], ROUND, -ROUND, ALU.add, ALU.add))
            nc.vector.tensor_tensor(g_lo[:, :], g[:, :], g_hi[:, :], ALU.subtract).then_inc(g_ready, 1)
            dve.wait_ge(prob_exp, 1)
            link(nc.vector.tensor_reduce(top[:, :], pr[:, :, :], AX.X, ALU.add))
            link(nc.vector.reciprocal(top[:, :], top[:, :]))
            link(nc.vector.tensor_tensor(pr[:, :, :], pr[:, :, :], top[:, :].unsqueeze(2).to_broadcast([P, TILES, E]), ALU.mult))
            iota = cst[:, IOTA:IOTA + E].unsqueeze(1).to_broadcast([P, TILES, E])

            def pick(hot, src):
                link(nc.vector.tensor_reduce(top[:, :], src[:, :, :], AX.X, ALU.max))
                topb = top[:, :].unsqueeze(2).to_broadcast([P, TILES, E])
                link(nc.vector.tensor_tensor(hit[:, :, :], src[:, :, :], topb, ALU.is_equal))
                link(nc.vector.tensor_tensor(hit[:, :, :], hit[:, :, :], iota, ALU.mult))
                link(nc.vector.tensor_reduce(top[:, :], hit[:, :, :], AX.X, ALU.min))
                link(nc.vector.tensor_tensor(hot[:, :, :], iota, topb, ALU.is_equal))

            pick(hot1, pr)
            link(nc.vector.scalar_tensor_tensor(hot2[:, :, :], hot1[:, :, :], -2.0, pr[:, :, :], ALU.mult, ALU.add))
            link(nc.vector.tensor_copy(comb[:, :, 0:E], hot2[:, :, :]))
            pick(hot2, comb[:, :, 0:E])
            link(nc.vector.tensor_tensor(hot1[:, :, :], hot1[:, :, :], hot2[:, :, :], ALU.add))
            nc.vector.tensor_tensor(comb[:, :, 0:E], hot1[:, :, :], pr[:, :, :], ALU.mult).then_inc(comb_ready, 1)
            dve.wait_ge(sums_out, 2)
            nc.vector.tensor_tensor(sum_g[:, :], sum_hi[:, :], sum_lo[:, :], ALU.add).then_inc(sumg_ready, 1)
            dve.wait_ge(gam_ready, 1)
            link(nc.vector.tensor_scalar(prep[:, :, NGAM * U:(NGAM + 1) * U], prep[:, :, GAM * U:(GAM + 1) * U],
                                         -1.0, None, ALU.mult))

        @block.gpsimd
        def _(pool):
            pool.wait_ge(var_ready, 1)
            nc.gpsimd.tensor_tensor(rstd[:, :], var[:, :], expo[:, :], ALU.pow).then_inc(pow_done, 1)

        @block.scalar
        def _(act):
            act.sem_inc(xt_kept, BASE)
            with act.Fori(0, BATCH) as b:
                for c in range(NC_):
                    k = c % 2
                    act.wait_ge(xnt_ps, b * NC_ + c + 1 + BASE)
                    act.wait_ge(small_ps, b * NC_ + max(c - 1, 0) + BASE)
                    nc.scalar.activation(xt[:, k, :], ps_t[k][:, 0:D], ACT.Copy).then_inc(xt_ready, 1)
                    nc.scalar.activation(xnT[:, :, bass.ds((b * NC_ + c) * P, P)],
                                         ps_t[k][:, 0:D].rearrange("p (k t) -> p k t", k=KT), ACT.Copy).then_inc(xt_kept, 1)
            act.wait_ge(small_out, 4 * TILES)
            act.wait_ge(w_loaded, 64)

            def units(ap):
                return ap.rearrange("p (s u) -> p s u", u=U)

            nc.scalar.activation(prep[:, :, BETA * U:(BETA + 1) * U], units(a_b[:, :]), ACT.Sigmoid).then_inc(act_s, 1)
            nc.scalar.activation(comb[:, :, E:E + 1], routed[:, :, E:E + 1], ACT.Sigmoid).then_inc(sg_ready, 1)
            act.wait_ge(u_ready, 1)
            nc.scalar.activation(absu[:, :], a_a[:, :], ACT.Abs).then_inc(act_s, 1)
            act.wait_ge(act_s, 2)
            nc.scalar.activation(em[:, :], absu[:, :], ACT.Exp, scale=-1.0).then_inc(e_ready, 1)
            nc.scalar.activation(a_exp[:, :], a_exp[:, :], ACT.Exp).then_inc(e_ready, 1)
            act.wait_ge(logit_ready, 1)
            nc.scalar.activation(pr[:, :, :], pr[:, :, :], ACT.Exp).then_inc(prob_exp, 1)
            act.wait_ge(sums_ps, 4)
            nc.scalar.activation(sum_hi[:, :], ps_g[0][:, :], ACT.Copy).then_inc(sums_out, 1)
            nc.scalar.activation(sum_lo[:, :], ps_g[1][:, :], ACT.Copy).then_inc(sums_out, 1)
            nc.scalar.activation(prep[:, :, WSUF * U:(WSUF + 1) * U], units(ps_g[2][:, :]), ACT.Exp).then_inc(act_s, 1)
            nc.scalar.activation(prep[:, :, GAMC * U:(GAMC + 1) * U], units(ps_g[3][:, :]), ACT.Exp).then_inc(act_s, 1)
            act.wait_ge(sumg_ready, 1)
            nc.scalar.activation(prep[:, :, GAM * U:(GAM + 1) * U], units(sum_g[:, :]), ACT.Exp).then_inc(gam_ready, 1)
            act.wait_ge(sums_out, 2)
            for kind, src in ((NHI, sum_hi), (NLO, sum_lo)):
                nc.scalar.activation(prep[:, :, kind * U:(kind + 1) * U], units(src[:, :]), ACT.Copy, scale=-1.0).then_inc(act_s, 1)
            act.wait_ge(rows_ps, 2)
            for k in range(2):
                nc.scalar.activation(rows[:, k, :], ps_t[k][:, :], ACT.Copy).then_inc(rows_out, 1)
            act.wait_ge(comb_ps, 1)
            nc.scalar.activation(combT[:, 0, :], ps_s[0][:, 0:P], ACT.Copy).then_inc(comb_out, 1)
            rest = TILES * (E + 1) - P
            nc.scalar.activation(combT[0:rest, 1, :], ps_s[1][0:rest, 0:P], ACT.Copy).then_inc(comb_out, 1)

        @block.tensor
        def _(pe):
            ident = cst[:, IDENT:IDENT + P]
            pe.sem_inc(xnt_ps, BASE)
            pe.sem_inc(small_ps, BASE)
            pe.wait_ge(w_loaded, 64)
            with pe.Fori(0, BATCH) as b:
                def transpose_tile(c):
                    k = c % 2
                    pe.wait_ge(xn_ready, b * NC_ + c + 1)
                    pe.wait_ge(xt_kept, b * NC_ + max(c - 1, 0) + BASE)
                    for m in range(KT):
                        last = nc.tensor.transpose(ps_t[k][:, m * P:(m + 1) * P], xn[:, k, m * P:(m + 1) * P], ident)
                    last.then_inc(xnt_ps, 1)

                def project_small(c):
                    k = c % 2
                    pe.wait_ge(xt_ready, b * NC_ + c + 1)
                    pe.wait_ge(small_out, TILES + 3 * (b * NC_ + max(c - 1, 0)))
                    for m in range(KT):
                        last = nc.tensor.matmul(ps_s[k][:, 0:NSMALL], xt[:, k, m * P:(m + 1) * P], ws[:, m, :],
                                                start=(m == 0), stop=(m == KT - 1))
                    last.then_inc(small_ps, 1)

                transpose_tile(0)
                for c in range(NC_):
                    if c < NC_ - 1:
                        transpose_tile(c + 1)
                    project_small(c)
            pe.wait_ge(g_ready, 1)
            for k, (at, src) in enumerate(((UPTO, g_hi), (UPTO, g_lo), (AFTER, g), (ONES, g))):
                nc.tensor.matmul(ps_g[k][:, :], cst[:, at:at + P], src[:, :], start=True, stop=True).then_inc(sums_ps, 1)
            pe.wait_ge(sums_out, 2)
            for k, src in enumerate((sum_hi, sum_lo)):
                for q in range(UNITS // P):
                    last = nc.tensor.transpose(ps_t[k][:, q * P:(q + 1) * P], src[:, q * P:(q + 1) * P], ident)
                last.then_inc(rows_ps, 1)
            pe.wait_ge(comb_ready, 1)
            pe.wait_ge(sg_ready, 1)
            flat = comb[:, :, :].rearrange("p t e -> p (t e)")
            rest = TILES * (E + 1) - P
            nc.tensor.transpose(ps_s[0][:, 0:P], flat[:, 0:P], ident)
            nc.tensor.transpose(ps_s[1][0:rest, 0:P], flat[:, P:P + rest], ident).then_inc(comb_ps, 1)


def ffn_block(nc, wg_dram, wu_dram, wd_dram, keep, comb_rows):
    xnT, gate = keep["xnT"], keep["gate"]
    spans = []
    for j in range(FT):
        at = j * P
        while at < (j + 1) * P:
            e = min(at // I_MOE, E)
            end = (j + 1) * P if e == E else min((e + 1) * I_MOE, (j + 1) * P)
            spans.append((j, at - j * P, end - j * P, e))
            at = end
    GROUPS = ((0, 1), (1, 4), (4, 9), (9, FT))
    comb_v = comb_rows.rearrange("(t e) c -> t e c", e=E + 1)
    with ExitStack() as ctx:
        def sb(name, shape, dt=F32):
            return ctx.enter_context(nc.sbuf_tensor(name, shape, dt))

        def sem(name):
            return ctx.enter_context(nc.semaphore(name))

        wg = sb("wg", [P, KT, FT * P])
        wu = sb("wu", [P, KT, FT * P])
        wd = sb("wd", [P, FT, D])
        hid = sb("hid", [P, FT, T])
        scale = sb("scale", [P, FT, T])
        silu_g = sb("silu_g", [P, 2, T])
        ps_g = [ctx.enter_context(nc.psum_tensor(f"fps_g{k}", [P, 512], F32)) for k in range(2)]
        ps_u = [ctx.enter_context(nc.psum_tensor(f"fps_u{k}", [P, 512], F32)) for k in range(2)]
        ps_o = [ctx.enter_context(nc.psum_tensor(f"fps_o{k}", [P, 512], F32)) for k in range(2)]
        w_in, wd_in, scale_in = [sem(f"ffn_w_in{k}") for k in range(len(GROUPS))], sem("wd_in"), sem("scale_in")
        g_ps, u_ps, silu_done, prod_done, hid_done = sem("g_ps"), sem("u_ps"), sem("silu_done"), sem("prod_done"), sem("hid_done")
        o_ps, gate_done = sem("o_ps"), sem("gate_done")
        block = ctx.enter_context(nc.Block())

        @block.sync
        def _(sp):
            for k, (j0, j1) in enumerate(GROUPS):
                cols = slice(j0 * P, j1 * P)
                sp.dma_start(wg[:, :, cols], wg_dram[:, :, cols]).then_inc(w_in[k], 16)
                sp.dma_start(wu[:, :, cols], wu_dram[:, :, cols]).then_inc(w_in[k], 16)
            sp.dma_start(wd[:, :, :], wd_dram).then_inc(wd_in, 16)

        @block.gpsimd
        def _(pool):
            with pool.Fori(0, BATCH) as b:
                pool.wait_ge(hid_done, b * FT + BASE)
                for j, p0, p1, e in spans:
                    src = comb_v[bass.ds(b * NC_, NC_), e, :].unsqueeze(0).to_broadcast([p1 - p0, NC_, P])
                    nc.gpsimd.dma_start(scale[p0:p1, j, :].rearrange("p (c t) -> p c t", c=NC_), src).then_inc(scale_in, 16)

        @block.scalar
        def _(act):
            act.sem_inc(silu_done, BASE)
            act.sem_inc(gate_done, BASE)
            with act.Fori(0, BATCH) as b:
                for j in range(FT):
                    act.wait_ge(g_ps, b * FT + j + 1)
                    act.wait_ge(hid_done, b * FT + max(j - 1, 0) + BASE)
                    nc.scalar.activation(silu_g[:, j % 2, :], ps_g[j % 2][:, :], ACT.Silu).then_inc(silu_done, 1)
                for c in range(NC_):
                    act.wait_ge(o_ps, b * NC_ + c + 1 + BASE)
                    nc.scalar.activation(gate[:, bass.ds(b * NC_ + c, 1), :], ps_o[c % 2][:, 0:D],
                                         ACT.Silu).then_inc(gate_done, 1)

        @block.vector
        def _(dve):
            dve.sem_inc(prod_done, BASE)
            dve.sem_inc(hid_done, BASE)
            with dve.Fori(0, BATCH) as b:
                dve.wait_ge(scale_in, b * (16 * len(spans)) + 16 * len(spans))
                for j in range(FT):
                    dve.wait_ge(silu_done, b * FT + j + 1 + BASE)
                    dve.wait_ge(u_ps, b * FT + j + 1)
                    if j == 0:
                        dve.wait_ge(o_ps, b * NC_ + BASE)
                    nc.vector.tensor_tensor(silu_g[:, j % 2, :], ps_u[j % 2][:, :], silu_g[:, j % 2, :],
                                            ALU.mult).then_inc(prod_done, 1)
                    dve.wait_ge(prod_done, b * FT + j + 1 + BASE)
                    nc.vector.tensor_tensor(hid[:, j, :], silu_g[:, j % 2, :], scale[:, j, :],
                                            ALU.mult).then_inc(hid_done, 1)

        @block.tensor
        def _(pe):
            pe.sem_inc(o_ps, BASE)
            with pe.Fori(0, BATCH) as b:
                for j in range(FT):
                    for k, (j0, _) in enumerate(GROUPS):
                        if j == j0:
                            pe.wait_ge(w_in[k], 32)
                    pe.wait_ge(silu_done, b * FT + max(j - 1, 0) + BASE)
                    pe.wait_ge(prod_done, b * FT + max(j - 1, 0) + BASE)
                    for w, ps, done in ((wg, ps_g, g_ps), (wu, ps_u, u_ps)):
                        for m in range(KT):
                            last = nc.tensor.matmul(ps[j % 2][:, :], w[:, m, j * P:(j + 1) * P],
                                                    xnT[:, m, bass.ds(b * T, T)], start=(m == 0), stop=(m == KT - 1))
                        last.then_inc(done, 1)
                pe.wait_ge(wd_in, 16)
                for c in range(NC_):
                    pe.wait_ge(gate_done, b * NC_ + max(c - 1, 0) + BASE)
                    if c == 0:
                        pe.wait_ge(hid_done, b * FT + FT + BASE)
                    for j in range(FT):
                        last = nc.tensor.matmul(ps_o[c % 2][:, 0:D], hid[:, j, c * P:(c + 1) * P], wd[:, j, :],
                                                start=(j == 0), stop=(j == FT - 1))
                    last.then_inc(o_ps, 1)


def recurrent_block(nc, x, w_in_dram, w_z_dram, w_out_dram, norm_dram, keep, g_rows, out):
    cst, xnT, prep, gate = keep["cst"], keep["xnT"], keep["prep"], keep["gate"]
    with ExitStack() as ctx:
        def sb(name, shape, dt=F32):
            return ctx.enter_context(nc.sbuf_tensor(name, shape, dt))

        def sem(name):
            return ctx.enter_context(nc.semaphore(name))

        acc = sb("acc", [P, TILES, D])
        w_in = sb("w_in", [P, KT * 4 * P + 4 * KC])
        w_z = sb("w_z", [P, KT, REP * P])
        w_out = sb("w_out", [P, REP, D])
        w_outn = sb("w_outn", [P, REP, D])
        norm_w = sb("norm_w", [P, 1])
        sums_row = sb("sums_row", [P, 2, U, C])
        cols = [sb(f"cols{k}", [P, KINDS * U]) for k in range(2)]
        eps8 = sb("eps8", [P, U])
        mhalf8 = sb("mhalf8", [P, U])
        half4 = sb("half4", [P, NC_])
        mone4 = sb("mone4", [P, NC_])
        scale8 = sb("scale8", [P, U])
        inv128 = sb("inv128", [P, U])
        decay = sb("decay", [P, U, C])
        decay1 = sb("decay1", [P, U, C])
        conv = sb("conv", [P, 4, T])
        mixed = sb("mixed", [P, 2, T])
        q_sq, k_sq = sb("q_sq", [P, NC_]), sb("k_sq", [P, NC_])
        q_t, k_t = sb("q_t", [P, NC_]), sb("k_t", [P, NC_])
        q_rinv, k_norm, k_inv2 = sb("q_rinv", [P, NC_]), sb("k_norm", [P, NC_]), sb("k_inv2", [P, NC_])
        beta_k2 = [sb(f"beta_k2{k}", [P, U]) for k in range(2)]
        q_scale = [sb(f"q_scale{k}", [P, U]) for k in range(2)]
        q_mean2 = [sb(f"q_mean2{k}", [P, U]) for k in range(2)]
        qkT = [sb(f"qkT{k}", [P, 2, T]) for k in range(2)]
        v = [sb(f"v{k}", [P, U, P]) for k in range(2)]
        kw = [sb(f"kw{k}", [P, U, P]) for k in range(2)]
        scores = [sb(f"scores{k}", [P, U, C]) for k in range(2)]
        bmat = sb("bmat", [P, U, C])
        bm1 = sb("bm1", [P, U, C])
        bs = [[sb(f"bs{g}{k}", [P, NC_, C]) for k in range(2)] for g in range(REP)]
        inv = [sb(f"inv{k}", [P, U, C]) for k in range(2)]
        invT = sb("invT", [P, U, C])
        wneg = sb("wneg", [P, U, C])
        state = sb("state", [P, REP * P])
        resid = sb("resid", [P, REP * P])
        from_state = sb("from_state", [P, REP * P])
        upd = sb("upd", [P, REP * P])
        o = sb("o", [P, NC_, REP * P])
        o_sq = sb("o_sq", [P, U])
        o_t = sb("o_t", [P, U])
        o_n = sb("o_n", [P, U])
        o_r = sb("o_r", [P, U])
        z = sb("z", [P, NC_, REP * P])
        gated = sb("gated", [P, NC_, REP * P])
        gatedT = sb("gatedT", [P, REP, T])
        ps = [ctx.enter_context(nc.psum_tensor(f"rps{k}", [P, 512], F32)) for k in range(8)]
        PROJ_BANK = (4, 5, 6, 7)
        ORDER = (1, 2, 3, 0)

        rows_in, cols_in, win_in, wz_in, wout_in, norm_in = (sem(s) for s in ("rows_in", "cols_in", "win_in", "wz_in", "wout_in", "norm_in"))
        init, passed = sem("init"), sem("passed")
        proj_ps, q_ps, k_ps, v_ps, kk_ps, w_ps, x_ps = (
            sem(s) for s in ("proj_ps", "q_ps", "k_ps", "v_ps", "kk_ps", "w_ps", "x_ps"))
        y_ps, z_ps, ks_ps, qs_ps, u_ps, s_ps, o_ps, gT_ps, out_ps = (
            sem(s) for s in ("y_ps", "z_ps", "ks_ps", "qs_ps", "u_ps", "s_ps", "o_ps", "gT_ps", "out_ps"))
        decay_done, conv0_done, mixed_done, ksq_done, qsq_done, v_done, w_done = (
            sem(s) for s in ("decay_done", "conv0_done", "mixed_done", "ksq_done", "qsq_done", "v_done", "w_done"))
        z_done, fs_done, upd_done, osq_done, gT_done, wout_done = (
            sem(s) for s in ("z_done", "fs_done", "upd_done", "osq_done", "gT_done", "wout_done"))
        diff_done, tap_done, bm1_done, b_done, m_done, kw_done, inv1_done, inv_done = (
            sem(s) for s in ("diff_done", "tap_done", "bm1_done", "b_done", "m_done", "kw_done", "inv1_done", "inv_done"))
        r_done, st_done, o_done, gated_done, acc_done = (sem(s) for s in ("r_done", "st_done", "o_done", "gated_done", "acc_done"))
        part_done, k_pow, q_pow, d1_done, x1_done, bs0_done, bs_done, o_pow = (
            sem(s) for s in ("part_done", "k_pow", "q_pow", "d1_done", "x1_done", "bs0_done", "bs_done", "o_pow"))
        x_in, stored, final = sem("x_in"), sem("stored"), sem("final")
        WX = 2 * NL
        INV = 4 * NL - 2
        BS = 2 * (NL - 1)
        x_back = [t[:, :, :].rearrange("p a n -> p (a n)")[:, 0:NC_ * D] for t in (decay, bm1, conv, mixed)]
        block = ctx.enter_context(nc.Block())

        def counts(i, b):
            return lambda k: i * (k * BATCH) + k * b + BASE

        @block.sync
        def _(sp):
            sp.dma_start(norm_w[:, :], norm_dram).then_inc(norm_in, 16)
            sp.dma_start(w_z[:, :, :], w_z_dram[0]).then_inc(wz_in, 16)
            sp.dma_start(w_out[:, :, :], w_out_dram[0]).then_inc(wout_in, 16)
            with sp.Fori(0, NK) as i:
                proj_used, taps_used = sp.snap(i * (4 * BATCH) + BASE), sp.snap(i * (12 * BATCH) + BASE)
                sp.wait_ge(proj_ps, proj_used)
                sp.sem_inc(passed, 1)
                sp.wait_ge(tap_done, taps_used)
                sp.sem_inc(passed, 1)
                sp.dma_start(w_in[:, :], w_in_dram[bass.ds(i, 1)].rearrange("o p n -> (o p) n")).then_inc(win_in, 16)
                for b in range(BATCH):
                    step = sp.snap(i * BATCH + b)
                    at = sp.snap(step * (U * C))
                    rows_used = sp.snap(step * 8 + BASE)
                    sp.wait_ge(diff_done, rows_used)
                    sp.sem_inc(passed, 1)
                    sp.dma_start(sums_row[:, :, :, :].rearrange("p k u t -> p k (u t)"),
                                 g_rows[:, bass.ds(at, U * C)].unsqueeze(0).to_broadcast([P, 2, U * C])).then_inc(rows_in, 16)
                    upd_used, st_used, fs_used = sp.snap(step * 4 + BASE), sp.snap(step * 5 + BASE), sp.snap(step * 6 + BASE)
                    sp.wait_ge(upd_done, upd_used)
                    sp.sem_inc(passed, 1)
                    sp.wait_ge(st_done, st_used)
                    sp.sem_inc(passed, 1)
                    sp.wait_ge(fs_done, fs_used)
                    sp.sem_inc(passed, 1)
                    sp.dma_start(cols[b % 2][:, :], prep[:, bass.ds(step, 1), :]).then_inc(cols_in, 16)
                    if b == 0:
                        z_used, out_used = sp.snap(i * (2 * BATCH) + 2 + BASE), sp.snap(i + 1)
                        sp.wait_ge(z_ps, z_used)
                        sp.sem_inc(passed, 1)
                        sp.dma_start(w_z[:, :, :], w_z_dram[bass.ds(i, 1)].rearrange("o p k n -> (o p) k n")).then_inc(wz_in, 16)
                        sp.wait_ge(wout_done, out_used)
                        sp.sem_inc(passed, 1)
                        sp.dma_start(w_out[:, :, :], w_out_dram[bass.ds(i, 1)].rearrange("o p v n -> (o p) v n")).then_inc(wout_in, 16)
            for k, (used, count) in enumerate(((m_done, 2), (x1_done, 2), (mixed_done, 4), (v_ps, 2))):
                sp.wait_ge(used, STEPS * count + BASE)
                sp.dma_start(x_back[k].rearrange("p (c d) -> p c d", c=NC_),
                             x[k].rearrange("(c p) d -> p c d", p=P)).then_inc(x_in, 16)
            sp.wait_ge(final, BATCH)
            for b in range(BATCH):
                sp.dma_start(out[b].rearrange("(c p) d -> p c d", p=P), acc[:, b * NC_:(b + 1) * NC_, :]).then_inc(stored, 16)
            sp.wait_ge(stored, 16 * BATCH)

        @block.tensor
        def _(pe):
            ident = cst[:, IDENT:IDENT + P]

            def scan_parts(r, n):
                def read_state(c):
                    pe.wait_ge(st_done, n(5) + (2 * c - 1))
                    pe.wait_ge(upd_done, n(4) + c)
                    cs = slice(c * C, (c + 1) * C)
                    nc.tensor.matmul(ps[6][:, 0:REP * P], qkT[r][:, 1, cs], state[:, :], start=True, stop=True).then_inc(ks_ps, 1)
                    pe.wait_ge(o_done, n(4) + c)
                    nc.tensor.matmul(ps[7][:, 0:REP * P], qkT[r][:, 0, cs], state[:, :], start=True, stop=True).then_inc(qs_ps, 1)

                def solve(c):
                    if c:
                        pe.wait_ge(r_done, n(6) + 2 * c)
                    for g in range(REP):
                        rhs = resid[:, g * P:(g + 1) * P] if c else v[r][:, g * NC_, :]
                        last = nc.tensor.matmul(ps[6][:, g * P:(g + 1) * P], inv[r][:, g * NC_ + c, :], rhs,
                                                start=True, stop=True)
                    last.then_inc(u_ps, 1)

                def attend(c):
                    pe.wait_ge(upd_done, n(4) + c + 1)
                    if c:
                        pe.wait_ge(fs_done, n(6) + 2 * c)
                    if c < NC_ - 1:
                        for g in range(REP):
                            last = nc.tensor.matmul(ps[6][:, (REP + g) * P:(REP + g + 1) * P], kw[r][:, g * NC_ + c, :],
                                                    upd[:, g * P:(g + 1) * P], start=True, stop=True)
                        last.then_inc(s_ps, 1)
                    for g in range(REP):
                        last = nc.tensor.matmul(ps[7][:, g * P:(g + 1) * P], scores[r][:, g * NC_ + c, :],
                                                upd[:, g * P:(g + 1) * P], start=True, stop=True)
                    last.then_inc(o_ps, 1)

                return read_state, solve, attend

            def gated_transpose(n, g):
                pe.wait_ge(gated_done, n(8) + 8)
                pe.wait_ge(inv_done, n(INV) + INV)
                for c in range(NC_):
                    last = nc.tensor.transpose(ps[2 + g][:, c * C:(c + 1) * C], gated[:, c, g * P:(g + 1) * P], ident)
                last.then_inc(gT_ps, 1)

            def project_out(n, c, loads):
                if c == 0:
                    pe.wait_ge(gT_done, n(2) + 2)
                    pe.wait_ge(wout_done, loads)
                for g in range(REP):
                    last = nc.tensor.matmul(ps[2 + c // 2][:, (c % 2) * D:(c % 2 + 1) * D],
                                            gatedT[:, g, c * C:(c + 1) * C], w_outn[:, g, :],
                                            start=(g == 0), stop=(g == REP - 1))
                if c % 2:
                    last.then_inc(out_ps, 1)

            def project_z(tb, c):
                for m in range(KT):
                    last = nc.tensor.matmul(ps[4 + c // 2][:, (c % 2) * D:(c % 2 + 1) * D],
                                            xnT[:, m, tb * T + c * C:tb * T + (c + 1) * C], w_z[:, m, :],
                                            start=(m == 0), stop=(m == KT - 1))
                if c % 2:
                    last.then_inc(z_ps, 1)

            def merge_w(n, lv, g):
                if lv == 0:
                    pe.wait_ge(bs0_done, n(2))
                    pe.wait_ge(inv1_done, n(2))
                    if g == 0:
                        pe.wait_ge(b_done, n(8))
                    else:
                        pe.wait_ge(m_done, n(2))
                else:
                    pe.wait_ge(bs_done, n(BS) + 2 * (lv - 1) + g + 1)
                    pe.wait_ge(inv_done, n(INV) + 4 * (lv - 1) + 2 * g + (2 if lv < NL - 1 else 1))
                for c in range(NC_):
                    last = nc.tensor.matmul(ps[g][:, c * C:(c + 1) * C], bs[g][lv % 2][:, c, :],
                                            invT[:, g * NC_ + c, :], start=True, stop=True)
                last.then_inc(w_ps, 1)

            def merge_x(n, lv, g, r):
                pe.wait_ge(w_done, n(WX) + 2 * lv + g + 1)
                if lv == 0:
                    pe.wait_ge(x1_done, n(2))
                    pe.wait_ge(acc_done, n(2))
                if lv == NL - 1:
                    pe.wait_ge(inv_done, n(INV) + 4 * (lv - 1) + 2 * g + 2)
                if lv == NL - 2:
                    for c in range(NC_):
                        u = g * NC_ + c
                        last = nc.tensor.matmul(ps[g][:, c * C:(c + 1) * C], inv[r][:, u, :], wneg[:, u, :], start=True, stop=True)
                    last.then_inc(y_ps, 1)
                for c in range(NC_):
                    u = g * NC_ + c
                    last = nc.tensor.matmul(ps[2 + g][:, c * C:(c + 1) * C], wneg[:, u, :], inv[r][:, u, :], start=True, stop=True)
                last.then_inc(x_ps, 1)

            for s in (proj_ps, q_ps, k_ps, v_ps, kk_ps, w_ps, x_ps,
                      y_ps, z_ps, ks_ps, qs_ps, u_ps, s_ps, o_ps, gT_ps, out_ps):
                pe.sem_inc(s, BASE)
            pe.wait_ge(init, 4)
            with pe.Fori(0, NK) as i:
                for b in range(BATCH):
                    p, r = b % 2, 1 - b % 2
                    n = counts(i, b)
                    read_state, solve, attend = scan_parts(r, n)

                    def project(j):
                        if j < 2:
                            pe.wait_ge(z_done, n(2))
                        else:
                            pe.wait_ge(upd_done, n(4))
                            pe.wait_ge(o_done, n(4))
                        if j == ORDER[0]:
                            pe.wait_ge(win_in, i * 16 + 16)
                        for m in range(KT):
                            last = nc.tensor.matmul(ps[PROJ_BANK[j]][:, :], w_in[:, m * 4 * P + j * P:m * 4 * P + (j + 1) * P],
                                                    xnT[:, m, b * T:(b + 1) * T], start=(m == 0), stop=(m == KT - 1))
                        last.then_inc(proj_ps, 1)

                    def by_token(j):
                        pe.wait_ge(mixed_done, n(4) + ORDER.index(j) + 1)
                        src = qkT[p][:, j, :] if j < 2 else mixed[:, j - 2, :]
                        for c in range(NC_):
                            last = nc.tensor.transpose(ps[PROJ_BANK[j]][:, c * C:(c + 1) * C], src[:, c * C:(c + 1) * C], ident)
                        last.then_inc((q_ps, k_ps, v_ps, v_ps)[j], 1)

                    def k_products(j):
                        pe.wait_ge(w_done, n(WX) + WX)
                        pe.wait_ge(mixed_done, n(4) + 4)
                        for c in range(NC_):
                            cs = slice(c * C, (c + 1) * C)
                            last = nc.tensor.matmul(ps[j][:, cs], qkT[p][:, 1, cs], qkT[p][:, 1 - j, cs], start=True, stop=True)
                        last.then_inc(kk_ps, 1)

                    project(1)
                    for lv in range(NL):
                        merge_w(n, lv, 0)
                        merge_w(n, lv, 1)
                        if lv == 4:
                            by_token(3)
                        if lv == 5:
                            by_token(0)
                        merge_x(n, lv, 0, r)
                        merge_x(n, lv, 1, r)
                        if lv == 0:
                            project(2)
                        if lv == 1:
                            project(3)
                        if lv == 2:
                            by_token(1)
                            project(0)
                        if lv == 3:
                            by_token(2)
                    k_products(0)
                    k_products(1)
                    pe.wait_ge(inv_done, n(INV) + INV)
                    pe.wait_ge(v_done, n(2) + 2)
                    loads = i + (1 if b < 2 else 2)
                    tb = (b - 1) % BATCH
                    solve(0)
                    gated_transpose(n, 0)
                    attend(0)
                    gated_transpose(n, 1)
                    read_state(1)
                    pe.wait_ge(qsq_done, n(1) + 1)
                    pe.wait_ge(wz_in, (i + (1 if b == 0 else 2)) * 16)
                    project_z(tb, 0)
                    solve(1)
                    project_z(tb, 1)
                    attend(1)
                    project_out(n, 0, loads)
                    read_state(2)
                    project_out(n, 1, loads)
                    solve(2)
                    pe.wait_ge(kw_done, n(8) + 8)
                    project_z(tb, 2)
                    attend(2)
                    project_z(tb, 3)
                    read_state(3)
                    project_out(n, 2, loads)
                    solve(3)
                    project_out(n, 3, loads)
                    attend(3)
            n = counts(NK, 0)
            read_state, solve, attend = scan_parts(1, n)
            for lv in range(NL):
                merge_w(n, lv, 0)
                merge_w(n, lv, 1)
                merge_x(n, lv, 0, 1)
                merge_x(n, lv, 1, 1)
            pe.wait_ge(inv_done, n(INV) + INV)
            pe.wait_ge(z_done, n(2))
            for g in range(REP):
                gated_transpose(n, g)
            for c in range(NC_):
                project_z(BATCH - 1, c)
            for c in range(NC_):
                if c:
                    read_state(c)
                solve(c)
                project_out(n, c, NK + 1)
                attend(c)
            n = counts(NK, 1)
            pe.wait_ge(acc_done, n(2))
            for g in range(REP):
                pe.wait_ge(gated_done, n(8) + 8)
                for c in range(NC_):
                    last = nc.tensor.transpose(ps[2 + g][:, c * C:(c + 1) * C], gated[:, c, g * P:(g + 1) * P], ident)
                last.then_inc(gT_ps, 1)
            for c in range(NC_):
                project_out(n, c, NK + 1)

        @block.scalar
        def _(act):
            def col(r, kind, u):
                return cols[r][:, kind * U + u:kind * U + u + 1]

            def chunks(ap):
                return ap.rearrange("p (c t) -> p c t", c=NC_)

            def scan_parts(r, n):
                def take_updates(c):
                    act.wait_ge(u_ps, n(4) + c + 1)
                    act.wait_ge(o_ps, n(4) + c)
                    for g in range(REP):
                        last = nc.scalar.activation(upd[:, g * P:(g + 1) * P], ps[6][:, g * P:(g + 1) * P], ACT.Copy,
                                                    scale=beta_k2[r][:, g * NC_ + c:g * NC_ + c + 1])
                    last.then_inc(upd_done, 1)

                def take_state_part(c):
                    act.wait_ge(qs_ps, n(3) + c)
                    act.wait_ge(o_done, n(4) + c)
                    for g in range(REP):
                        nc.scalar.activation(from_state[:, g * P:(g + 1) * P], ps[7][:, g * P:(g + 1) * P], ACT.Copy,
                                             scale=col(r, GAM, g * NC_ + c)).then_inc(fs_done, 1)

                def squares(c):
                    act.wait_ge(o_done, n(4) + c + 1)
                    if c == 0:
                        act.wait_ge(o_pow, n(4))
                        act.wait_ge(gT_ps, n(2) + 2)
                    for g in range(REP):
                        u = g * NC_ + c
                        last = nc.scalar.activation(gated[:, c, g * P:(g + 1) * P], o[:, c, g * P:(g + 1) * P], ACT.Square,
                                                    accum_out=o_sq[:, u:u + 1])
                    last.then_inc(osq_done, 1)

                return take_updates, take_state_part, squares

            def take_transposes(n):
                act.wait_ge(out_ps, n(2))
                for g in range(REP):
                    act.wait_ge(gT_ps, n(2) + g + 1)
                    nc.scalar.activation(gatedT[:, g, :], ps[2 + g][:, :], ACT.Copy).then_inc(gT_done, 1)

            def gate_z(n, h):
                act.wait_ge(gated_done, n(8) + 8)
                act.wait_ge(z_ps, n(2) + h + 1)
                nc.scalar.activation(z[:, 2 * h:2 * h + 2, :], ps[4 + h][:, :].rearrange("p (c d) -> p c d", c=2),
                                     ACT.Silu).then_inc(z_done, 1)

            def take_w(n, lv, g):
                act.wait_ge(w_ps, n(WX) + 2 * lv + g + 1)
                act.wait_ge(x_ps, n(WX) + max(2 * lv + g - 1, 0))
                nc.scalar.activation(wneg[:, g * NC_:(g + 1) * NC_, :], chunks(ps[g][:, :]), ACT.Copy, scale=-1.0).then_inc(w_done, 1)

            def scale_out_weights(loads):
                act.wait_ge(wout_in, loads * 16)
                nc.scalar.activation(w_outn[:, :, :], w_out[:, :, :], ACT.Copy, scale=norm_w[:, 0:1]).then_inc(wout_done, 1)

            for s in (decay_done, conv0_done, mixed_done, ksq_done, qsq_done, v_done, w_done,
                      z_done, fs_done, upd_done, osq_done, gT_done):
                act.sem_inc(s, BASE)
            act.wait_ge(norm_in, 16)
            act.wait_ge(init, 4)
            scale_out_weights(1)
            with act.Fori(0, NK) as i:
                for b in range(BATCH):
                    p, r = b % 2, 1 - b % 2
                    n = counts(i, b)
                    take_updates, take_state_part, squares = scan_parts(r, n)

                    def first_tap(j):
                        act.wait_ge(proj_ps, n(4) + ORDER.index(j) + 1)
                        act.wait_ge(mixed_done, n(4))
                        act.wait_ge(ksq_done, n(1))
                        act.wait_ge(qsq_done, n(1))
                        nc.scalar.activation(conv[:, j, :], ps[PROJ_BANK[j]][:, :], ACT.Copy,
                                             scale=w_in[:, KT * 4 * P + j * KC + KC - 1:KT * 4 * P + (j + 1) * KC]).then_inc(conv0_done, 1)

                    def silu(j):
                        act.wait_ge(tap_done, n(12) + 3 * ORDER.index(j) + 3)
                        if j < 2:
                            act.wait_ge(qs_ps, n(3))
                            dst = qkT[p][:, j, :]
                        else:
                            act.wait_ge(v_ps, n(2))
                            dst = mixed[:, j - 2, :]
                        nc.scalar.activation(dst, conv[:, j, :], ACT.Silu).then_inc(mixed_done, 1)

                    def squares_by_token(j):
                        if j:
                            act.wait_ge(k_ps, n(1) + 1)
                            act.wait_ge(k_pow, n(4))
                        else:
                            act.wait_ge(q_ps, n(1) + 1)
                            act.wait_ge(q_pow, n(5))
                        sums, done = ((q_sq, qsq_done), (k_sq, ksq_done))[j]
                        for c in range(NC_):
                            last = nc.scalar.activation(conv[:, j, c * C:(c + 1) * C], ps[4 + j][:, c * C:(c + 1) * C], ACT.Square,
                                                        accum_out=sums[:, c:c + 1])
                        last.then_inc(done, 1)

                    def take_v(j):
                        act.wait_ge(v_ps, n(2) + j + 1)
                        act.wait_ge(k_pow, n(4) + 4)
                        for c in range(NC_):
                            last = nc.scalar.activation(v[p][:, j * NC_ + c, :], ps[6 + j][:, c * C:(c + 1) * C], ACT.Copy,
                                                        scale=k_norm[:, c:c + 1])
                        last.then_inc(v_done, 1)

                    if b == 2:
                        act.wait_ge(out_ps, n(2))
                        scale_out_weights(i + 2)
                    for lv in range(NL):
                        take_w(n, lv, 0)
                        take_w(n, lv, 1)
                        if lv == 0:
                            first_tap(1)
                            first_tap(2)
                        if lv == 1:
                            silu(1)
                            first_tap(3)
                        if lv == 2:
                            silu(2)
                            squares_by_token(1)
                            first_tap(0)
                        if lv == 3:
                            silu(3)
                        if lv == 4:
                            silu(0)
                            for g in range(REP):
                                act.wait_ge(diff_done, n(8) + NC_ * (g + 1))
                                us = slice(g * NC_, (g + 1) * NC_)
                                nc.scalar.activation(decay[:, us, :], decay[:, us, :], ACT.Exp).then_inc(decay_done, 1)
                            take_v(0)
                    take_v(1)
                    squares_by_token(0)
                    take_updates(0)
                    take_transposes(n)
                    take_state_part(1)
                    take_updates(1)
                    gate_z(n, 0)
                    squares(0)
                    take_state_part(2)
                    take_updates(2)
                    squares(1)
                    gate_z(n, 1)
                    take_state_part(3)
                    take_updates(3)
                    squares(2)
                    squares(3)
            n = counts(NK, 0)
            take_updates, take_state_part, squares = scan_parts(1, n)
            for lv in range(NL):
                take_w(n, lv, 0)
                take_w(n, lv, 1)
            take_transposes(n)
            gate_z(n, 0)
            gate_z(n, 1)
            for c in range(NC_):
                if c:
                    take_state_part(c)
                take_updates(c)
                squares(c)
            take_transposes(counts(NK, 1))

        @block.vector
        def _(dve):
            def col(r, kind, u):
                return cols[r][:, kind * U + u:kind * U + u + 1]

            def chunks(ap):
                return ap.rearrange("p (c t) -> p c t", c=NC_)

            def scan_parts(r, n):
                def residual(c):
                    dve.wait_ge(ks_ps, n(3) + c)
                    dve.wait_ge(u_ps, n(4) + c)
                    for g in range(REP):
                        u = g * NC_ + c
                        nc.vector.scalar_tensor_tensor(resid[:, g * P:(g + 1) * P], ps[6][:, g * P:(g + 1) * P],
                                                       col(r, NGAM, u), v[r][:, u, :], ALU.mult, ALU.add).then_inc(r_done, 1)

                def output(c):
                    if c < NC_ - 1:
                        dve.wait_ge(s_ps, n(3) + c + 1)
                        dve.wait_ge(st_done, n(5) + max(2 * c - 1, 0))
                        if c:
                            for g in range(REP):
                                part = slice(g * P, (g + 1) * P)
                                nc.vector.scalar_tensor_tensor(state[:, part], state[:, part], col(r, GAMC, g * NC_ + c),
                                                               ps[6][:, (REP + g) * P:(REP + g + 1) * P],
                                                               ALU.mult, ALU.add).then_inc(st_done, 1)
                        else:
                            nc.vector.tensor_copy(state[:, :], ps[6][:, REP * P:2 * REP * P]).then_inc(st_done, 1)
                    dve.wait_ge(o_ps, n(4) + c + 1)
                    if c:
                        dve.wait_ge(fs_done, n(6) + 2 * c)
                        nc.vector.tensor_tensor(o[:, c, :], ps[7][:, 0:REP * P], from_state[:, :], ALU.add).then_inc(o_done, 1)
                    else:
                        dve.wait_ge(osq_done, n(4))
                        nc.vector.tensor_copy(o[:, c, :], ps[7][:, 0:REP * P]).then_inc(o_done, 1)

                return residual, output

            def gating(n, g):
                dve.wait_ge(o_pow, n(4))
                dve.wait_ge(o_done, n(4))
                dve.wait_ge(z_done, n(2))
                dve.wait_ge(gT_ps, n(2))
                for c in range(NC_):
                    u = g * NC_ + c
                    part = slice(g * P, (g + 1) * P)
                    nc.vector.scalar_tensor_tensor(gated[:, c, part], o[:, c, part], o_r[:, u:u + 1], z[:, c, part],
                                                   ALU.mult, ALU.mult).then_inc(gated_done, 1)

            def add_out(n, tb, h):
                dve.wait_ge(out_ps, n(2) + h + 1)
                at = slice(tb * NC_ + 2 * h, tb * NC_ + 2 * h + 2)
                nc.vector.tensor_tensor(acc[:, at, :], ps[2 + h][:, :].rearrange("p (c d) -> p c d", c=2),
                                        acc[:, at, :], ALU.add).then_inc(acc_done, 1)

            def update_inverse(n, lv, g, r):
                us = slice(g * NC_, (g + 1) * NC_)
                if lv:
                    dve.wait_ge(inv_done, n(INV) + 4 * (lv - 1) + 2 * g + 2)
                if lv == NL - 2:
                    dve.wait_ge(y_ps, n(2) + g + 1)
                    nc.vector.tensor_tensor(invT[:, us, :], chunks(ps[g][:, :]), invT[:, us, :], ALU.add).then_inc(inv_done, 1)
                dve.wait_ge(x_ps, n(WX) + 2 * lv + g + 1)
                nc.vector.tensor_tensor(inv[r][:, us, :], chunks(ps[2 + g][:, :]), inv[r][:, us, :], ALU.add).then_inc(inv_done, 1)
                if lv < NL - 2:
                    dve.wait_ge(inv_done, n(INV) + 4 * lv + 2 * g + 1)
                    nc.vector.transpose(invT[:, us, :], inv[r][:, us, :]).then_inc(inv_done, 1)

            for s in (diff_done, tap_done, bm1_done, b_done, m_done, kw_done, inv1_done, inv_done,
                      r_done, st_done, o_done, gated_done, acc_done):
                dve.sem_inc(s, BASE)
            for t in (qkT[1], v[1], kw[1], scores[1], inv[1], invT, bmat, bs[0][0], bs[1][0]):
                nc.vector.memset(t[:, :, :], 0.0)
            nc.vector.memset(o[:, :, :], 0.0)
            for t in (o_r, beta_k2[1], q_scale[1], q_mean2[1]):
                nc.vector.memset(t[:, :], 0.0)
            nc.vector.memset(eps8[:, :], L2_EPS)
            nc.vector.memset(mhalf8[:, :], -0.5)
            nc.vector.memset(half4[:, :], 0.5)
            nc.vector.memset(mone4[:, :], -1.0)
            nc.vector.memset(inv128[:, :], 1.0 / (P * P))
            nc.vector.memset(scale8[:, :], float(P) ** -0.5).then_inc(init, 1)
            nc.vector.memset(cols[1][:, :], 0.0).then_inc(init, 1)
            dve.wait_ge(init, 4)

            with dve.Fori(0, NK) as i:
                for b in range(BATCH):
                    p, r = b % 2, 1 - b % 2
                    n = counts(i, b)
                    residual, output = scan_parts(r, n)

                    def taps(j):
                        for t in range(KC - 1):
                            shift = KC - 1 - t
                            k = 4 * KT * P + j * KC + t
                            if t == 0:
                                dve.wait_ge(conv0_done, n(4) + ORDER.index(j) + 1)
                            else:
                                dve.wait_ge(tap_done, n(12) + 3 * ORDER.index(j) + t)
                            nc.vector.scalar_tensor_tensor(conv[:, j, shift:T], ps[PROJ_BANK[j]][:, 0:T - shift], w_in[:, k:k + 1],
                                                           conv[:, j, shift:T], ALU.mult, ALU.add).then_inc(tap_done, 1)

                    def differences(g):
                        dve.wait_ge(part_done, n(4) + 4)
                        for c in range(NC_):
                            u = g * NC_ + c
                            nc.vector.scalar_tensor_tensor(decay[:, u, :], decay[:, u, :], col(p, NHI, u), sums_row[:, 1, u, :],
                                                           ALU.add, ALU.add).then_inc(diff_done, 1)

                    def b_of_head(g, part):
                        dst, scale, done = ((bm1, decay1, bm1_done), (bmat, decay, b_done))[part]
                        for c in range(NC_):
                            u = g * NC_ + c
                            nc.vector.scalar_tensor_tensor(dst[:, u, :], ps[0][:, c * C:(c + 1) * C], beta_k2[p][:, u:u + 1],
                                                           scale[:, u, :], ALU.mult, ALU.mult).then_inc(done, 1)

                    def scores_of_head(g):
                        us = slice(g * NC_, (g + 1) * NC_)
                        dve.wait_ge(kk_ps, n(2) + 2)
                        nc.vector.tensor_tensor(scores[p][:, us, :], chunks(ps[1][:, :]), decay[:, us, :], ALU.mult).then_inc(m_done, 1)

                    def decayed_k(g):
                        for c in range(NC_):
                            u = g * NC_ + c
                            nc.vector.tensor_scalar(kw[p][:, u, :], ps[5][:, c * C:(c + 1) * C], col(p, WSUF, u), None,
                                                    ALU.mult).then_inc(kw_done, 1)

                    def first_transpose(g):
                        us = slice(g * NC_, (g + 1) * NC_)
                        dve.wait_ge(x1_done, n(2) + g + 1)
                        nc.vector.transpose(invT[:, us, :], inv[p][:, us, :]).then_inc(inv1_done, 1)

                    for lv in range(NL):
                        update_inverse(n, lv, 0, r)
                        update_inverse(n, lv, 1, r)
                        if lv == 0:
                            gating(n, 0)
                            taps(1)
                        if lv == 1:
                            taps(2)
                            dve.wait_ge(cols_in, n(16) - BASE + 16)
                            differences(0)
                        if lv == 2:
                            taps(3)
                        if lv == 3:
                            taps(0)
                            differences(1)
                        if lv == 4:
                            gating(n, 1)
                            dve.wait_ge(ksq_done, n(1) + 1)
                            decayed_k(0)
                    decayed_k(1)
                    output(0)
                    dve.wait_ge(kk_ps, n(2) + 1)
                    dve.wait_ge(decay_done, n(2) + 2)
                    dve.wait_ge(d1_done, n(2) + 2)
                    dve.wait_ge(k_pow, n(4) + 4)
                    dve.wait_ge(bs_done, n(BS) + BS)
                    dve.wait_ge(bs0_done, n(2))
                    dve.wait_ge(x1_done, n(2))
                    b_of_head(0, 0)
                    residual(1)
                    b_of_head(1, 0)
                    output(1)
                    b_of_head(0, 1)
                    residual(2)
                    b_of_head(1, 1)
                    output(2)
                    add_out(n, (b - 2) % BATCH, 0)
                    residual(3)
                    dve.wait_ge(w_ps, n(WX) + WX)
                    first_transpose(0)
                    first_transpose(1)
                    scores_of_head(0)
                    output(3)
                    scores_of_head(1)
                    add_out(n, (b - 2) % BATCH, 1)

            n = counts(NK, 0)
            residual, output = scan_parts(1, n)
            for g in range(REP):
                gating(n, g)
            for lv in range(NL):
                update_inverse(n, lv, 0, 1)
                update_inverse(n, lv, 1, 1)
            for c in range(NC_):
                if c:
                    residual(c)
                output(c)
            add_out(n, BATCH - 2, 0)
            add_out(n, BATCH - 2, 1)
            n = counts(NK, 1)
            for g in range(REP):
                gating(n, g)
            add_out(n, BATCH - 1, 0)
            add_out(n, BATCH - 1, 1)
            dve.wait_ge(acc_done, n(2) + 2)
            for b in range(BATCH):
                at = slice(b * NC_, (b + 1) * NC_)
                nc.vector.tensor_tensor(acc[:, at, :], acc[:, at, :], gate[:, at, :], ALU.mult).then_inc(acc_done, 1)
            dve.wait_ge(x_in, 16 * BATCH)
            dve.wait_ge(acc_done, n(2) + 2 + BATCH)
            for b in range(BATCH):
                row = acc[:, b * NC_:(b + 1) * NC_, :].rearrange("p c d -> p (c d)")
                nc.vector.tensor_tensor(row, row, x_back[b], ALU.add).then_inc(final, 1)

        @block.gpsimd
        def _(pool):
            def output_norms(n, r):
                pool.wait_ge(osq_done, n(4) + 4)
                pool.wait_ge(gated_done, n(8) + 8)
                nc.gpsimd.tensor_tensor(o_t[:, :], o_sq[:, :], q_mean2[r][:, :], ALU.mult).then_inc(o_pow, 1)
                pool.wait_ge(o_pow, n(4) + 1)
                nc.gpsimd.tensor_tensor(o_t[:, :], o_t[:, :], eps8[:, :], ALU.add).then_inc(o_pow, 1)
                pool.wait_ge(o_pow, n(4) + 2)
                nc.gpsimd.tensor_tensor(o_n[:, :], o_t[:, :], mhalf8[:, :], ALU.pow).then_inc(o_pow, 1)
                pool.wait_ge(o_pow, n(4) + 3)
                nc.gpsimd.tensor_tensor(o_r[:, :], o_n[:, :], q_scale[r][:, :], ALU.mult).then_inc(o_pow, 1)

            def masked(dst, src, g, at):
                mask = cst[:, at:at + P].unsqueeze(1).to_broadcast([P, NC_, P])
                return nc.gpsimd.tensor_tensor(dst, src[:, g * NC_:(g + 1) * NC_, :], mask, ALU.mult)

            def mask_level(n, lv, g):
                pool.wait_ge(w_ps, n(WX) + (2 * (lv - 2) + g + 1 if lv > 1 else 0))
                masked(bs[g][lv % 2][:, :, :], bmat, g, MERGE2 + lv * P).then_inc(bs_done, 1)

            for s in (part_done, k_pow, q_pow, d1_done, x1_done, bs0_done, bs_done, o_pow):
                pool.sem_inc(s, BASE)
            for t in (z, acc):
                nc.gpsimd.memset(t[:, :, :], 0.0).then_inc(init, 1)
            pool.wait_ge(init, 4)
            with pool.Fori(0, NK) as i:
                for b in range(BATCH):
                    p = b % 2
                    n = counts(i, b)

                    def two_heads(small):
                        return small[:, :].unsqueeze(1).to_broadcast([P, REP, NC_])

                    def by_head(row):
                        return row.rearrange("p (g c) -> p g c", g=REP)

                    def k_norms():
                        pool.wait_ge(ksq_done, n(1) + 1)
                        pool.wait_ge(v_done, n(2))
                        pool.wait_ge(upd_done, n(4))
                        pool.wait_ge(cols_in, n(16) - BASE + 16)
                        nc.gpsimd.tensor_tensor(k_t[:, :], k_sq[:, :], eps8[:, 0:NC_], ALU.add).then_inc(k_pow, 1)
                        pool.wait_ge(k_pow, n(4) + 1)
                        nc.gpsimd.tensor_tensor(k_norm[:, :], k_t[:, :], half4[:, :], ALU.pow).then_inc(k_pow, 1)
                        nc.gpsimd.tensor_tensor(k_inv2[:, :], k_t[:, :], mone4[:, :], ALU.pow).then_inc(k_pow, 1)
                        pool.wait_ge(k_pow, n(4) + 3)
                        nc.gpsimd.tensor_tensor(by_head(beta_k2[p][:, :]), by_head(cols[p][:, BETA * U:(BETA + 1) * U]),
                                                two_heads(k_inv2), ALU.mult).then_inc(k_pow, 1)

                    def q_norms():
                        pool.wait_ge(qsq_done, n(1) + 1)
                        nc.gpsimd.tensor_tensor(q_t[:, :], q_sq[:, :], eps8[:, 0:NC_], ALU.add).then_inc(q_pow, 1)
                        pool.wait_ge(q_pow, n(5) + 1)
                        nc.gpsimd.tensor_tensor(q_rinv[:, :], q_t[:, :], mhalf8[:, 0:NC_], ALU.pow).then_inc(q_pow, 1)
                        pool.wait_ge(q_pow, n(5) + 2)
                        nc.gpsimd.tensor_tensor(by_head(q_scale[p][:, :]), two_heads(q_rinv), by_head(scale8[:, :]),
                                                ALU.mult).then_inc(q_pow, 1)
                        nc.gpsimd.tensor_tensor(q_t[:, :], q_rinv[:, :], q_rinv[:, :], ALU.mult).then_inc(q_pow, 1)
                        pool.wait_ge(q_pow, n(5) + 4)
                        nc.gpsimd.tensor_tensor(by_head(q_mean2[p][:, :]), two_heads(q_t), by_head(inv128[:, :]),
                                                ALU.mult).then_inc(q_pow, 1)

                    for lv in range(1, NL):
                        for g in range(REP):
                            mask_level(n, lv, g)
                        if lv == 2:
                            pool.wait_ge(rows_in, n(16) - BASE + 16)
                            pool.wait_ge(cols_in, n(16) - BASE + 16)
                            pool.wait_ge(b_done, n(8))
                            pool.wait_ge(m_done, n(2))
                            pool.wait_ge(d1_done, n(2))
                            for g in range(REP):
                                us = slice(g * NC_, (g + 1) * NC_)
                                nc.gpsimd.tensor_tensor(decay[:, us, :], sums_row[:, 0, us, :],
                                                        cst[:, HIDE:HIDE + P].unsqueeze(1).to_broadcast([P, NC_, C]),
                                                        ALU.add).then_inc(part_done, 1)
                            for g in range(REP):
                                us = slice(g * NC_, (g + 1) * NC_)
                                nc.gpsimd.tensor_tensor(sums_row[:, 1, us, :], sums_row[:, 1, us, :],
                                                        cols[p][:, NLO * U + g * NC_:NLO * U + (g + 1) * NC_].unsqueeze(2).to_broadcast([P, NC_, C]),
                                                        ALU.add).then_inc(part_done, 1)
                        if lv == 5:
                            pool.wait_ge(bm1_done, n(8))
                            for g in range(REP):
                                pool.wait_ge(decay_done, n(2) + g + 1)
                                masked(decay1[:, g * NC_:(g + 1) * NC_, :], decay, g, MERGE1).then_inc(d1_done, 1)
                        if lv == 3:
                            k_norms()
                    q_norms()
                    for g in range(REP):
                        us = slice(g * NC_, (g + 1) * NC_)
                        pool.wait_ge(bm1_done, n(8) + NC_ * (g + 1))
                        pool.wait_ge(u_ps, n(4))
                        nc.gpsimd.tensor_tensor(inv[p][:, us, :], bm1[:, us, :],
                                                cst[:, IDENT:IDENT + P].unsqueeze(1).to_broadcast([P, NC_, P]),
                                                ALU.add).then_inc(x1_done, 1)
                    for g in range(REP):
                        pool.wait_ge(b_done, n(8) + NC_ * (g + 1))
                        pool.wait_ge(w_ps, n(WX) + WX)
                        masked(bs[g][0][:, :, :], bmat, g, MERGE2).then_inc(bs0_done, 1)
                    output_norms(n, 1 - p)
            n = counts(NK, 0)
            for lv in range(1, NL):
                for g in range(REP):
                    mask_level(n, lv, g)
            output_norms(n, 1)


_INS = ["x", "small_w", "decay_rows", "consts", "ffn_gate", "ffn_up", "ffn_down", "w_in", "w_z", "w_out", "norm_w"]


def program(nc, a, out):
    with ExitStack() as ctx:
        def sb(name, shape):
            return ctx.enter_context(nc.sbuf_tensor(name, shape, F32))

        keep = {
            "cst": sb("cst", [P, NCONST]),
            "xnT": sb("xnT", [P, KT, BATCH * T]),
            "gate": sb("gate", [P, TILES, D]),
            "prep": sb("prep", [P, STEPS, KINDS * U]),
            "cst_dram": a["consts"],
        }
        g_rows = nc.dram_tensor("g_rows", [2, UNITS * C], F32).ap()
        comb_rows = nc.dram_tensor("comb_rows", [TILES * (E + 1), P], F32).ap()
        prepare_block(nc, a["x"], a["small_w"], a["decay_rows"], keep, g_rows, comb_rows)
        ffn_block(nc, a["ffn_gate"], a["ffn_up"], a["ffn_down"], keep, comb_rows)
        recurrent_block(nc, a["x"], a["w_in"], a["w_z"], a["w_out"], a["norm_w"], keep, g_rows, out)


def kernel(**inputs):
    import concourse.bacc as bacc
    from concourse.bass_utils import run_bass_kernel_spmd

    x = {k: np.asarray(v_) for k, v_ in inputs.items()}

    def rows(w):
        return w.reshape(KT, P, -1).transpose(1, 0, 2)

    def padded(w):
        return np.concatenate([w, np.zeros((FT * P - F,) + w.shape[1:], w.dtype)])

    def by_unit(row):
        return np.broadcast_to(row.reshape(NK, 1, REP, 1), (NK, BATCH, REP, NC_)).reshape(UNITS)

    keys = NK * P
    wqkv, conv_w = x["L0_attn_W_qkv"], x["L0_attn_conv_w"]
    heads = [wqkv[:, :keys].reshape(D, NK, 1, P), wqkv[:, keys:2 * keys].reshape(D, NK, 1, P),
             wqkv[:, 2 * keys:].reshape(D, NK, REP, P)]
    w_in = np.concatenate(heads, 2).reshape(KT, P, NK, 4 * P).transpose(2, 1, 0, 3).reshape(NK, P, KT * 4 * P)
    taps = np.concatenate([conv_w[:keys].reshape(NK, 1, P, KC), conv_w[keys:2 * keys].reshape(NK, 1, P, KC),
                           conv_w[2 * keys:].reshape(NK, REP, P, KC)], 1).transpose(0, 2, 1, 3).reshape(NK, P, 4 * KC)
    gu_e, gu_s = x["L0_ffn_We_gate_up"], x["L0_ffn_Ws_gate_up"]

    def up_or_gate(k):
        return padded(np.concatenate([gu_e[:, :, k * I_MOE:(k + 1) * I_MOE].transpose(0, 2, 1).reshape(E * I_MOE, D),
                                      gu_s[:, k * I_SH:(k + 1) * I_SH].T])).T

    down = padded(np.concatenate([x["L0_ffn_We_down"].reshape(E * I_MOE, D), x["L0_ffn_Ws_down"]]))
    data = {
        "x": x["L0_attn_hidden_states"],
        "small_w": rows(np.concatenate([x["L0_attn_W_b"], x["L0_attn_W_a"], x["L0_ffn_W_router"].T, x["L0_ffn_W_sgate"].T], 1)),
        "decay_rows": np.stack([by_unit(x["L0_attn_dt_bias"]), by_unit(x["L0_attn_A_log"])]),
        "consts": constants(),
        "ffn_gate": rows(up_or_gate(0)),
        "ffn_up": rows(up_or_gate(1)),
        "ffn_down": down.reshape(FT, P, D).transpose(1, 0, 2),
        "w_in": np.concatenate([w_in, taps], 2),
        "w_z": x["L0_attn_W_z"].reshape(KT, P, NK, REP * P).transpose(2, 1, 0, 3),
        "w_out": x["L0_attn_W_out"].reshape(NK, REP, P, D).transpose(0, 2, 1, 3),
        "norm_w": x["L0_attn_norm_w"].reshape(P, 1),
    }
    nc = bacc.Bacc("TRN2", target_bir_lowering=False, num_devices=1)
    arrays, aps = {}, {}
    for name in _INS:
        arr = np.ascontiguousarray(data[name])
        arrays[f"in_{name}"] = arr
        aps[name] = nc.dram_tensor(f"in_{name}", arr.shape, mybir.dt.from_np(arr.dtype), kind="ExternalInput").ap()
    out = nc.dram_tensor("out", [BATCH, T, D], F32, kind="ExternalOutput").ap()
    program(nc, aps, out)
    r = run_bass_kernel_spmd(nc, [arrays], core_ids=[0])
    return r.results[0]["out"]
```
